# Optimizing a Trainium2 kernel written in Bass

```python
import numpy as np
import jax
import jax.numpy as jnp

def _softmax(x, axis=-1):
    return jax.nn.softmax(x, axis=axis)
def _gelu(x):
    return jax.nn.gelu(x, approximate=True)
def _silu(x):
    return jax.nn.silu(x)
def _sigmoid(x):
    return jax.nn.sigmoid(x)
def _layernorm(x, axis=-1, eps=1e-5):
    m = jnp.mean(x, axis=axis, keepdims=True)
    v = jnp.var(x, axis=axis, keepdims=True)
    return (x - m) / jnp.sqrt(v + eps)
def _scatter_add(tgt, idx, src, axis=0):
    return tgt.at[idx].add(src)
def _segment_sum(src, seg, n):
    return jax.ops.segment_sum(src, seg, n)

kernel_name = 'mk_conv_preact_d2_conv_nchw384_4d7d0f'

def setup_inputs(seed: int = 0):
    np.random.seed(seed)
    _w = jnp.asarray
    def _rec_inputs():
        import jax
        import jax.numpy as jnp
        _gk = jax.random.key(seed)
        x = -0.0001538 + 1 * jax.random.normal(jax.random.fold_in(_gk, 1), (4, 384, 64, 64), jnp.float32)
        return x
    x = _rec_inputs()
    def _L0_conv_setup():
        import jax, jax.numpy as jnp
        import numpy as np
        DIM = 384
        PD = 96
        QK = 16
        VD = PD
        QKV_OUT = 2 * QK + VD
        EPS = 1e-05

        def _bn(y, g, b, m, v):
            inv = g / jnp.sqrt(v + EPS)
            return y * inv[None, :, None, None] + (b - m * inv)[None, :, None, None]
        key = jax.random.key(seed)
        ks = jax.random.split(key, 12)
        B, H, W = (4, 64, 64)
        x = jax.random.normal(ks[0], (B, DIM, H, W), dtype=jnp.float32)
        ln_w = jnp.ones((PD,), jnp.float32)
        ln_b = jnp.zeros((PD,), jnp.float32)
        w_qkv = jax.random.normal(ks[1], (QKV_OUT, PD), jnp.float32) * 0.05
        bn1_g = jax.random.uniform(ks[2], (QKV_OUT,), jnp.float32, 0.5, 1.5)
        bn1_b = jax.random.normal(ks[3], (QKV_OUT,), jnp.float32) * 0.05
        bn1_m = jax.random.normal(ks[4], (QKV_OUT,), jnp.float32) * 0.05
        bn1_v = jax.random.uniform(ks[5], (QKV_OUT,), jnp.float32, 0.5, 1.5)
        w_proj = jax.random.normal(ks[6], (DIM, DIM), jnp.float32) * 0.02
        bn2_g = jax.random.uniform(ks[7], (DIM,), jnp.float32, 0.5, 1.5)
        bn2_b = jax.random.normal(ks[8], (DIM,), jnp.float32) * 0.05
        bn2_m = jax.random.normal(ks[9], (DIM,), jnp.float32) * 0.05
        bn2_v = jax.random.uniform(ks[10], (DIM,), jnp.float32, 0.5, 1.5)
        return {'x': x, 'ln_w': ln_w, 'ln_b': ln_b, 'w_qkv': w_qkv, 'bn1_g': bn1_g, 'bn1_b': bn1_b, 'bn1_m': bn1_m, 'bn1_v': bn1_v, 'w_proj': w_proj, 'bn2_g': bn2_g, 'bn2_b': bn2_b, 'bn2_m': bn2_m, 'bn2_v': bn2_v}
    _L0_conv_all = _L0_conv_setup()
    _L0_conv_in = {k: v for k, v in _L0_conv_all.items() if k in ('ln_w', 'ln_b', 'w_qkv', 'bn1_g', 'bn1_b', 'bn1_m', 'bn1_v', 'w_proj', 'bn2_g', 'bn2_b', 'bn2_m', 'bn2_v', )}
    del _L0_conv_all

    def _L1_conv_setup():
        import jax, jax.numpy as jnp
        import numpy as np
        D_MODEL = 384
        D_STATE = 64
        D_CONV = 3
        EXPAND = 2
        HEADDIM = 64
        NGROUPS = 1
        CHUNK = 256
        D_INNER = EXPAND * D_MODEL
        NHEADS = D_INNER // HEADDIM
        CONV_DIM = D_INNER + 2 * NGROUPS * D_STATE
        D_IN_PROJ = 2 * D_INNER + 2 * NGROUPS * D_STATE + NHEADS
        EPS = 1e-05

        def _chunk_scan(x, dt, A, Bm, Cm):
            b, l, h, p = x.shape
            nc = l // CHUNK
            xc = x.reshape(b, nc, CHUNK, h, p)
            dtc = dt.reshape(b, nc, CHUNK, h)
            hpg = h // NGROUPS
            Bh = jnp.repeat(Bm.reshape(b, nc, CHUNK, NGROUPS, D_STATE), hpg, axis=3)
            Ch = jnp.repeat(Cm.reshape(b, nc, CHUNK, NGROUPS, D_STATE), hpg, axis=3)
            dA = dtc * A
            dA_cs = jnp.cumsum(dA, axis=2)
            Lmat = jnp.exp(dA_cs[:, :, :, None, :] - dA_cs[:, :, None, :, :])
            causal = jnp.tril(jnp.ones((CHUNK, CHUNK), bool))
            att = jnp.einsum('bcihn,bcjhn->bcijh', Ch, Bh) * Lmat * dtc[:, :, None, :, :]
            att = jnp.where(causal[None, None, :, :, None], att, 0.0)
            y_intra = jnp.einsum('bcijh,bcjhp->bcihp', att, xc)
            decay_to_end = jnp.exp(dA_cs[:, :, -1:, :] - dA_cs)
            states = jnp.einsum('bcjhn,bcjh,bcjhp->bchpn', Bh, decay_to_end * dtc, xc)
            chunk_decay = jnp.exp(dA_cs[:, :, -1, :])

            def step(carry, inp):
                st, dec = inp
                new = carry * dec[:, :, None, None] + st
                return (new, carry)
            init = jnp.zeros((b, h, p, D_STATE), x.dtype)
            _, prevs = jax.lax.scan(step, init, (jnp.moveaxis(states, 1, 0), jnp.moveaxis(chunk_decay, 1, 0)))
            prev_states = jnp.moveaxis(prevs, 0, 1)
            y_inter = jnp.einsum('bcihn,bcih,bchpn->bcihp', Ch, jnp.exp(dA_cs), prev_states)
            return (y_intra + y_inter).reshape(b, l, h, p)
        key = jax.random.key(seed)
        ks = jax.random.split(key, 8)
        B, H, W = (16, 32, 32)
        u = jax.random.normal(ks[0], (B, D_MODEL, H, W), jnp.float32)
        in_proj_w = jax.random.normal(ks[1], (D_IN_PROJ, D_MODEL), jnp.float32) / np.sqrt(D_MODEL)
        conv_w = jax.random.normal(ks[2], (CONV_DIM, 1, D_CONV, D_CONV), jnp.float32) / np.sqrt(D_CONV * D_CONV)
        conv_b = jax.random.normal(ks[3], (CONV_DIM,), jnp.float32) * 0.01
        dt = jnp.exp(jax.random.uniform(ks[4], (NHEADS,)) * (np.log(0.1) - np.log(0.001)) + np.log(0.001))
        dt = jnp.clip(dt, 0.0001, None)
        dt_bias = dt + jnp.log(-jnp.expm1(-dt))
        A_log = jnp.log(jax.random.uniform(ks[5], (NHEADS,), minval=1.0, maxval=16.0))
        D = jnp.ones((NHEADS,), jnp.float32)
        norm_w = jnp.ones((D_INNER,), jnp.float32)
        norm_b = jnp.zeros((D_INNER,), jnp.float32)
        out_proj_w = jax.random.normal(ks[6], (D_MODEL, D_INNER), jnp.float32) / np.sqrt(D_INNER)
        return {'u': u, 'in_proj_w': in_proj_w, 'conv_w': conv_w, 'conv_b': conv_b, 'dt_bias': dt_bias, 'A_log': A_log, 'D': D, 'norm_w': norm_w, 'norm_b': norm_b, 'out_proj_w': out_proj_w}
    _L1_conv_all = _L1_conv_setup()
    _L1_conv_in = {k: v for k, v in _L1_conv_all.items() if k in ('in_proj_w', 'conv_w', 'conv_b', 'dt_bias', 'A_log', 'D', 'norm_w', 'norm_b', 'out_proj_w', )}
    del _L1_conv_all

    return {
        "x": x,
        "L0_conv_ln_w": _L0_conv_in["ln_w"],
        "L0_conv_ln_b": _L0_conv_in["ln_b"],
        "L0_conv_w_qkv": _L0_conv_in["w_qkv"],
        "L0_conv_bn1_g": _L0_conv_in["bn1_g"],
        "L0_conv_bn1_b": _L0_conv_in["bn1_b"],
        "L0_conv_bn1_m": _L0_conv_in["bn1_m"],
        "L0_conv_bn1_v": _L0_conv_in["bn1_v"],
        "L0_conv_w_proj": _L0_conv_in["w_proj"],
        "L0_conv_bn2_g": _L0_conv_in["bn2_g"],
        "L0_conv_bn2_b": _L0_conv_in["bn2_b"],
        "L0_conv_bn2_m": _L0_conv_in["bn2_m"],
        "L0_conv_bn2_v": _L0_conv_in["bn2_v"],
        "L1_conv_in_proj_w": _L1_conv_in["in_proj_w"],
        "L1_conv_conv_w": _L1_conv_in["conv_w"],
        "L1_conv_conv_b": _L1_conv_in["conv_b"],
        "L1_conv_dt_bias": _L1_conv_in["dt_bias"],
        "L1_conv_A_log": _L1_conv_in["A_log"],
        "L1_conv_D": _L1_conv_in["D"],
        "L1_conv_norm_w": _L1_conv_in["norm_w"],
        "L1_conv_norm_b": _L1_conv_in["norm_b"],
        "L1_conv_out_proj_w": _L1_conv_in["out_proj_w"],
    }

def reference(x, L0_conv_ln_w, L0_conv_ln_b, L0_conv_w_qkv, L0_conv_bn1_g, L0_conv_bn1_b, L0_conv_bn1_m, L0_conv_bn1_v, L0_conv_w_proj, L0_conv_bn2_g, L0_conv_bn2_b, L0_conv_bn2_m, L0_conv_bn2_v, L1_conv_in_proj_w, L1_conv_conv_w, L1_conv_conv_b, L1_conv_dt_bias, L1_conv_A_log, L1_conv_D, L1_conv_norm_w, L1_conv_norm_b, L1_conv_out_proj_w):
    import jax
    import jax.numpy as jnp
    def _L0_conv_ref(x, ln_w, ln_b, w_qkv, bn1_g, bn1_b, bn1_m, bn1_v, w_proj, bn2_g, bn2_b, bn2_m, bn2_v):
        import jax, jax.numpy as jnp
        import numpy as np
        DIM = 384
        PD = 96
        QK = 16
        VD = PD
        QKV_OUT = 2 * QK + VD
        EPS = 1e-05

        def _bn(y, g, b, m, v):
            inv = g / jnp.sqrt(v + EPS)
            return y * inv[None, :, None, None] + (b - m * inv)[None, :, None, None]
        B, C, H, W = x.shape
        N = H * W
        scale = QK ** (-0.5)
        x_attn = x[:, :PD]
        x_skip = x[:, PD:]
        u = x_attn.mean(axis=1, keepdims=True)
        s = ((x_attn - u) ** 2).mean(axis=1, keepdims=True)
        xn = (x_attn - u) / jnp.sqrt(s + EPS)
        xn = xn * ln_w[None, :, None, None] + ln_b[None, :, None, None]
        qkv = jnp.einsum('oc,bchw->bohw', w_qkv, xn)
        qkv = _bn(qkv, bn1_g, bn1_b, bn1_m, bn1_v)
        q = qkv[:, :QK].reshape(B, QK, N)
        k = qkv[:, QK:2 * QK].reshape(B, QK, N)
        v = qkv[:, 2 * QK:].reshape(B, VD, N)
        attn = jax.nn.softmax(jnp.einsum('bcn,bcm->bnm', q, k) * scale, axis=-1)
        out = jnp.einsum('bcn,bmn->bcm', v, attn).reshape(B, VD, H, W)
        xm = jax.nn.relu(jnp.concatenate([out, x_skip], axis=1))
        y = jnp.einsum('oc,bchw->bohw', w_proj, xm)
        y = _bn(y, bn2_g, bn2_b, bn2_m, bn2_v)
        return y

    def _L1_conv_ref(u, in_proj_w, conv_w, conv_b, dt_bias, A_log, D, norm_w, norm_b, out_proj_w):
        import jax, jax.numpy as jnp
        import numpy as np
        D_MODEL = 384
        D_STATE = 64
        D_CONV = 3
        EXPAND = 2
        HEADDIM = 64
        NGROUPS = 1
        CHUNK = 256
        D_INNER = EXPAND * D_MODEL
        NHEADS = D_INNER // HEADDIM
        CONV_DIM = D_INNER + 2 * NGROUPS * D_STATE
        D_IN_PROJ = 2 * D_INNER + 2 * NGROUPS * D_STATE + NHEADS
        EPS = 1e-05

        def _chunk_scan(x, dt, A, Bm, Cm):
            b, l, h, p = x.shape
            nc = l // CHUNK
            xc = x.reshape(b, nc, CHUNK, h, p)
            dtc = dt.reshape(b, nc, CHUNK, h)
            hpg = h // NGROUPS
            Bh = jnp.repeat(Bm.reshape(b, nc, CHUNK, NGROUPS, D_STATE), hpg, axis=3)
            Ch = jnp.repeat(Cm.reshape(b, nc, CHUNK, NGROUPS, D_STATE), hpg, axis=3)
            dA = dtc * A
            dA_cs = jnp.cumsum(dA, axis=2)
            Lmat = jnp.exp(dA_cs[:, :, :, None, :] - dA_cs[:, :, None, :, :])
            causal = jnp.tril(jnp.ones((CHUNK, CHUNK), bool))
            att = jnp.einsum('bcihn,bcjhn->bcijh', Ch, Bh) * Lmat * dtc[:, :, None, :, :]
            att = jnp.where(causal[None, None, :, :, None], att, 0.0)
            y_intra = jnp.einsum('bcijh,bcjhp->bcihp', att, xc)
            decay_to_end = jnp.exp(dA_cs[:, :, -1:, :] - dA_cs)
            states = jnp.einsum('bcjhn,bcjh,bcjhp->bchpn', Bh, decay_to_end * dtc, xc)
            chunk_decay = jnp.exp(dA_cs[:, :, -1, :])

            def step(carry, inp):
                st, dec = inp
                new = carry * dec[:, :, None, None] + st
                return (new, carry)
            init = jnp.zeros((b, h, p, D_STATE), x.dtype)
            _, prevs = jax.lax.scan(step, init, (jnp.moveaxis(states, 1, 0), jnp.moveaxis(chunk_decay, 1, 0)))
            prev_states = jnp.moveaxis(prevs, 0, 1)
            y_inter = jnp.einsum('bcihn,bcih,bchpn->bcihp', Ch, jnp.exp(dA_cs), prev_states)
            return (y_intra + y_inter).reshape(b, l, h, p)
        B, C, H, W = u.shape
        L = H * W
        useq = u.reshape(B, C, L).transpose(0, 2, 1)
        zxbcdt = useq @ in_proj_w.T
        z = zxbcdt[..., :D_INNER]
        xBC = zxbcdt[..., D_INNER:D_INNER + CONV_DIM]
        dt = jax.nn.softplus(zxbcdt[..., D_INNER + CONV_DIM:] + dt_bias)
        xBC = xBC.reshape(B, H, W, CONV_DIM)
        kern = jnp.transpose(conv_w, (2, 3, 1, 0))
        xBC = jax.lax.conv_general_dilated(xBC, kern, (1, 1), 'SAME', dimension_numbers=('NHWC', 'HWIO', 'NHWC'), feature_group_count=CONV_DIM) + conv_b
        xBC = jax.nn.silu(xBC).reshape(B, L, CONV_DIM)
        x = xBC[..., :D_INNER].reshape(B, L, NHEADS, HEADDIM)
        Bm = xBC[..., D_INNER:D_INNER + NGROUPS * D_STATE].reshape(B, L, NGROUPS, D_STATE)
        Cm = xBC[..., D_INNER + NGROUPS * D_STATE:].reshape(B, L, NGROUPS, D_STATE)
        A = -jnp.exp(A_log)
        y = _chunk_scan(x, dt, A, Bm, Cm) + D[None, None, :, None] * x
        y = y.reshape(B, L, D_INNER)
        mu = jnp.mean(y, axis=-1, keepdims=True)
        var = jnp.var(y, axis=-1, keepdims=True)
        y = (y - mu) / jnp.sqrt(var + EPS) * norm_w + norm_b
        y = y * z
        out = y @ out_proj_w.T
        return out.reshape(B, H, W, C).transpose(0, 3, 1, 2)

    def _gn(v, G=32, eps=1e-5):
        B_, C_, H_, W_ = v.shape
        g = v.reshape(B_, G, C_ // G, H_, W_)
        m = jnp.mean(g, axis=(2, 3, 4), keepdims=True)
        s = jnp.var(g, axis=(2, 3, 4), keepdims=True)
        return ((g - m) / jnp.sqrt(s + eps)).reshape(v.shape)

    def _ln_c(v, eps=1e-6):
        m = jnp.mean(v, axis=1, keepdims=True)
        s = jnp.var(v, axis=1, keepdims=True)
        return (v - m) / jnp.sqrt(s + eps)

    def _ln_t(v, eps=1e-5):
        m = jnp.mean(v, axis=-1, keepdims=True)
        s = jnp.var(v, axis=-1, keepdims=True)
        return (v - m) / jnp.sqrt(s + eps)

    def _to_tokens(v):
        B_, C_, H_, W_ = v.shape
        return v.reshape(B_, C_, H_ * W_).transpose(0, 2, 1)
    def _from_tokens(t, like):
        B_, C_, H_, W_ = like.shape
        return t.transpose(0, 2, 1).reshape(B_, C_, H_, W_)

    x = x + _L0_conv_ref(_gn(x), L0_conv_ln_w, L0_conv_ln_b, L0_conv_w_qkv, L0_conv_bn1_g, L0_conv_bn1_b, L0_conv_bn1_m, L0_conv_bn1_v, L0_conv_w_proj, L0_conv_bn2_g, L0_conv_bn2_b, L0_conv_bn2_m, L0_conv_bn2_v)
    x = x + _L1_conv_ref(_gn(x), L1_conv_in_proj_w, L1_conv_conv_w, L1_conv_conv_b, L1_conv_dt_bias, L1_conv_A_log, L1_conv_D, L1_conv_norm_w, L1_conv_norm_b, L1_conv_out_proj_w)
    return x


_drawn_inputs = setup_inputs


def setup_inputs(seed=0):
    import zlib

    import numpy as np

    out = dict(_drawn_inputs(seed))
    spreads = {'L0_conv_ln_w': (1.0, 0.6),
     'L0_conv_ln_b': (0.0, 0.8),
     'L1_conv_D': (1.0, 0.553),
     'L1_conv_norm_w': (1.0, 0.2),
     'L1_conv_norm_b': (0.0, 0.3)}
    factors = {'L0_conv_w_qkv': 7.115,
     'L0_conv_bn1_g': 8.0,
     'L0_conv_bn1_b': 6.575,
     'L0_conv_bn1_m': 6.288,
     'L0_conv_bn1_v': 8.0,
     'L1_conv_conv_b': 6.606,
     'L0_conv_bn2_b': 3.855,
     'L0_conv_bn2_m': 3.555}
    for name, (base, spread) in spreads.items():
        noise = np.random.default_rng([zlib.crc32(name.encode()), seed]).standard_normal(out[name].shape)
        drawn = base * np.exp(spread * noise) if base else spread * noise
        out[name] = jnp.asarray(drawn.astype(out[name].dtype))
    for name, factor in factors.items():
        out[name] = (out[name] * factor).astype(out[name].dtype)
    return out
```

```python
from contextlib import ExitStack

import concourse.bass as bass
import concourse.mybir as mybir
import numpy as np

F32 = mybir.dt.float32
BF16 = mybir.dt.bfloat16
ALU = mybir.AluOpType
ACT = mybir.ActivationFunctionType
AX = mybir.AxisListType

B, C, H, W = 4, 384, 64, 64
L = H * W
P = 128
CT = C // P
TB = 512
NB = L // TB
ROWS = TB // W
WP = W + 2
GROUPS = 32
PD, QK = 96, 16
DI = 768
NT = DI // P
NS = 64
HD = 64
NH = DI // HD
XT_ = (DI + 2 * NS) // P
DIN = 2 * DI + 2 * NS
CH = 128
NC = TB // CH
HP = NT // 2
NU = 2 * NC
R3 = 64 + NH
QG = 6
QR = QG * QK
KS = QR + 3
QPART = (0, 0, 1, 1, 0, 2)
KPART = (0, 1, 0, 1, 2, 0)
NEG = -1e30

V_BN1, V_LN, V_BN2, V_CW, V_CB, V_NW, V_NB, V_D, V_DTB, V_AL = 0, 12, 14, 26, 89, 96, 102, 108, 114, 115
NV = 116
K_ID, K_ONE, K_M768, K_M96, K_G, K_GT, K_MASK = 0, 128, 256, 384, 480, 576, 960
K_EPS = K_MASK + 8
NK = K_EPS + 1
B_ID, B_BIG, B_DELTA, B_ONES, B_SEL = 0, 128, 512, 1280, 1536
NBF = 1664


def constants():
    k = np.zeros((P, NK), np.float32)
    k[:, K_ID:K_ID + P] = np.eye(P)
    k[:, K_ONE:K_ONE + P] = 1
    k[:, K_M768:K_M768 + P] = 1 / DI
    k[:, K_M96:K_M96 + PD] = 1 / PD
    k[:, K_EPS] = 1e-5
    per = C // GROUPS
    for t in range(CT):
        for p in range(P):
            g = (t * P + p) // per
            k[p, K_G + t * GROUPS + g] = 1 / per
            k[g, K_GT + t * P + p] = 1
    for r in range(QR + 3):
        q = QPART[r // QK] if r < QR else r - QR
        kk = KPART[r // QK] if r < QR else 0
        k[r, K_MASK + 0], k[r, K_MASK + 1] = -(q > 0), -(q == 2)
        k[r, K_MASK + 2], k[r, K_MASK + 3] = -(kk > 0), -(kk == 2)
    bf = np.zeros((P, NBF), np.float32)
    bf[:, B_ID:B_ID + P] = np.eye(P)
    j, i = np.arange(P)[:, None], np.arange(CH)[None, :]
    bf[:, B_BIG:B_BIG + HP * CH] = np.tile(np.where(j > i, NEG, 0), (1, HP))
    for part in range(3):
        for h in range(NH):
            r = 32 * part + h
            k[r, K_MASK + 4], k[r, K_MASK + 5] = -(part > 0), -(part == 2)
            k[r, K_MASK + 6 + h % 2] = -1
            bf[r, B_DELTA + (h // 2) * CH:B_DELTA + (h // 2 + 1) * CH] = 1
            bf[r, B_ONES + (h % 2) * P:B_ONES + (h % 2 + 1) * P] = 1
            bf[r, B_SEL + (h % 2) * 64:B_SEL + (h % 2 + 1) * 64] = 1
    return k, bf.astype(mybir.dt.np(BF16))


ONE = 1


class Steps:

    def __init__(self, eng, sem):
        self.eng, self.sem, self.base, self.n = eng, sem, 0, 0

    def enter(self, base):
        self.base, self.n = base, 0

    def __call__(self, ins):
        ins.then_inc(self.sem, 1)
        self.n += 1

    def join(self, but=0):
        self.eng.wait_ge(self.sem, self.base + (self.n - but + ONE))


def program(nc, x, vecs, wqkv, wproj, win, wdt, wout, consts, constb, out):
    ctx = ExitStack()
    with ctx:
        def sb(name, shape, dt=F32):
            return ctx.enter_context(nc.sbuf_tensor(name, shape, dt))

        def sem(name):
            return ctx.enter_context(nc.semaphore(name))

        xs_ = sb("x_sample", [P, CT, L])
        w_in = sb("w_in", [P, CT, DIN])
        w_out = sb("w_out", [P, NT, C])
        w_proj = sb("w_proj", [P, CT, C])
        w_dt_raw = sb("w_dt_raw", [P, CT, R3])
        w_dt = sb("w_dt", [P, CT, R3])
        w_qkv = sb("w_qkv", [PD, 3, PD])
        vec = sb("vec", [P, NV])
        kf = sb("kf", [P, NK])
        kb = sb("kb", [P, NBF], BF16)
        bn1s, bn1o = sb("bn1s", [PD, 3]), sb("bn1o", [PD, 3])
        bn2s, bn2o = sb("bn2s", [P, CT]), sb("bn2o", [P, CT])
        a_neg = sb("a_neg", [R3, 1])
        chan_stats = sb("chan_stats", [P, CT, NB, 6])
        chan_mv = sb("chan_mv", [P, CT, 2])
        group_mv = sb("group_mv", [GROUPS, 2])
        group_sc = sb("group_sc", [GROUPS, 4])
        gn_ab = sb("gn_ab", [P, CT, 2])
        beta = sb("beta", [P, XT_ + NT + 1])
        maxes = sb("maxes", [P, 4, 8])
        max4 = sb("max4", [P, 4])
        ident, one, mean768 = kf[:, K_ID:K_ID + P], kf[:, K_ONE:K_ONE + P], kf[:, K_M768:K_M768 + P]
        mean96 = kf[0:PD, K_M96:K_M96 + PD]

        def eps(rows=slice(0, P)):
            return kf[rows, K_EPS:K_EPS + 1]

        def mask(n, rows):
            return kf[rows, K_MASK + n:K_MASK + n + 1]

        AR = 29400
        arena = sb("arena", [P, AR])
        at = [0]

        def take(cols, dt=F32, rows=slice(0, P)):
            words = cols if dt == F32 else cols // 2
            v = arena[rows, at[0]:at[0] + words]
            at[0] += words
            assert at[0] <= AR, at[0]
            return v if dt == F32 else v.bitcast(dt)

        def shaped(v, *dims):
            names = "abcd"[:len(dims)]
            return v.rearrange(f"p ({' '.join(names)}) -> p {' '.join(names)}", **dict(zip(names, dims)))

        xn = shaped(take(CT * L), CT, L)
        q_st, k_st = take(L, BF16), take(L, BF16)
        v_t = shaped(take(32 * 97), 32, 97)
        common = at[0]
        ln_x = shaped(take(2 * TB), 2, TB)
        ln_sq = shaped(take(2 * TB), 2, TB)
        ln_y = shaped(take(2 * TB), 2, TB)
        qk_f = shaped(take(4 * TB), 2, 2, TB)
        qk_h = shaped(take(4 * TB, BF16), 2, 2, TB)
        qk_m = shaped(take(4 * TB, BF16), 2, 2, TB)
        v_sb = shaped(take(2 * TB), 2, TB)
        at[0] = common
        p_sb = shaped(take(4 * TB), 2, 2, TB)
        cat = shaped(take(CT * TB), CT, TB)
        rec_b = take(TB)
        rec = take(TB)
        proj_y = shaped(take(CT * TB), CT, TB)
        negmax = shaped(take(4 * KS), 4, KS)
        nm_f, nm_h, nm_m = take(TB), take(TB, BF16), take(TB, BF16)
        at[0] = 0
        pre = shaped(take(XT_ * (ROWS + 2) * WP), XT_, ROWS + 2, WP)
        acc = shaped(take(XT_ * TB), XT_, TB)
        xbc = shaped(take(XT_ * TB), XT_, TB)
        y_sb = shaped(take(NT * TB), NT, TB)
        both = take(4 * HP * CH * 2)
        decay = shaped(both[:, 0:4 * HP * CH], 2, 2, HP, CH)
        att = shaped(both[:, 4 * HP * CH:], 2, 2, HP, CH)
        sq = shaped(both, NT, TB)
        grow = shaped(take(2 * HP * CH), 2, HP, CH)
        c_dec = shaped(take(2 * HP * CH), 2, HP, CH)
        both_x = take(2 * 2 * 2 * HP * HD)
        x_dt = shaped(both_x[:, 0:4 * HP * HD], 2, HP, 2, HD)
        x_w = shaped(both_x[:, 4 * HP * HD:], 2, HP, 2, HD)
        sum3 = shaped(both_x, HP, TB)
        c_dup = take(TB)
        state = shaped(take(NT * P), NT, P)
        st_dec = shaped(take(HP * P), HP, P)
        small = shaped(take(2 * 204), 2, 204)
        cs_diag = shaped(take(NT * TB, BF16), NT, TB)
        cs_neg = shaped(take(2 * TB, BF16), 2, TB)
        sp_e, sp_l, sp_d, sp_r, dt_sb, cs = (take(TB) for _ in range(6))
        cs_st, cs_h = take(TB, BF16), take(TB, BF16)
        row = take(TB)

        ps = ctx.enter_context(nc.psum_tensor("ps", [P, 8, TB], F32))

        names = """
        weights_loaded waited steps_v steps_a steps_p prepared vec_prepared met_v met
        x_loaded0 x_loaded1 x_loaded2 win_loaded stored stats_ready group_sums groups_ready group_back ab_ready
        vars_ready roots_ready ln_root row_root xn0_ready xn1_ready xn2_ready cleared
        mean_ready centred squared var_ready scaled ln_ready q_ready k_ready v_ready qk_taken qk_rounded
        v_taken vt_ready vt_copied q_stacked k_stacked
        max_scores max_read nm_ready nm_turned nm_taken nm_stacked
        scores exps pv_done recip_ready recip_spread recip_copied normed skip_relu proj_mm proj_taken x1_added
        beta_mm beta_ready w_scaled row0_mm row0_done row0_carried top_clear bottom_clear state_clear
        pj_mm pj_read0 pj_read1  centre_done conv_done silu_done carried bc_dup
        small_mm small_copied xt_mm xdt_ready e_mm exp_done xw_ready cd_ready sdec_ready att_ready
        y_mm y_read st_mm state_done
        dt_mm dt_abs dt_relu sp_ln sp_prod sp_recip dt_ready cs_rounded cs_stacked diag_ready
        sum1_ready y_centred sq_ready sum2_ready y_scaled y_affine z_copied gated out_read
        """.split()
        s = {n: sem(n) for n in names}

        started = sem("started")
        block = ctx.enter_context(nc.Block())
        MEETS = 4

        def own(eng):
            eng.sem_inc(s["waited"], 1)

        def meet(eng, b, n):
            own(eng)
            eng.drain().then_inc(s["met"], 1)
            eng.wait_ge(s["met"], ONE + 5 * (MEETS * b + n + 1))
            own(eng)

        def begin(eng):
            eng.wait_ge(started, 1)

        @block.sync
        def _(sp):
            for first in s.values():
                sp.sem_inc(first, ONE)
            sp.sem_inc(started, 1)
            for dst, src in ((vec, vecs), (kf, consts), (kb, constb), (w_qkv, wqkv), (w_proj, wproj),
                             (w_dt_raw, wdt), (w_out, wout)):
                sp.dma_start(dst[:], src[:]).then_inc(s["weights_loaded"], 16)
            with sp.Fori(0, B) as b:
                sp.wait_ge(s["stored"], ONE + b * (16 * CT * NB))
                own(sp)
                for t in range(CT):
                    src = x.rearrange("b (t p) l -> (b t) p l", p=P)
                    sp.dma_start(xs_[:, t, :], src[b * CT + t]).then_inc(s[f"x_loaded{t}"], 16)
                sp.dma_start(w_in[:], win[:]).then_inc(s["win_loaded"], 16)
                for n in range(MEETS - 1):
                    meet(sp, b, n)
                with sp.Fori(0, NB) as i:
                    G = sp.snap(b * NB + i)
                    sp.wait_ge(s["silu_done"], ONE + G * XT_ + 1)
                    for half in range(2):
                        sp.dma_start(c_dup[64 * half:64 * half + 64, :], xbc[64:128, XT_ - 1, :]).then_inc(s["bc_dup"], 16)
                    for m in range(CT):
                        sp.wait_ge(s["out_read"], ONE + G * CT + m + 1)
                        own(sp)
                        dst = out.rearrange("b (t p) l -> (b t) p l", p=P)
                        sp.dma_start(dst[b * CT + m, :, bass.ds(i * TB, TB)],
                                     xs_[:, m, bass.ds(i * TB, TB)]).then_inc(s["stored"], 16)
                meet(sp, b, MEETS - 1)
            sp.wait_ge(s["stored"], ONE + 16 * B * CT * NB)

        def gn_pe(pe, n):
            pe.wait_ge(s["stats_ready"], ONE + n + 1)
            for t in range(CT):
                mm = nc.tensor.matmul(ps[0:GROUPS, 7, 0:2], kf[:, K_G + t * GROUPS:K_G + (t + 1) * GROUPS],
                                      chan_mv[:, t, :], start=(t == 0), stop=(t == CT - 1))
            mm.then_inc(s["group_sums"], 1)
            pe.wait_ge(s["groups_ready"], ONE + n + 1)
            for t in range(CT):
                mm = nc.tensor.matmul(ps[:, 7, 8 + 2 * t:10 + 2 * t], kf[0:GROUPS, K_GT + t * P:K_GT + (t + 1) * P],
                                      group_sc[:, 2:4], start=True, stop=True)
            mm.then_inc(s["group_back"], 1)

        def qkv_pe(pe, b, u):
            G = pe.snap(b * (NB // 2) + u)
            for j in range(2):
                pe.wait_ge(s["v_taken"], ONE + 2 * G)
                mm = nc.tensor.matmul(ps[0:PD, j, :], mean96, xn[0:PD, 0, bass.ds(u * (2 * TB) + j * TB, TB)],
                                      start=True, stop=True)
                mm.then_inc(s["mean_ready"], 1)
            for j in range(2):
                pe.wait_ge(s["squared"], ONE + 2 * G + j + 1)
                pe.wait_ge(s["vt_copied"], ONE + 2 * G)
                nc.tensor.matmul(ps[0:PD, 2 + j, :], mean96, ln_sq[0:PD, j, :], start=True, stop=True)\
                    .then_inc(s["var_ready"], 1)
            for j in range(2):
                pe.wait_ge(s["ln_ready"], ONE + 2 * G + j + 1)
                pe.wait_ge(s["qk_taken"], ONE + 4 * G)
                for w, name in ((0, "q_ready"), (1, "k_ready")):
                    nc.tensor.matmul(ps[0:PD, 4 + 2 * w + j, :], w_qkv[:, w, :], ln_y[0:PD, j, :],
                                     start=True, stop=True).then_inc(s[name], 1)
                nc.tensor.matmul(ps[0:PD, j, :], w_qkv[:, 2, :], ln_y[0:PD, j, :], start=True, stop=True)\
                    .then_inc(s["v_ready"], 1)
            for j in range(2):
                pe.wait_ge(s["v_taken"], ONE + 2 * G + j + 1)
                for c in range(TB // P):
                    mm = nc.tensor.transpose(ps[:, 2 + j, c * PD:(c + 1) * PD], v_sb[0:PD, j, c * P:(c + 1) * P],
                                             ident[0:PD, 0:PD])
                mm.then_inc(s["vt_ready"], 1)

        def max_pe(pe, b, nq, g, n):
            mt, kc = n // NB, n % NB
            pe.wait_ge(s["max_read"], ONE + 32 * g + (n - 1 if n >= 2 else 0))
            nc.tensor.matmul(ps[:, 4 + n % 2, :], q_st[0:QR, bass.ds(nq * TB + mt * P, P)],
                             k_st[0:QR, kc * TB:(kc + 1) * TB], start=True, stop=True).then_inc(s["max_scores"], 1)

        def turn_pe(pe, g, now):
            pe.wait_ge(s["nm_ready"], ONE + g + 1)
            pe.wait_ge(s["proj_taken"], ONE + CT * now)
            for mt in range(4):
                mm = nc.tensor.matmul(ps[0:KS, 7, mt * P:(mt + 1) * P], negmax[:, mt, :], ident,
                                      start=True, stop=True)
            mm.then_inc(s["nm_turned"], 1)

        MAX_AT = [min(3 * st, 32) for st in range(17)]
        TURN_AT = 13

        def attend_pe(pe, b, qb, has_next):
            g = pe.snap(b * NB + qb) if not isinstance(qb, int) else b * NB + qb
            pe.wait_ge(s["nm_stacked"], ONE + g + 1)
            for st in range(17):
                if st < 16:
                    if st >= 2:
                        pe.wait_ge(s["exps"], ONE + 16 * g + st - 1)
                    for r in range(2):
                        kt = 2 * st + r
                        mm = nc.tensor.matmul(ps[:, 2 * (st % 2) + r, :], k_st[0:KS, kt * P:(kt + 1) * P],
                                              q_st[0:KS, bass.ds(qb * TB, TB)], start=True, stop=True)
                    mm.then_inc(s["scores"], 1)
                    if has_next:
                        for n in range(MAX_AT[st], MAX_AT[st + 1]):
                            max_pe(pe, b, qb + 1, g + 1, n)
                        if st == TURN_AT:
                            turn_pe(pe, g + 1, g)
                if st >= 1:
                    pe.wait_ge(s["exps"], ONE + 16 * g + st)
                    if st == 1:
                        pe.wait_ge(s["normed"], ONE + g)
                    for r in range(2):
                        kt = 2 * (st - 1) + r
                        mm = nc.tensor.matmul(ps[0:97, 6, :], v_t[:, kt, :], p_sb[:, (st - 1) % 2, r, :],
                                              start=(kt == 0), stop=(kt == 31))
                    mm.then_inc(s["pv_done"], 1)
            pe.wait_ge(s["recip_ready"], ONE + g + 1)
            pe.wait_ge(s["nm_taken"], ONE + (g + 2 if has_next else g + 1))
            nc.tensor.matmul(ps[0:PD, 7, :], one[96:97, 0:PD], rec[96:97, :], start=True, stop=True)\
                .then_inc(s["recip_spread"], 1)
            pe.wait_ge(s["normed"], ONE + g + 1)
            pe.wait_ge(s["skip_relu"], ONE + 2 * g + 2)
            for m in range(CT):
                if m:
                    pe.wait_ge(s["proj_taken"], ONE + CT * g + m)
                for t in range(CT):
                    mm = nc.tensor.matmul(ps[:, 7, :], w_proj[:, t, m * P:(m + 1) * P], cat[:, t, :],
                                          start=(t == 0), stop=(t == CT - 1))
                mm.then_inc(s["proj_mm"], 1)

        OUTS = 2 + NT + CT
        PER = XT_ + OUTS
        ALL = NB * PER

        def item(kind, i, last, j):
            if kind == "A":
                return XT_ + j, PER
            return (2 * XT_ if not last else XT_) + j, PER

        def pj_wait(pe, b, i, at0):
            pe.wait_ge(s[f"pj_read{at0 % 2}"], ONE + b * (ALL // 2) + i * (PER // 2) + at0 // 2)

        def in_proj_pe(pe, b, i, t, at0, rows):
            pj_wait(pe, b, i, at0)
            n = rows * W
            start = (i + 1) * TB + W
            for k in range(CT):
                mm = nc.tensor.matmul(ps[:, at0 % 2, 0:n], w_in[:, k, DI + t * P:DI + (t + 1) * P],
                                      xs_[:, k, bass.ds(start, n)], start=(k == 0), stop=(k == CT - 1))
            mm.then_inc(s["pj_mm"], 1)

        def dt_pe(pe, G, i1):
            pe.wait_ge(s["small_copied"], ONE + NC * G)
            for k in range(CT):
                mm = nc.tensor.matmul(ps[0:R3, 5, :], w_dt[:, k, :], xs_[:, k, bass.ds(i1 * TB, TB)],
                                      start=(k == 0), stop=(k == CT - 1))
            mm.then_inc(s["dt_mm"], 1)

        def unit_a_pe(pe, G, u):
            c, hf = u // 2, u % 2
            tok = slice(c * CH, (c + 1) * CH)
            pairs = slice(HP * hf, HP * hf + HP)
            if hf == 0:
                if c == 0:
                    pe.wait_ge(s["bc_dup"], ONE + 32 * G + 32)
                    pe.wait_ge(s["silu_done"], ONE + XT_ * G + XT_)
                    pe.wait_ge(s["dt_ready"], ONE + G + 1)
                    pe.wait_ge(s["dt_abs"], ONE + G + 1)
                    pe.wait_ge(s["dt_relu"], ONE + G + 1)
                pe.wait_ge(s["small_copied"], ONE + NC * G + c)
                nc.tensor.matmul(ps[:, 5, 0:P], xbc[0:NS, XT_ - 1, tok], c_dup[0:NS, tok], start=True, stop=True)
                nc.tensor.transpose(ps[:, 5, P:P + NS], xbc[0:NS, XT_ - 1, tok], ident[0:NS, 0:NS])
                nc.tensor.transpose(ps[:, 5, P + NS:P + NS + NH], dt_sb[0:NH, tok], ident[0:NH, 0:NH])\
                    .then_inc(s["small_mm"], 1)
            pe.wait_ge(s["xdt_ready"], ONE + NU * G + u)
            for t in range(HP):
                mm = nc.tensor.transpose(ps[:, 4, t * P:(t + 1) * P], xbc[:, HP * hf + t, tok], ident)
            mm.then_inc(s["xt_mm"], 1)
            if hf == 0:
                pe.wait_ge(s["diag_ready"], ONE + NC * G + c + 1)
            for par in range(3):
                e = 3 * u + par
                pe.wait_ge(s["exp_done"], ONE + 3 * NU * G + (e - 1 if e >= 2 else 0))
                bank = ps[:, 2 + e % 2, 0:HP * CH]
                diag = cs_diag[0:R3, pairs, tok]
                if par == 2:
                    mm = nc.tensor.matmul(bank, kb[0:R3, B_SEL:B_SEL + P], diag, start=True, stop=True)
                else:
                    nc.tensor.matmul(bank, kb[0:R3, B_ONES + par * P:B_ONES + (par + 1) * P], diag,
                                     start=True, stop=False)
                    nc.tensor.matmul(bank, cs_neg[0:R3, par, tok],
                                     kb[0:R3, B_DELTA + HP * hf * CH:B_DELTA + HP * (hf + 1) * CH],
                                     start=False, stop=False)
                    mm = nc.tensor.matmul(bank, kb[:, B_ID:B_ID + P], kb[:, B_BIG:B_BIG + HP * CH],
                                          start=False, stop=True)
                mm.then_inc(s["e_mm"], 1)

        def unit_b_pe(pe, b, G, u):
            c, hf, d = u // 2, u % 2, u % 2
            pe.wait_ge(s["y_read"], ONE + NU * G + u)
            pe.wait_ge(s["cd_ready"], ONE + NU * G + u + 1)
            pe.wait_ge(s["att_ready"], ONE + NU * G + u + 1)
            pe.wait_ge(s["state_done"], ONE + NU * G + max(u - 1, 0))
            if u < 2:
                pe.wait_ge(s["state_clear"], ONE + b + 1)
            for t in range(HP):
                y = ps[:, 6, t * CH:(t + 1) * CH]
                nc.tensor.matmul(y, state[:, HP * hf + t, :], c_dec[:, d, t, :], start=True, stop=False,
                                 skip_group_check=True)
                for par in range(2):
                    mm = nc.tensor.matmul(y[64 * par:64 * par + 64, :], x_dt[:, d, t, par, :], att[:, d, par, t, :],
                                          start=False, stop=(par == 1), skip_group_check=True)
            mm.then_inc(s["y_mm"], 1)
            pe.wait_ge(s["state_done"], ONE + NU * G + u)
            pe.wait_ge(s["xw_ready"], ONE + NU * G + u + 1)
            for par in range(2):
                mm = nc.tensor.matmul(ps[64 * par:64 * par + 64, 7, 0:HP * HD], small[:, c % 2, P:P + NS],
                                      x_w[:, d, :, par, :], start=True, stop=True)
            mm.then_inc(s["st_mm"], 1)

        def block_pe(pe, b, i, nxt):
            G = b * NB + i if isinstance(i, int) else pe.snap(b * NB + i)
            for u in range(NU):
                unit_a_pe(pe, G, u)
                if u:
                    unit_b_pe(pe, b, G, u - 1)
                if nxt and u % 2 == 1:
                    for t in (u - 1, u):
                        if t < XT_:
                            in_proj_pe(pe, b, i, t, item("A", i, False, t)[0], nxt)
            unit_b_pe(pe, b, G, NU - 1)
            if nxt:
                dt_pe(pe, G + 1, i + 1)
            B0 = item("B", i, not nxt, 0)[0]
            pj_wait(pe, b, i, B0)
            pe.wait_ge(s["sum1_ready"], ONE + G + 1)
            nc.tensor.matmul(ps[:, B0 % 2, :], mean768, row, start=True, stop=True).then_inc(s["pj_mm"], 1)

            def z(t, at0):
                pj_wait(pe, b, i, at0)
                for k in range(CT):
                    mm = nc.tensor.matmul(ps[:, at0 % 2, :], w_in[:, k, t * P:(t + 1) * P],
                                          xs_[:, k, bass.ds(i * TB, TB)], start=(k == 0), stop=(k == CT - 1))
                mm.then_inc(s["pj_mm"], 1)

            for t in range(4):
                z(t, B0 + 1 + t)
            pj_wait(pe, b, i, B0 + 5)
            pe.wait_ge(s["sum2_ready"], ONE + G + 1)
            nc.tensor.matmul(ps[:, (B0 + 5) % 2, :], mean768, row, start=True, stop=True).then_inc(s["pj_mm"], 1)
            for t in range(4, NT):
                z(t, B0 + 2 + t)
            for m in range(CT):
                at0 = B0 + 2 + NT + m
                pj_wait(pe, b, i, at0)
                for t in range(NT):
                    if m == 0:
                        pe.wait_ge(s["gated"], ONE + NT * G + t + 1)
                    mm = nc.tensor.matmul(ps[:, at0 % 2, :], w_out[:, t, m * P:(m + 1) * P], y_sb[:, t, :],
                                          start=(t == 0), stop=(t == NT - 1))
                mm.then_inc(s["pj_mm"], 1)

        @block.tensor
        def _(pe):
            begin(pe)
            pe.wait_ge(s["weights_loaded"], ONE + 16 * 7)
            with pe.Fori(0, B) as b:
                gn_pe(pe, 2 * b)
                pe.wait_ge(s["xn0_ready"], ONE + b + 1)
                own(pe)
                with pe.Fori(0, NB // 2) as u:
                    qkv_pe(pe, b, u)
                meet(pe, b, 0)
                for n in range(32):
                    max_pe(pe, b, 0, b * NB, n)
                turn_pe(pe, b * NB, b * NB)
                with pe.Fori(0, NB - 1) as qb:
                    attend_pe(pe, b, qb, True)
                attend_pe(pe, b, NB - 1, False)
                meet(pe, b, 1)
                gn_pe(pe, 2 * b + 1)
                pe.wait_ge(s["win_loaded"], ONE + 16 * b + 16)
                pe.wait_ge(s["ab_ready"], ONE + 2 * b + 2)
                for m in range(XT_ + NT + 1):
                    rows = P if m < XT_ + NT else R3
                    for k in range(CT):
                        w = w_in[:, k, m * P:(m + 1) * P] if m < XT_ + NT else w_dt_raw[:, k, :]
                        mm = nc.tensor.matmul(ps[0:rows, 6, m:m + 1], w, gn_ab[:, k, 1:2], start=(k == 0),
                                              stop=(k == CT - 1))
                mm.then_inc(s["beta_mm"], 1)
                meet(pe, b, 2)
                for t in range(XT_):
                    for k in range(CT):
                        mm = nc.tensor.matmul(ps[:, 4, t * W:(t + 1) * W], w_in[:, k, DI + t * P:DI + (t + 1) * P],
                                              xs_[:, k, 0:W], start=(k == 0), stop=(k == CT - 1))
                mm.then_inc(s["row0_mm"], 1)
                dt_pe(pe, b * NB, 0)
                for t in range(XT_):
                    in_proj_pe(pe, b, -1, t, PER + t, ROWS)
                pe.wait_ge(s["row0_done"], ONE + b + 1)
                own(pe)
                with pe.Fori(0, NB - 2) as i:
                    block_pe(pe, b, i, ROWS)
                block_pe(pe, b, NB - 2, ROWS - 1)
                block_pe(pe, b, NB - 1, 0)
                meet(pe, b, 3)

        def gn_act(act, n):
            act.wait_ge(s["vars_ready"], ONE + n + 1)
            nc.scalar.activation(group_sc[:, 1:2], group_sc[:, 1:2], ACT.Sqrt, bias=eps(slice(0, GROUPS)))\
                .then_inc(s["roots_ready"], 1)

        def block_act(act, b, i, nxt, step):
            G = b * NB + i if isinstance(i, int) else act.snap(b * NB + i)
            act.wait_ge(s["gated"], ONE + NT * G)
            act.wait_ge(s["conv_done"], ONE + XT_ * G + XT_)
            for t in (XT_ - 1, *range(XT_ - 1)):
                nc.scalar.activation(xbc[:, t, :], acc[:, t, :], ACT.Silu).then_inc(s["silu_done"], 1)
            for u in range(NU):
                c, hf, d = u // 2, u % 2, u % 2
                if hf == 0:
                    act.wait_ge(s["small_mm"], ONE + NC * G + c + 1)
                    act.wait_ge(s["att_ready"], ONE + NU * G + max(2 * c - 2, 0))
                    act.wait_ge(s["st_mm"], ONE + NU * G + max(2 * c - 2, 0))
                    nc.scalar.copy(small[:, c % 2, :], ps[:, 5, 0:204]).then_inc(s["small_copied"], 1)
                for par in range(3):
                    e = 3 * u + par
                    act.wait_ge(s["e_mm"], ONE + 3 * NU * G + e + 1)
                    if par == 0:
                        for name in ("att_ready", "xw_ready", "cd_ready", "sdec_ready"):
                            act.wait_ge(s[name], ONE + NU * G + max(u - 1, 0))
                        if u == 0:
                            act.wait_ge(s["sum2_ready"], ONE + G)
                    dst = grow[:, d, :, :] if par == 2 else decay[:, d, par, :, :]
                    nc.scalar.activation(dst, shaped(ps[:, 2 + e % 2, 0:HP * CH], HP, CH), ACT.Exp)\
                        .then_inc(s["exp_done"], 1)
                if nxt and hf == 1:
                    for t in (u - 1, u):
                        if t < XT_:
                            take_pre(act, b, i, G + 1, t, item("A", i, False, t)[0], nxt)
            if nxt:
                softplus_act(act, G + 1)
            B0 = item("B", i, not nxt, 0)[0]

            def z_copy(t, at0):
                act.wait_ge(s["pj_mm"], ONE + b * ALL + i * PER + at0 + 1)
                if t == 0:
                    act.wait_ge(s["y_read"], ONE + NU * G + NU)
                    act.wait_ge(s["st_mm"], ONE + NU * G + NU)
                nc.scalar.activation(xbc[:, t, :], ps[:, at0 % 2, :], ACT.Identity, bias=beta[:, t:t + 1])\
                    .then_inc(s[f"pj_read{at0 % 2}"], 1)

            for half in range(2):
                act.wait_ge(s["y_centred"], ONE + 2 * G + half + 1)
                if half == 0:
                    act.wait_ge(s["y_mm"], ONE + NU * G + NU)
                nc.scalar.activation(sq[:, HP * half:HP * half + HP, :], y_sb[:, HP * half:HP * half + HP, :],
                                     ACT.Square).then_inc(s["sq_ready"], 1)
                for t in (2 * half, 2 * half + 1):
                    z_copy(t, B0 + 1 + t)
            at0 = B0 + 5
            act.wait_ge(s["pj_mm"], ONE + b * ALL + i * PER + at0 + 1)
            nc.scalar.activation(row, ps[:, at0 % 2, :], ACT.Sqrt, bias=eps()).then_inc(s[f"pj_read{at0 % 2}"], 1)
            for t in range(4, NT):
                z_copy(t, B0 + 2 + t)
            for t in range(NT):
                act.wait_ge(s["y_scaled"], ONE + 2 * G + t // HP + 1)
                nc.scalar.activation(y_sb[:, t, :], y_sb[:, t, :], ACT.Identity, bias=vec[:, V_NB + t:V_NB + t + 1],
                                     scale=vec[:, V_NW + t:V_NW + t + 1]).then_inc(s["y_affine"], 1)

        def take_pre(act, b, i, G1, t, at0, rows):
            act.wait_ge(s["pj_mm"], ONE + b * ALL + i * PER + at0 + 1)
            act.wait_ge(s["carried"], ONE + G1 * XT_ + t + 1)
            nc.scalar.activation(pre[:, t, 2:2 + rows, 1:1 + W], shaped(ps[:, at0 % 2, 0:rows * W], rows, W),
                                 ACT.Identity, bias=beta[:, NT + t:NT + t + 1]).then_inc(s[f"pj_read{at0 % 2}"], 1)
            act.wait_ge(s[f"pj_read{at0 % 2}"], ONE + b * (ALL // 2) + i * (PER // 2) + at0 // 2 + 1)
            act.wait_ge(s["silu_done"], ONE + G1 * XT_)
            nc.scalar.activation(shaped(acc[:, t, :], ROWS, W), pre[:, t, 1:1 + ROWS, 1:1 + W], ACT.Identity,
                                 bias=vec[:, V_CB + t:V_CB + t + 1],
                                 scale=vec[:, V_CW + 9 * t + 4:V_CW + 9 * t + 5]).then_inc(s["centre_done"], 1)

        def softplus_act(act, G1):
            act.wait_ge(s["dt_mm"], ONE + G1 + 1)
            act.wait_ge(s["sp_prod"], ONE + G1)
            dtb = beta[0:R3, XT_ + NT:XT_ + NT + 1]
            nc.scalar.activation(sp_l[0:R3, :], ps[0:R3, 5, :], ACT.Abs, bias=dtb).then_inc(s["dt_abs"], 1)
            act.wait_ge(s["cs_stacked"], ONE + G1)
            nc.scalar.activation(cs[0:R3, :], ps[0:R3, 5, :], ACT.Relu, bias=dtb).then_inc(s["dt_relu"], 1)
            act.wait_ge(s["dt_abs"], ONE + G1 + 1)
            nc.scalar.activation(sp_e[0:R3, :], sp_l[0:R3, :], ACT.Exp, scale=-1.0).then_inc(s["sp_ln"], 1)
            act.wait_ge(s["sp_ln"], ONE + 2 * G1 + 1)
            nc.scalar.activation(sp_l[0:R3, :], sp_e[0:R3, :], ACT.Ln, bias=one[0:R3, 0:1]).then_inc(s["sp_ln"], 1)

        @block.scalar
        def _(act):
            begin(act)
            act.wait_ge(s["weights_loaded"], ONE + 16 * 7)
            nc.scalar.activation(a_neg[:, :], vec[0:R3, V_AL:V_AL + 1], ACT.Exp).then_inc(s["steps_a"], 1)
            act.wait_ge(s["steps_a"], ONE + 1)
            nc.scalar.activation(a_neg[:, :], a_neg[:, :], ACT.Copy, scale=-1.0).then_inc(s["prepared"], 1)
            nc.scalar.activation(bn1s[:], vec[0:PD, V_BN1 + 9:V_BN1 + 12], ACT.Sqrt, bias=eps(slice(0, PD)))\
                .then_inc(s["prepared"], 1)
            nc.scalar.activation(bn2s[:], vec[:, V_BN2 + 9:V_BN2 + 12], ACT.Sqrt, bias=eps()).then_inc(s["prepared"], 1)
            act.wait_ge(s["vec_prepared"], ONE + 1)
            with act.Fori(0, B) as b:
                gn_act(act, 2 * b)
                act.wait_ge(s["ab_ready"], ONE + 2 * b + 1)
                nc.scalar.activation(xn[:, 0, :], xs_[:, 0, :], ACT.Identity, bias=gn_ab[:, 0, 1:2],
                                     scale=gn_ab[:, 0, 0:1]).then_inc(s["xn0_ready"], 1)
                with act.Fori(0, NB // 2) as u:
                    G = act.snap(b * (NB // 2) + u)
                    for j in range(2):
                        act.wait_ge(s["centred"], ONE + 2 * G + j + 1)
                        act.wait_ge(s["scaled"], ONE + 2 * G)
                        nc.scalar.activation(ln_sq[0:PD, j, :], ln_x[0:PD, j, :], ACT.Square).then_inc(s["squared"], 1)
                    for j in range(2):
                        act.wait_ge(s["var_ready"], ONE + 2 * G + j + 1)
                        nc.scalar.activation(ln_sq[0:PD, j, :], ps[0:PD, 2 + j, :], ACT.Sqrt, bias=eps(slice(0, PD)))\
                            .then_inc(s["ln_root"], 1)
                    for j in range(2):
                        act.wait_ge(s["scaled"], ONE + 2 * G + j + 1)
                        act.wait_ge(s["v_ready"], ONE + 2 * G)
                        nc.scalar.activation(ln_y[0:PD, j, :], ln_x[0:PD, j, :], ACT.Identity,
                                             bias=vec[0:PD, V_LN + 1:V_LN + 2], scale=vec[0:PD, V_LN:V_LN + 1])\
                            .then_inc(s["ln_ready"], 1)
                    for j in range(2):
                        act.wait_ge(s["v_ready"], ONE + 2 * G + j + 1)
                        act.wait_ge(s["q_stacked"], ONE + 2 * G)
                        act.wait_ge(s["k_stacked"], ONE + 2 * G)
                        act.wait_ge(s["vt_ready"], ONE + 2 * G)
                        nc.scalar.activation(v_sb[0:PD, j, :], ps[0:PD, j, :], ACT.Identity, bias=bn1o[:, 2:3],
                                             scale=bn1s[:, 2:3]).then_inc(s["v_taken"], 1)
                        for w in range(2):
                            bank = ps[0:PD, 4 + 2 * w + j, :]
                            nc.scalar.activation(qk_f[0:PD, w, j, :], bank, ACT.Identity, bias=bn1o[:, w:w + 1],
                                                 scale=bn1s[:, w:w + 1])
                            nc.scalar.activation(qk_h[0:PD, w, j, :], bank, ACT.Identity, bias=bn1o[:, w:w + 1],
                                                 scale=bn1s[:, w:w + 1]).then_inc(s["qk_taken"], 1)
                meet(act, b, 0)

                def take_max(g):
                    act.wait_ge(s["nm_turned"], ONE + g + 1)
                    nc.scalar.copy(nm_f[96:99, :], ps[96:99, 7, :])
                    nc.scalar.copy(nm_h[96:99, :], ps[96:99, 7, :]).then_inc(s["nm_taken"], 1)

                def attend_act(qb, has_next):
                    g = act.snap(b * NB + qb) if not isinstance(qb, int) else b * NB + qb
                    blk = bass.ds(qb * TB, TB)
                    act.wait_ge(s["proj_mm"], ONE + CT * g)
                    act.wait_ge(s["xn1_ready"], ONE + b + 1)
                    act.wait_ge(s["xn2_ready"], ONE + b + 1)
                    nc.scalar.activation(cat[PD:P, 0, :], xn[PD:P, 0, blk], ACT.Relu).then_inc(s["skip_relu"], 1)
                    nc.scalar.activation(cat[:, 1:CT, :], xn[:, 1:CT, blk], ACT.Relu).then_inc(s["skip_relu"], 1)
                    for st in range(16):
                        act.wait_ge(s["scores"], ONE + 16 * g + st + 1)
                        act.wait_ge(s["pv_done"], ONE + 16 * g + max(st - 1, 0))
                        nc.scalar.activation(p_sb[:, st % 2, :, :], ps[:, 2 * (st % 2):2 * (st % 2) + 2, :], ACT.Exp,
                                             scale=QK ** -0.5).then_inc(s["exps"], 1)
                        if has_next and st == TURN_AT:
                            take_max(g + 1)
                    act.wait_ge(s["recip_spread"], ONE + g + 1)
                    nc.scalar.copy(rec_b[0:PD, :], ps[0:PD, 7, :]).then_inc(s["recip_copied"], 1)
                    for m in range(CT):
                        act.wait_ge(s["proj_mm"], ONE + CT * g + m + 1)
                        act.wait_ge(s["x1_added"], ONE + CT * g)
                        nc.scalar.activation(proj_y[:, m, :], ps[:, 7, :], ACT.Identity, bias=bn2o[:, m:m + 1],
                                             scale=bn2s[:, m:m + 1]).then_inc(s["proj_taken"], 1)

                take_max(b * NB)
                with act.Fori(0, NB - 1) as qb:
                    attend_act(qb, True)
                attend_act(NB - 1, False)
                meet(act, b, 1)
                gn_act(act, 2 * b + 1)
                meet(act, b, 2)
                act.wait_ge(s["row0_mm"], ONE + b + 1)
                act.wait_ge(s["top_clear"], ONE + 2 * b + 2)
                for t in range(XT_):
                    ins = nc.scalar.activation(pre[:, t, 9, 1:1 + W], ps[:, 4, t * W:(t + 1) * W], ACT.Identity,
                                               bias=beta[:, NT + t:NT + t + 1])
                ins.then_inc(s["row0_done"], 1)
                softplus_act(act, b * NB)
                for t in range(XT_):
                    take_pre(act, b, -1, b * NB, t, PER + t, ROWS)
                with act.Fori(0, NB - 2) as i:
                    block_act(act, b, i, ROWS, None)
                block_act(act, b, NB - 2, ROWS - 1, None)
                block_act(act, b, NB - 1, 0, None)
                meet(act, b, 3)

        def dt_pool(pool, G1, step):
            r = slice(0, R3)
            pool.wait_ge(s["sp_ln"], ONE + 2 * G1 + 1)
            pool.wait_ge(s["dt_ready"], ONE + G1)
            own(pool)
            step(nc.gpsimd.tensor_scalar(sp_d[r, :], sp_e[r, :], 1.0, -1.0, ALU.add, ALU.add))
            step.join()
            own(pool)
            step(nc.gpsimd.tensor_scalar(sp_r[r, :], sp_d[r, :], 0.0, None, ALU.is_equal))
            step.join()
            step(nc.gpsimd.tensor_tensor(sp_d[r, :], sp_d[r, :], sp_r[r, :], ALU.add))
            pool.wait_ge(s["sp_ln"], ONE + 2 * G1 + 2)
            step(nc.gpsimd.tensor_tensor(sp_r[r, :], sp_l[r, :], sp_r[r, :], ALU.add))
            step.join()
            nc.gpsimd.tensor_tensor(sp_l[r, :], sp_r[r, :], sp_e[r, :], ALU.mult).then_inc(s["sp_prod"], 1)

        def diag_pool(pool, G1):
            pool.wait_ge(s["cs_stacked"], ONE + G1 + 1)
            own(pool)
            for c in range(NC):
                tok = slice(c * CH, (c + 1) * CH)
                for par in range(2):
                    nc.gpsimd.tensor_scalar(cs_neg[0:R3, par, tok], cs_st[0:R3, tok], mask(6 + par, slice(0, R3)),
                                            None, ALU.mult)
                nc.gpsimd.tensor_tensor(cs_diag[0:R3, :, tok],
                                        cs_st[0:R3, tok].unsqueeze(1).broadcast_to([R3, NT, CH]),
                                        shaped(kb[0:R3, B_DELTA:B_DELTA + NT * CH], NT, CH), ALU.mult)\
                    .then_inc(s["diag_ready"], 1)

        def carry_pool(pool, G1, t):
            pool.wait_ge(s["conv_done"], ONE + G1 * XT_)
            own(pool)
            nc.gpsimd.tensor_copy(pre[:, t, 0:2, :], pre[:, t, ROWS:ROWS + 2, :]).then_inc(s["carried"], 1)

        def block_pool(pool, b, i, nxt, step):
            G = b * NB + i if isinstance(i, int) else pool.snap(b * NB + i)
            if nxt:
                for t in range(XT_):
                    carry_pool(pool, G + 1, t)
            if nxt == ROWS - 1:
                pool.wait_ge(s["carried"], ONE + (G + 2) * XT_)
                own(pool)
                nc.gpsimd.memset(pre[:, :, ROWS + 1, :], 0.0).then_inc(s["bottom_clear"], 1)
            for u in range(NU):
                c, hf, d = u // 2, u % 2, u % 2
                tok = slice(c * CH, (c + 1) * CH)
                pool.wait_ge(s["exp_done"], ONE + 3 * NU * G + 3 * u + 3)
                if u == 0:
                    pool.wait_ge(s["bc_dup"], ONE + 32 * G + 32)
                pool.wait_ge(s["y_mm"], ONE + NU * G + max(u - 1, 0))
                nc.gpsimd.tensor_tensor(c_dec[:, d, :, :], grow[:, d, :, :],
                                        c_dup[:, tok].unsqueeze(1).broadcast_to([P, HP, CH]), ALU.mult)\
                    .then_inc(s["cd_ready"], 1)
                pool.wait_ge(s["st_mm"], ONE + NU * G + max(u - 1, 0))
                pool.wait_ge(s["xdt_ready"], ONE + NU * G + u + 1)
                last = decay[:, d, :, :, CH - 1].rearrange("p a t -> p t a")
                nc.gpsimd.tensor_tensor(x_w[:, d, :, :, :], x_dt[:, d, :, :, :],
                                        last.unsqueeze(3).broadcast_to([P, HP, 2, HD]), ALU.mult)\
                    .then_inc(s["xw_ready"], 1)
                pool.wait_ge(s["state_done"], ONE + NU * G + u)
                if u < 2:
                    pool.wait_ge(s["state_clear"], ONE + b + 1)
                nc.gpsimd.tensor_tensor(st_dec, state[:, HP * hf:HP * hf + HP, :],
                                        grow[:, d, :, CH - 1:CH].broadcast_to([P, HP, P]), ALU.mult)\
                    .then_inc(s["sdec_ready"], 1)
            pool.wait_ge(s["st_mm"], ONE + NU * G + NU)
            pool.wait_ge(s["y_read"], ONE + NU * G + NU)
            step(nc.gpsimd.tensor_tensor(sum3[:, :, :], y_sb[:, 0:HP, :], y_sb[:, HP:NT, :], ALU.add))
            step.join()
            step(nc.gpsimd.tensor_tensor(row, sum3[:, 0, :], sum3[:, 1, :], ALU.add))
            step.join()
            nc.gpsimd.tensor_tensor(row, row, sum3[:, 2, :], ALU.add).then_inc(s["sum1_ready"], 1)
            if nxt:
                dt_pool(pool, G + 1, step)
            pool.wait_ge(s["sq_ready"], ONE + 2 * G + 2)
            pool.wait_ge(s["sum1_ready"], ONE + G + 1)
            step(nc.gpsimd.tensor_tensor(sum3[:, :, :], sq[:, 0:HP, :], sq[:, HP:NT, :], ALU.add))
            step.join()
            step(nc.gpsimd.tensor_tensor(row, sum3[:, 0, :], sum3[:, 1, :], ALU.add))
            step.join()
            step(nc.gpsimd.tensor_tensor(row, row, sum3[:, 2, :], ALU.add))
            step.join()
            pool.sem_inc(s["sum2_ready"], 1)
            if nxt:
                pool.wait_ge(s["e_mm"], ONE + 3 * NU * G + 3 * NU)
                diag_pool(pool, G + 1)

        POOL_BLK, POOL_END, POOL_PRO = 9, 5, 4
        POOL_ALL = POOL_PRO + POOL_BLK * (NB - 1) + POOL_END

        @block.gpsimd
        def _(pool):
            step = Steps(pool, s["steps_p"])
            begin(pool)
            pool.wait_ge(s["weights_loaded"], ONE + 16 * 7)
            with pool.Fori(0, B) as b:
                nc.gpsimd.memset(v_t[:, :, 96:97], 1.0)
                pool.wait_ge(s["ab_ready"], ONE + 2 * b + 1)
                own(pool)
                nc.gpsimd.tensor_scalar(xn[:, 2, :], xs_[:, 2, :], gn_ab[:, 2, 0:1], gn_ab[:, 2, 1:2], ALU.mult,
                                        ALU.add).then_inc(s["xn2_ready"], 1)
                meet(pool, b, 0)
                with pool.Fori(0, NB) as qb:
                    g = pool.snap(b * NB + qb)
                    for m in range(CT):
                        pool.wait_ge(s["proj_taken"], ONE + CT * g + m + 1)
                        xb = xs_[:, m, bass.ds(qb * TB, TB)]
                        nc.gpsimd.tensor_tensor(xb, xb, proj_y[:, m, :], ALU.add).then_inc(s["x1_added"], 1)
                meet(pool, b, 1)
                nc.gpsimd.memset(pre[:, :, :, :], 0.0).then_inc(s["top_clear"], 1)
                nc.gpsimd.memset(state[:, :, :], 0.0).then_inc(s["state_clear"], 1)
                pool.wait_ge(s["top_clear"], ONE + 2 * b + 1)
                pool.sem_inc(s["top_clear"], 1)
                meet(pool, b, 2)
                step.enter(b * POOL_ALL)
                pool.wait_ge(s["row0_done"], ONE + b + 1)
                for t in range(XT_):
                    carry_pool(pool, b * NB, t)
                dt_pool(pool, b * NB, step)
                assert step.n == POOL_PRO, step.n
                diag_pool(pool, b * NB)
                with pool.Fori(0, NB - 2) as i:
                    step.enter(pool.snap(b * POOL_ALL + i * POOL_BLK + POOL_PRO))
                    block_pool(pool, b, i, ROWS, step)
                    assert step.n == POOL_BLK, step.n
                step.enter(b * POOL_ALL + (NB - 2) * POOL_BLK + POOL_PRO)
                block_pool(pool, b, NB - 2, ROWS - 1, step)
                step.enter(b * POOL_ALL + (NB - 1) * POOL_BLK + POOL_PRO)
                block_pool(pool, b, NB - 1, 0, step)
                assert step.n == POOL_END, step.n
                meet(pool, b, 3)

        V = nc.vector

        def gn_dve(dve, n, step):
            own(dve)
            for t in range(CT):
                step(V.bn_aggr(chan_mv[:, t, :], chan_stats[:, t, :, :]))
            step.join()
            for t in range(CT):
                ins = V.scalar_tensor_tensor(chan_mv[:, t, 1:2], chan_mv[:, t, 0:1], chan_mv[:, t, 0:1],
                                             chan_mv[:, t, 1:2], ALU.mult, ALU.add)
            ins.then_inc(s["stats_ready"], 1)
            dve.wait_ge(s["group_sums"], ONE + n + 1)
            step(V.tensor_copy(group_mv[:], ps[0:GROUPS, 7, 0:2]))
            step.join()
            step(V.tensor_scalar(group_sc[:, 0:1], group_mv[:, 0:1], group_mv[:, 0:1], None, ALU.mult))
            step.join()
            V.tensor_tensor(group_sc[:, 1:2], group_mv[:, 1:2], group_sc[:, 0:1], ALU.subtract)\
                .then_inc(s["vars_ready"], 1)
            dve.wait_ge(s["roots_ready"], ONE + n + 1)
            step(V.reciprocal(group_sc[:, 2:3], group_sc[:, 1:2]))
            step.join()
            V.scalar_tensor_tensor(group_sc[:, 3:4], group_mv[:, 0:1], -1.0, group_sc[:, 2:3], ALU.mult, ALU.mult)\
                .then_inc(s["groups_ready"], 1)
            dve.wait_ge(s["group_back"], ONE + n + 1)
            V.tensor_copy(gn_ab[:], shaped(ps[:, 7, 8:8 + 2 * CT], CT, 2)).then_inc(s["ab_ready"], 1)
        GN_STEPS = CT + 3

        def max_dve(dve, g, n):
            dve.wait_ge(s["max_scores"], ONE + 32 * g + n + 1)
            V.tensor_reduce(maxes[:, n // NB, n % NB:n % NB + 1], ps[:, 4 + n % 2, :], AX.X, ALU.max)\
                .then_inc(s["max_read"], 1)

        def negmax_dve(dve, g, step):
            dve.wait_ge(s["max_read"], ONE + 32 * g + 32)
            step(V.tensor_reduce(max4[:], maxes[:], AX.X, ALU.max))
            step.join()
            dve.wait_ge(s["nm_turned"], ONE + g)
            V.tensor_scalar(negmax[:, :, QR:KS], max4[:].unsqueeze(2).broadcast_to([P, 4, 3]), -1.0, None, ALU.mult)\
                .then_inc(s["nm_ready"], 1)

        def split_max(dve, g, nq, step):
            r = slice(96, 99)
            dve.wait_ge(s["nm_taken"], ONE + g + 1)
            step(V.scalar_tensor_tensor(nm_f[r, :], nm_h[r, :], mask(0, r), nm_f[r, :], ALU.mult, ALU.add))
            step.join()
            step(V.tensor_copy(nm_m[r, :], nm_f[r, :]))
            step.join()
            V.scalar_tensor_tensor(q_st[r, bass.ds(nq * TB, TB)], nm_m[r, :], mask(1, r), nm_f[r, :], ALU.mult,
                                   ALU.add).then_inc(s["nm_stacked"], 1)

        def attend_dve(dve, b, qb, has_next, step):
            g = b * NB + qb if isinstance(qb, int) else dve.snap(b * NB + qb)
            if has_next:
                for n in range(32):
                    max_dve(dve, g + 1, n)
                negmax_dve(dve, g + 1, step)
                split_max(dve, g + 1, qb + 1, step)
            dve.wait_ge(s["pv_done"], ONE + 16 * g + 16)
            V.reciprocal(rec[96:97, :], ps[96:97, 6, :]).then_inc(s["recip_ready"], 1)
            dve.wait_ge(s["recip_copied"], ONE + g + 1)
            V.scalar_tensor_tensor(cat[0:PD, 0, :], ps[0:PD, 6, :], 0.0, rec_b[0:PD, :], ALU.max, ALU.mult)\
                .then_inc(s["normed"], 1)
            for m in range(CT):
                dve.wait_ge(s["x1_added"], ONE + CT * g + m + 1)
                step(V.bn_stats(chan_stats[:, m, qb, :] if isinstance(qb, int) else
                                chan_stats[:, m, bass.ds(qb, 1), :], xs_[:, m, bass.ds(qb * TB, TB)]))

        TAPS = [0, 1, 2, 3, 5, 6, 7, 8]

        def conv_dve(dve, G1, tiles, step):
            for k, tap in enumerate(TAPS):
                for t in tiles:
                    if k == 0:
                        dve.wait_ge(s["centre_done"], ONE + XT_ * G1 + t + 1)
                    else:
                        step.join(len(tiles) - 1)
                    dy, dx = tap // 3, tap % 3
                    a = shaped(acc[:, t, :], ROWS, W)
                    step(V.scalar_tensor_tensor(a, pre[:, t, dy:dy + ROWS, dx:dx + W],
                                                vec[:, V_CW + 9 * t + tap:V_CW + 9 * t + tap + 1], a, ALU.mult,
                                                ALU.add))
            step.join()
            dve.sem_inc(s["conv_done"], len(tiles))

        def dt_dve(dve, G1, step):
            r = slice(0, R3)
            dve.wait_ge(s["sp_prod"], ONE + G1 + 1)
            step(V.reciprocal(sp_r[r, :], sp_d[r, :]))
            step.join()
            step(V.tensor_tensor(sp_d[r, :], sp_l[r, :], sp_r[r, :], ALU.mult))
            step.join()
            dve.wait_ge(s["small_mm"], ONE + NC * G1)
            dve.wait_ge(s["dt_relu"], ONE + G1 + 1)
            V.tensor_tensor(dt_sb[r, :], sp_d[r, :], cs[r, :], ALU.add).then_inc(s["dt_ready"], 1)
            dve.wait_ge(s["dt_ready"], ONE + G1 + 1)
            step(V.tensor_scalar(sp_r[r, :], dt_sb[r, :], a_neg[r, :], None, ALU.mult))
            step.join()
            for c in range(NC):
                tok = slice(c * CH, (c + 1) * CH)
                step(V.tensor_tensor_scan(cs[r, tok], one[r, 0:CH], sp_r[r, tok], 0.0, ALU.mult, ALU.add))
            step.join()
            step(V.tensor_copy(cs_h[r, :], cs[r, :]))
            step.join()
            step(V.scalar_tensor_tensor(cs[r, :], cs_h[r, :], mask(4, r), cs[r, :], ALU.mult, ALU.add))
            step.join()
            step(V.tensor_copy(cs_h[r, :], cs[r, :]))
            step.join()
            dve.wait_ge(s["diag_ready"], ONE + NC * G1)
            V.scalar_tensor_tensor(cs_st[r, :], cs_h[r, :], mask(5, r), cs[r, :], ALU.mult, ALU.add)\
                .then_inc(s["cs_stacked"], 1)
        DT_STEPS = 10

        def unit_a_dve(dve, G, u):
            c, hf, d = u // 2, u % 2, u % 2
            dve.wait_ge(s["xt_mm"], ONE + NU * G + u + 1)
            dve.wait_ge(s["small_copied"], ONE + NC * G + c + 1)
            for name in ("y_mm", "xw_ready"):
                dve.wait_ge(s[name], ONE + NU * G + max(u - 1, 0))
            if u == 0:
                dve.wait_ge(s["sum2_ready"], ONE + G)
            heads = slice(P + NS + 2 * HP * hf, P + NS + 2 * HP * (hf + 1))
            V.tensor_tensor(x_dt[:, d, :, :, :].rearrange("p a b c -> p (a b) c"),
                            shaped(ps[:, 4, 0:HP * P], 2 * HP, HD),
                            small[:, c % 2, heads].unsqueeze(2).broadcast_to([P, 2 * HP, HD]), ALU.mult)\
                .then_inc(s["xdt_ready"], 1)
            dve.wait_ge(s["exp_done"], ONE + 3 * NU * G + 3 * u + 2)
            V.tensor_tensor(att[:, d, :, :, :].rearrange("p a b c -> p (a b) c"),
                            decay[:, d, :, :, :].rearrange("p a b c -> p (a b) c"),
                            small[:, c % 2, 0:P].unsqueeze(1).broadcast_to([P, 2 * HP, CH]), ALU.mult)\
                .then_inc(s["att_ready"], 1)

        def unit_b_dve(dve, G, u):
            c, hf, d = u // 2, u % 2, u % 2
            tok = slice(c * CH, (c + 1) * CH)
            dve.wait_ge(s["y_mm"], ONE + NU * G + u + 1)
            for t in range(HP):
                T = HP * hf + t
                ins = V.scalar_tensor_tensor(y_sb[:, T, tok], xbc[:, T, tok], vec[:, V_D + T:V_D + T + 1],
                                             ps[:, 6, t * CH:(t + 1) * CH], ALU.mult, ALU.add)
            ins.then_inc(s["y_read"], 1)
            dve.wait_ge(s["st_mm"], ONE + NU * G + u + 1)
            dve.wait_ge(s["sdec_ready"], ONE + NU * G + u + 1)
            for par in range(2):
                rr = slice(64 * par, 64 * par + 64)
                ins = V.tensor_tensor(state[rr, HP * hf:HP * hf + HP, rr], shaped(ps[rr, 7, 0:HP * HD], HP, HD),
                                      st_dec[rr, :, rr], ALU.add)
            ins.then_inc(s["state_done"], 1)

        def block_dve(dve, b, i, nxt, step):
            G = b * NB + i if isinstance(i, int) else dve.snap(b * NB + i)
            dve.wait_ge(s["pj_mm"], ONE + b * ALL + i * PER)
            if nxt == ROWS - 1:
                dve.wait_ge(s["bottom_clear"], ONE + b + 1)
            for u in range(NU):
                unit_a_dve(dve, G, u)
                if u:
                    unit_b_dve(dve, G, u - 1)
                if nxt and u in (3, 5):
                    conv_dve(dve, G + 1, (u - 3, u - 2), step)
            unit_b_dve(dve, G, NU - 1)
            B0 = item("B", i, not nxt, 0)[0]
            pj = b * ALL + i * PER
            dve.wait_ge(s["pj_mm"], ONE + pj + B0 + 1)
            for half in range(2):
                h3 = slice(HP * half, HP * half + HP)
                V.tensor_tensor(y_sb[:, h3, :], y_sb[:, h3, :],
                                ps[:, B0 % 2:B0 % 2 + 1, :].broadcast_to([P, HP, TB]), ALU.subtract)\
                    .then_inc(s["y_centred"], 1)
            dve.wait_ge(s["y_centred"], ONE + 2 * G + 2)
            dve.sem_inc(s[f"pj_read{B0 % 2}"], 1)
            if nxt:
                dt_dve(dve, G + 1, step)
                conv_dve(dve, G + 1, (4, 5), step)
            at0 = B0 + 5
            dve.wait_ge(s[f"pj_read{at0 % 2}"], ONE + b * (ALL // 2) + i * (PER // 2) + at0 // 2 + 1)
            V.reciprocal(row, row).then_inc(s["row_root"], 1)
            dve.wait_ge(s["row_root"], ONE + G + 1)
            dve.wait_ge(s["sq_ready"], ONE + 2 * G + 2)
            for half in range(2):
                h3 = slice(HP * half, HP * half + HP)
                V.tensor_tensor(y_sb[:, h3, :], y_sb[:, h3, :], row.unsqueeze(1).broadcast_to([P, HP, TB]),
                                ALU.mult).then_inc(s["y_scaled"], 1)
            if nxt:
                conv_dve(dve, G + 1, (6,), step)
            for t in range(NT):
                dve.wait_ge(s["y_affine"], ONE + NT * G + t + 1)
                z_at = B0 + 1 + t if t < 4 else B0 + 2 + t
                dve.wait_ge(s[f"pj_read{z_at % 2}"], ONE + b * (ALL // 2) + i * (PER // 2) + z_at // 2 + 1)
                V.tensor_tensor(y_sb[:, t, :], y_sb[:, t, :], xbc[:, t, :], ALU.mult).then_inc(s["gated"], 1)
            for m in range(CT):
                at0 = B0 + 2 + NT + m
                dve.wait_ge(s["pj_mm"], ONE + pj + at0 + 1)
                xb = xs_[:, m, bass.ds(i * TB, TB)]
                V.tensor_tensor(xb, ps[:, at0 % 2, :], xb, ALU.add).then_inc(s["out_read"], 1)
                dve.wait_ge(s["out_read"], ONE + CT * G + m + 1)
                dve.sem_inc(s[f"pj_read{at0 % 2}"], 1)

        QKV_STEPS = 6
        ATT_STEPS, ATT_LAST = 6, 3
        BLK_STEPS = 8 * XT_ + DT_STEPS
        V_GN0 = 24 + GN_STEPS
        V_QKV = V_GN0 + QKV_STEPS * (NB // 2)
        V_MAX0 = V_QKV + 3
        V_ATT = V_MAX0 + ATT_STEPS * (NB - 1) + ATT_LAST
        V_GN1 = V_ATT + GN_STEPS
        V_SSD = V_GN1 + BLK_STEPS
        V_ALL = V_SSD + BLK_STEPS * (NB - 1)

        @block.vector
        def _(dve):
            step = Steps(dve, s["steps_v"])
            begin(dve)
            dve.wait_ge(s["weights_loaded"], ONE + 16 * 7)
            dve.wait_ge(s["prepared"], ONE + 3)
            b1 = shaped(vec[0:PD, V_BN1:V_BN1 + 12], 4, 3)
            b2 = shaped(vec[:, V_BN2:V_BN2 + 12], 4, 3)
            for v, sc, of in ((b1, bn1s, bn1o), (b2, bn2s, bn2o)):
                step(V.reciprocal(of[:], sc[:]))
                step.join()
                step(V.tensor_tensor(sc[:], v[:, 0, :], of[:], ALU.mult))
                step.join()
                step(V.tensor_tensor(of[:], v[:, 2, :], sc[:], ALU.mult))
                step.join()
                step(V.tensor_tensor(of[:], v[:, 1, :], of[:], ALU.subtract))
                step.join()
            V_PRE = step.n
            V.memset(rec[96:97, 0:1], 0.0).then_inc(s["vec_prepared"], 1)
            with dve.Fori(0, B) as b:
                base = dve.snap(b * V_ALL + V_PRE)
                step.enter(base)
                V.memset(k_st[96:99, :], 1.0)
                for t in range(CT):
                    dve.wait_ge(s[f"x_loaded{t}"], ONE + 16 * b + 16)
                    for k in range(NB):
                        step(V.bn_stats(chan_stats[:, t, k, :], xs_[:, t, k * TB:(k + 1) * TB]))
                step.join()
                gn_dve(dve, 2 * b, step)
                assert step.n == V_GN0
                dve.wait_ge(s["ab_ready"], ONE + 2 * b + 1)
                V.tensor_scalar(xn[:, 1, :], xs_[:, 1, :], gn_ab[:, 1, 0:1], gn_ab[:, 1, 1:2], ALU.mult, ALU.add)\
                    .then_inc(s["xn1_ready"], 1)
                with dve.Fori(0, NB // 2) as u:
                    step.enter(dve.snap(b * V_ALL + u * QKV_STEPS + (V_PRE + V_GN0)))
                    G = dve.snap(b * (NB // 2) + u)
                    dve.wait_ge(s["xn0_ready"], ONE + b + 1)
                    for j in range(2):
                        dve.wait_ge(s["mean_ready"], ONE + 2 * G + j + 1)
                        dve.wait_ge(s["ln_ready"], ONE + 2 * G)
                        V.tensor_tensor(ln_x[0:PD, j, :], xn[0:PD, 0, bass.ds(u * (2 * TB) + j * TB, TB)],
                                        ps[0:PD, j, :], ALU.subtract).then_inc(s["centred"], 1)
                    for j in range(2):
                        dve.wait_ge(s["ln_root"], ONE + 2 * G + j + 1)
                        dve.wait_ge(s["centred"], ONE + 2 * G + j + 1)
                        step(V.reciprocal(ln_sq[0:PD, j, :], ln_sq[0:PD, j, :]))
                        step.join()
                        V.tensor_tensor(ln_x[0:PD, j, :], ln_x[0:PD, j, :], ln_sq[0:PD, j, :], ALU.mult)\
                            .then_inc(s["scaled"], 1)
                    for w, name in ((0, "q_stacked"), (1, "k_stacked")):
                        st = (q_st, k_st)[w]
                        dve.wait_ge(s["qk_taken"], ONE + 4 * G + 4)
                        f, h, m = (v[0:PD, w, :, :] for v in (qk_f, qk_h, qk_m))
                        step(V.scalar_tensor_tensor(f, h, mask(2 * w, slice(0, PD)), f, ALU.mult, ALU.add))
                        step.join()
                        step(V.tensor_copy(m, f))
                        step.join()
                        V.scalar_tensor_tensor(st[0:PD, bass.ds(u * (2 * TB), 2 * TB)],
                                               m.rearrange("p a b -> p (a b)"), mask(2 * w + 1, slice(0, PD)),
                                               f.rearrange("p a b -> p (a b)"), ALU.mult, ALU.add)\
                            .then_inc(s[name], 2)
                    for j in range(2):
                        dve.wait_ge(s["vt_ready"], ONE + 2 * G + j + 1)
                        V.tensor_copy(v_t[:, bass.ds(u * 8 + j * 4, 4), 0:PD], shaped(ps[:, 2 + j, 0:4 * PD], 4, PD))\
                            .then_inc(s["vt_copied"], 1)
                    assert step.n == QKV_STEPS, step.n
                meet(dve, b, 0)
                step.enter(dve.snap(b * V_ALL + (V_PRE + V_QKV)))
                for n in range(32):
                    max_dve(dve, b * NB, n)
                V.memset(negmax[:], 0.0).then_inc(s["cleared"], 1)
                dve.wait_ge(s["cleared"], ONE + b + 1)
                negmax_dve(dve, b * NB, step)
                split_max(dve, b * NB, 0, step)
                assert step.n == 3
                with dve.Fori(0, NB - 1) as qb:
                    step.enter(dve.snap(b * V_ALL + qb * ATT_STEPS + (V_PRE + V_MAX0)))
                    attend_dve(dve, b, qb, True, step)
                    assert step.n == ATT_STEPS
                step.enter(dve.snap(b * V_ALL + (V_PRE + V_MAX0 + ATT_STEPS * (NB - 1))))
                attend_dve(dve, b, NB - 1, False, step)
                step.join()
                meet(dve, b, 1)
                step.enter(dve.snap(b * V_ALL + (V_PRE + V_ATT)))
                gn_dve(dve, 2 * b + 1, step)
                dve.wait_ge(s["beta_mm"], ONE + b + 1)
                dve.wait_ge(s["ab_ready"], ONE + 2 * b + 2)
                V.tensor_copy(beta[:, 0:XT_ + NT], ps[:, 6, 0:XT_ + NT])
                V.tensor_tensor(beta[0:R3, XT_ + NT:XT_ + NT + 1], ps[0:R3, 6, XT_ + NT:XT_ + NT + 1],
                                vec[0:R3, V_DTB:V_DTB + 1], ALU.add)
                for k in range(CT):
                    V.tensor_scalar(w_in[:, k, :], w_in[:, k, :], gn_ab[:, k, 0:1], None, ALU.mult)
                    V.tensor_scalar(w_dt[:, k, :], w_dt_raw[:, k, :], gn_ab[:, k, 0:1], None, ALU.mult)
                meet(dve, b, 2)
                step.enter(dve.snap(b * V_ALL + (V_PRE + V_GN1)))
                dt_dve(dve, b * NB, step)
                for tiles in ((0, 1), (2, 3), (4, 5), (6,)):
                    for t in tiles:
                        dve.wait_ge(s[f"pj_read{(PER + t) % 2}"], ONE + b * (ALL // 2) + t // 2 + 1)
                    conv_dve(dve, b * NB, tiles, step)
                assert step.n == BLK_STEPS, step.n
                with dve.Fori(0, NB - 2) as i:
                    step.enter(dve.snap(b * V_ALL + i * BLK_STEPS + (V_PRE + V_SSD)))
                    block_dve(dve, b, i, ROWS, step)
                    assert step.n == BLK_STEPS, step.n
                step.enter(dve.snap(b * V_ALL + (V_PRE + V_SSD + (NB - 2) * BLK_STEPS)))
                block_dve(dve, b, NB - 2, ROWS - 1, step)
                step.enter(dve.snap(b * V_ALL + (V_PRE + V_SSD + (NB - 1) * BLK_STEPS)))
                block_dve(dve, b, NB - 1, 0, step)
                meet(dve, b, 3)


def lay_out(i):
    f = {k: np.asarray(v) for k, v in i.items()}
    x = np.ascontiguousarray(f["x"].reshape(B, C, L))
    g = lambda n: f["L0_conv_" + n]
    m = lambda n: f["L1_conv_" + n]
    qkv = g("w_qkv")
    wq, wk, wv = qkv[:QK], qkv[QK:2 * QK], qkv[2 * QK:]
    rep = lambda a: np.concatenate([a] * QG, 0)
    wqkv = np.stack([rep(wq).T, rep(wk).T, wv.T], 1)
    vecs = np.zeros((P, NV), np.float32)
    for n, name in enumerate(("bn1_g", "bn1_b", "bn1_m", "bn1_v")):
        v = g(name)
        for k, part in enumerate((rep(v[:QK]), rep(v[QK:2 * QK]), v[2 * QK:])):
            vecs[:PD, V_BN1 + 3 * n + k] = part
    vecs[:PD, V_LN], vecs[:PD, V_LN + 1] = g("ln_w"), g("ln_b")
    tiles = lambda v: v.reshape(-1, P).T
    for n, name in enumerate(("bn2_g", "bn2_b", "bn2_m", "bn2_v")):
        vecs[:, V_BN2 + 3 * n:V_BN2 + 3 * n + 3] = tiles(g(name))
    cw = m("conv_w").reshape(XT_, P, 9)
    vecs[:, V_CW:V_CW + 63] = cw.transpose(1, 0, 2).reshape(P, 63)
    vecs[:, V_CB:V_CB + XT_] = tiles(m("conv_b"))
    vecs[:, V_NW:V_NW + NT], vecs[:, V_NB:V_NB + NT] = tiles(m("norm_w")), tiles(m("norm_b"))
    vecs[:, V_D:V_D + NT] = tiles(np.repeat(m("D"), HD))
    w = m("in_proj_w")
    wdt = np.zeros((R3, C), np.float32)
    for part in range(3):
        r = slice(32 * part, 32 * part + NH)
        vecs[r, V_DTB], vecs[r, V_AL] = m("dt_bias"), m("A_log")
        wdt[r] = w[DIN:]
    kmajor = lambda a: np.ascontiguousarray(a.T.reshape(-1, P, a.shape[0]).transpose(1, 0, 2))
    consts, constb = constants()
    return {"x": x, "vecs": vecs, "wqkv": np.ascontiguousarray(wqkv), "wproj": kmajor(g("w_proj")),
            "win": kmajor(w[:DIN]), "wdt": kmajor(wdt), "wout": kmajor(m("out_proj_w")),
            "consts": consts, "constb": constb}


def kernel(**inputs):
    import concourse.bacc as bacc
    from concourse.bass_utils import run_bass_kernel_spmd

    nc = bacc.Bacc("TRN2", target_bir_lowering=False, num_devices=1)
    arrays = lay_out(inputs)
    args = [nc.dram_tensor(n, a.shape, mybir.dt.from_np(a.dtype), kind="ExternalInput").ap()
            for n, a in arrays.items()]
    args.append(nc.dram_tensor("out", (B, C, L), F32, kind="ExternalOutput").ap())
    program(nc, *args)
    r = run_bass_kernel_spmd(nc, [arrays], core_ids=[0])
    return r.results[0]["out"].reshape(B, C, H, W)
```

```python
from contextlib import ExitStack

import concourse.bass as bass
import concourse.mybir as mybir
import numpy as np

F32 = mybir.dt.float32
BF16 = mybir.dt.bfloat16
ALU = mybir.AluOpType
ACT = mybir.ActivationFunctionType
AX = mybir.AxisListType

B, C, H, W = 4, 384, 64, 64
L = H * W
P = 128
CT = C // P
TB = 512
NB = L // TB
ROWS = TB // W
WP = W + 2
GROUPS = 32
PD, QK = 96, 16
DI = 768
NT = DI // P
NS = 64
HD = 64
NH = DI // HD
XT_ = (DI + 2 * NS) // P
DIN = 2 * DI + 2 * NS
CH = 128
NC = TB // CH
HP = NT // 2
NU = 2 * NC
R3 = 64 + NH
QG = 6
QR = QG * QK
KS = QR + 3
QPART = (0, 0, 1, 1, 0, 2)
KPART = (0, 1, 0, 1, 2, 0)
NEG = -1e30
ORDER = (XT_ - 1, *range(XT_ - 1))
TAPS = (0, 1, 2, 3, 5, 6, 7, 8)
CONV = [(j, k) for js in ((0, 1), (2, 3), (4,), (5,), (6,)) for k in range(len(TAPS)) for j in js]

V_BN1, V_LN, V_BN2, V_CW, V_CB, V_NW, V_NB, V_D, V_DTB, V_AL = 0, 12, 14, 26, 89, 96, 102, 108, 114, 115
NV = 116
K_ID, K_ONE, K_M768, K_M96, K_G, K_GT, K_MASK = 0, 128, 256, 384, 480, 576, 960
K_EPS = K_MASK + 8
NK = K_EPS + 1
B_ID, B_BIG, B_DELTA, B_ONES, B_SEL = 0, 128, 512, 1280, 1536
NBF = 1664


def constants():
    k = np.zeros((P, NK), np.float32)
    k[:, K_ID:K_ID + P] = np.eye(P)
    k[:, K_ONE:K_ONE + P] = 1
    k[:, K_M768:K_M768 + P] = 1 / DI
    k[:, K_M96:K_M96 + PD] = 1 / PD
    k[:, K_EPS] = 1e-5
    per = C // GROUPS
    for t in range(CT):
        for p in range(P):
            g = (t * P + p) // per
            k[p, K_G + t * GROUPS + g] = 1 / per
            k[g, K_GT + t * P + p] = 1
    for r in range(QR + 3):
        q = QPART[r // QK] if r < QR else r - QR
        kk = KPART[r // QK] if r < QR else 0
        k[r, K_MASK + 0], k[r, K_MASK + 1] = -(q > 0), -(q == 2)
        k[r, K_MASK + 2], k[r, K_MASK + 3] = -(kk > 0), -(kk == 2)
    bf = np.zeros((P, NBF), np.float32)
    bf[:, B_ID:B_ID + P] = np.eye(P)
    j, i = np.arange(P)[:, None], np.arange(CH)[None, :]
    bf[:, B_BIG:B_BIG + HP * CH] = np.tile(np.where(j > i, NEG, 0), (1, HP))
    for part in range(3):
        for h in range(NH):
            r = 32 * part + h
            k[r, K_MASK + 4], k[r, K_MASK + 5] = -(part > 0), -(part == 2)
            k[r, K_MASK + 6 + h % 2] = -1
            bf[r, B_DELTA + (h // 2) * CH:B_DELTA + (h // 2 + 1) * CH] = 1
            bf[r, B_ONES + (h % 2) * P:B_ONES + (h % 2 + 1) * P] = 1
            bf[r, B_SEL + (h % 2) * 64:B_SEL + (h % 2 + 1) * 64] = 1
    return k, bf.astype(mybir.dt.np(BF16))


ONE = 1


class Steps:

    def __init__(self, eng, sem):
        self.eng, self.sem, self.base, self.n = eng, sem, 0, 0

    def enter(self, base):
        self.base, self.n = base, 0

    def __call__(self, ins):
        ins.then_inc(self.sem, 1)
        self.n += 1

    def join(self, but=0):
        self.eng.wait_ge(self.sem, self.base + (self.n - but + ONE))


def program(nc, x, vecs, wqkv, wproj, win, wdt, wout, consts, constb, out):
    ctx = ExitStack()
    with ctx:
        def sb(name, shape, dt=F32):
            return ctx.enter_context(nc.sbuf_tensor(name, shape, dt))

        def sem(name):
            return ctx.enter_context(nc.semaphore(name))

        xs_ = sb("x_sample", [P, CT, L])
        w_in = sb("w_in", [P, CT, DIN])
        w_out = sb("w_out", [P, NT, C])
        w_proj = sb("w_proj", [P, CT, C])
        w_dt_raw = sb("w_dt_raw", [P, CT, R3])
        w_dt = sb("w_dt", [P, CT, R3])
        w_qkv = sb("w_qkv", [PD, 3, PD])
        vec = sb("vec", [P, NV])
        kf = sb("kf", [P, NK])
        kb = sb("kb", [P, NBF], BF16)
        bn1s, bn1o = sb("bn1s", [PD, 3]), sb("bn1o", [PD, 3])
        bn2s, bn2o = sb("bn2s", [P, CT]), sb("bn2o", [P, CT])
        a_neg = sb("a_neg", [R3, 1])
        chan_stats = sb("chan_stats", [P, CT, NB, 6])
        chan_mv = sb("chan_mv", [P, CT, 2])
        group_mv = sb("group_mv", [GROUPS, 2])
        group_sc = sb("group_sc", [GROUPS, 4])
        gn_ab = sb("gn_ab", [P, CT, 2])
        beta = sb("beta", [P, XT_ + NT + 1])
        maxes = sb("maxes", [P, 4, 8])
        max4 = sb("max4", [P, 4])
        ident, one, mean768 = kf[:, K_ID:K_ID + P], kf[:, K_ONE:K_ONE + P], kf[:, K_M768:K_M768 + P]
        mean96 = kf[0:PD, K_M96:K_M96 + PD]

        def eps(rows=slice(0, P)):
            return kf[rows, K_EPS:K_EPS + 1]

        def mask(n, rows):
            return kf[rows, K_MASK + n:K_MASK + n + 1]

        AR = 29400
        arena = sb("arena", [P, AR])
        at = [0]

        def take(cols, dt=F32, rows=slice(0, P)):
            words = cols if dt == F32 else cols // 2
            v = arena[rows, at[0]:at[0] + words]
            at[0] += words
            assert at[0] <= AR, at[0]
            return v if dt == F32 else v.bitcast(dt)

        def shaped(v, *dims):
            names = "abcd"[:len(dims)]
            return v.rearrange(f"p ({' '.join(names)}) -> p {' '.join(names)}", **dict(zip(names, dims)))

        xn = shaped(take(CT * L), CT, L)
        q_st, k_st = take(L, BF16), take(L, BF16)
        v_t = shaped(take(32 * 97), 32, 97)
        common = at[0]
        ln_x = shaped(take(2 * TB), 2, TB)
        ln_sq = shaped(take(2 * TB), 2, TB)
        ln_y = shaped(take(2 * TB), 2, TB)
        qk_f = shaped(take(4 * TB), 2, 2, TB)
        qk_h = shaped(take(4 * TB, BF16), 2, 2, TB)
        qk_m = shaped(take(4 * TB, BF16), 2, 2, TB)
        v_sb = shaped(take(2 * TB), 2, TB)
        at[0] = common
        p_sb = shaped(take(4 * TB), 4, TB)
        cat = shaped(take(CT * TB), CT, TB)
        rec_b = take(TB)
        rec = take(TB)
        proj_y = shaped(take(CT * TB), CT, TB)
        negmax = shaped(take(4 * KS), 4, KS)
        nm_f, nm_h, nm_m = take(TB), take(TB, BF16), take(TB, BF16)
        at[0] = 0
        pre = shaped(take(XT_ * (ROWS + 2) * WP), XT_, ROWS + 2, WP)
        acc = shaped(take(XT_ * TB), XT_, TB)
        xbc = shaped(take(XT_ * TB), XT_, TB)
        y_sb = shaped(take(NT * TB), NT, TB)
        both = take(4 * HP * CH * 2)
        decay = shaped(both[:, 0:4 * HP * CH], 2, 2, HP, CH)
        att = shaped(both[:, 4 * HP * CH:], 2, 2, HP, CH)
        sq = shaped(both, NT, TB)
        grow = shaped(take(2 * HP * CH), 2, HP, CH)
        c_dec = shaped(take(2 * HP * CH), 2, HP, CH)
        both_x = take(2 * 2 * 2 * HP * HD)
        x_dt = shaped(both_x[:, 0:4 * HP * HD], 2, HP, 2, HD)
        x_w = shaped(both_x[:, 4 * HP * HD:], 2, HP, 2, HD)
        sum3 = shaped(both_x, HP, TB)
        c_dup = take(TB)
        state = shaped(take(NT * P), NT, P)
        st_dec = shaped(take(HP * P), HP, P)
        small = shaped(take(2 * 204), 2, 204)
        cs_diag = shaped(take(NT * TB, BF16), NT, TB)
        cs_neg = shaped(take(2 * TB, BF16), 2, TB)
        sp_e, sp_l, sp_d, sp_r, dt_sb, cs = (take(TB) for _ in range(6))
        cs_st, cs_h = take(TB, BF16), take(TB, BF16)
        row = take(TB)

        ps = ctx.enter_context(nc.psum_tensor("ps", [P, 8, TB], F32))

        names = """
        weights_loaded waited steps_v steps_a steps_p prepared vec_prepared met_v met
        x_loaded0 x_loaded1 x_loaded2 win_loaded stored stats_ready group_sums groups_ready group_back ab_ready
        vars_ready roots_ready ln_root row_root xn0_ready xn1_ready xn2_ready cleared
        mean_ready centred squared var_ready scaled ln_ready q_ready k_ready v_ready qk_taken qk_rounded
        v_taken vt_ready vt_copied q_stacked k_stacked
        max_scores max_read nm_ready nm_turned nm_taken nm_stacked
        scores exps pv_done recip_ready recip_spread recip_copied normed skip_relu proj_mm proj_taken x1_added
        beta_mm beta_ready w_scaled row0_mm row0_done row0_carried top_clear bottom_clear state_clear
        pj_mm pj_read0 pj_read1  centre_done conv_done silu_done carried bc_dup
        small_mm small_copied xt_mm xdt_ready e_mm exp_done xw_ready cd_ready sdec_ready att_ready
        y_mm y_read st_mm state_done
        dt_mm dt_abs dt_relu sp_ln sp_zero sp_prod sp_recip dt_ready cs_rounded cs_stacked cs_negated diag_ready
        sum1_ready y_centred sq_ready sum2_ready y_scaled y_affine z_copied gated out_read
        """.split()
        s = {n: sem(n) for n in names}

        started = sem("started")
        block = ctx.enter_context(nc.Block())
        MEETS = 4

        def own(eng):
            eng.sem_inc(s["waited"], 1)

        def meet(eng, b, n):
            own(eng)
            eng.drain().then_inc(s["met"], 1)
            eng.wait_ge(s["met"], ONE + 5 * (MEETS * b + n + 1))
            own(eng)

        def begin(eng):
            eng.wait_ge(started, 1)

        @block.sync
        def _(sp):
            for first in s.values():
                sp.sem_inc(first, ONE)
            sp.sem_inc(started, 1)
            for dst, src in ((vec, vecs), (kf, consts), (kb, constb), (w_qkv, wqkv), (w_proj, wproj),
                             (w_dt_raw, wdt), (w_out, wout)):
                sp.dma_start(dst[:], src[:]).then_inc(s["weights_loaded"], 16)
            with sp.Fori(0, B) as b:
                sp.wait_ge(s["stored"], ONE + b * (16 * CT * NB))
                own(sp)
                for t in range(CT):
                    src = x.rearrange("b (t p) l -> (b t) p l", p=P)
                    sp.dma_start(xs_[:, t, :], src[b * CT + t]).then_inc(s[f"x_loaded{t}"], 16)
                sp.dma_start(w_in[:], win[:]).then_inc(s["win_loaded"], 16)
                for n in range(MEETS - 1):
                    meet(sp, b, n)
                with sp.Fori(0, NB) as i:
                    G = sp.snap(b * NB + i)
                    sp.wait_ge(s["silu_done"], ONE + G * XT_ + 1)
                    for half in range(2):
                        sp.dma_start(c_dup[64 * half:64 * half + 64, :], xbc[64:128, XT_ - 1, :]).then_inc(s["bc_dup"], 16)
                    for m in range(CT):
                        sp.wait_ge(s["out_read"], ONE + G * CT + m + 1)
                        own(sp)
                        dst = out.rearrange("b (t p) l -> (b t) p l", p=P)
                        sp.dma_start(dst[b * CT + m, :, bass.ds(i * TB, TB)],
                                     xs_[:, m, bass.ds(i * TB, TB)]).then_inc(s["stored"], 16)
                meet(sp, b, MEETS - 1)
            sp.wait_ge(s["stored"], ONE + 16 * B * CT * NB)

        def gn_pe(pe, n):
            pe.wait_ge(s["stats_ready"], ONE + n + 1)
            for t in range(CT):
                mm = nc.tensor.matmul(ps[0:GROUPS, 7, 0:2], kf[:, K_G + t * GROUPS:K_G + (t + 1) * GROUPS],
                                      chan_mv[:, t, :], start=(t == 0), stop=(t == CT - 1))
            mm.then_inc(s["group_sums"], 1)
            pe.wait_ge(s["groups_ready"], ONE + n + 1)
            for t in range(CT):
                mm = nc.tensor.matmul(ps[:, 7, 8 + 2 * t:10 + 2 * t], kf[0:GROUPS, K_GT + t * P:K_GT + (t + 1) * P],
                                      group_sc[:, 2:4], start=True, stop=True)
            mm.then_inc(s["group_back"], 1)

        def qkv_pe(pe, b, u):
            G = pe.snap(b * (NB // 2) + u)
            for j in range(2):
                pe.wait_ge(s["v_taken"], ONE + 2 * G)
                mm = nc.tensor.matmul(ps[0:PD, j, :], mean96, xn[0:PD, 0, bass.ds(u * (2 * TB) + j * TB, TB)],
                                      start=True, stop=True)
                mm.then_inc(s["mean_ready"], 1)
            for j in range(2):
                pe.wait_ge(s["squared"], ONE + 2 * G + j + 1)
                pe.wait_ge(s["vt_copied"], ONE + 2 * G)
                nc.tensor.matmul(ps[0:PD, 2 + j, :], mean96, ln_sq[0:PD, j, :], start=True, stop=True)\
                    .then_inc(s["var_ready"], 1)
            for j in range(2):
                pe.wait_ge(s["ln_ready"], ONE + 2 * G + j + 1)
                pe.wait_ge(s["qk_taken"], ONE + 4 * G)
                for w, name in ((0, "q_ready"), (1, "k_ready")):
                    nc.tensor.matmul(ps[0:PD, 4 + 2 * w + j, :], w_qkv[:, w, :], ln_y[0:PD, j, :],
                                     start=True, stop=True).then_inc(s[name], 1)
                nc.tensor.matmul(ps[0:PD, j, :], w_qkv[:, 2, :], ln_y[0:PD, j, :], start=True, stop=True)\
                    .then_inc(s["v_ready"], 1)
            for j in range(2):
                pe.wait_ge(s["v_taken"], ONE + 2 * G + j + 1)
                for c in range(TB // P):
                    mm = nc.tensor.transpose(ps[:, 2 + j, c * PD:(c + 1) * PD], v_sb[0:PD, j, c * P:(c + 1) * P],
                                             ident[0:PD, 0:PD])
                mm.then_inc(s["vt_ready"], 1)

        KT = L // P
        MAX_AT = [min(KT, max(0, st - 3) * 3 // 2) for st in range(KT + 2)]
        TURN_AT, SPREAD_AT, PROJ_AT = 27, 3, (6, 9, 12)

        def out_bank(qb):
            return 6 + qb % 2

        def max_pe(pe, b, nq, g, n):
            mt, kc = n // NB, n % NB
            pe.wait_ge(s["max_read"], ONE + KT * g + (n - 1 if n >= 2 else 0))
            nc.tensor.matmul(ps[:, 2 + n % 2, :], q_st[0:QR, bass.ds(nq * TB + mt * P, P)],
                             k_st[0:QR, kc * TB:(kc + 1) * TB], start=True, stop=True).then_inc(s["max_scores"], 1)

        def turn_pe(pe, g, now):
            pe.wait_ge(s["nm_ready"], ONE + g + 1)
            pe.wait_ge(s["proj_taken"], ONE + CT * now)
            for mt in range(4):
                mm = nc.tensor.matmul(ps[0:KS, 4, mt * P:(mt + 1) * P], negmax[:, mt, :], ident,
                                      start=True, stop=True)
            mm.then_inc(s["nm_turned"], 1)

        def spread_pe(pe, g, turned):
            pe.wait_ge(s["recip_ready"], ONE + g + 1)
            pe.wait_ge(s["nm_taken"], ONE + turned)
            nc.tensor.matmul(ps[0:PD, 4, :], one[96:97, 0:PD], rec[96:97, :], start=True, stop=True)\
                .then_inc(s["recip_spread"], 1)

        def proj_pe(pe, g, m):
            if m == 0:
                pe.wait_ge(s["normed"], ONE + g + 1)
                pe.wait_ge(s["skip_relu"], ONE + 2 * g + 2)
            else:
                pe.wait_ge(s["proj_taken"], ONE + CT * g + m)
            for t in range(CT):
                mm = nc.tensor.matmul(ps[:, 4, :], w_proj[:, t, m * P:(m + 1) * P], cat[:, t, :],
                                      start=(t == 0), stop=(t == CT - 1))
            mm.then_inc(s["proj_mm"], 1)

        def attend_pe(pe, b, qb, has_prev, has_next):
            g = pe.snap(b * NB + qb) if not isinstance(qb, int) else b * NB + qb
            pe.wait_ge(s["nm_stacked"], ONE + g + 1)
            for st in range(KT + 1):
                if st < KT:
                    pe.wait_ge(s["exps"], ONE + KT * g + (st - 1 if st >= 2 else 0))
                    nc.tensor.matmul(ps[:, st % 2, :], k_st[0:KS, st * P:(st + 1) * P],
                                     q_st[0:KS, bass.ds(qb * TB, TB)], start=True, stop=True).then_inc(s["scores"], 1)
                    items = range(MAX_AT[st], MAX_AT[st + 1]) if has_next else ()
                    for n in items[:1]:
                        max_pe(pe, b, qb + 1, g + 1, n)
                if has_prev:
                    if st == SPREAD_AT:
                        spread_pe(pe, g - 1, g + 1)
                    if st in PROJ_AT:
                        proj_pe(pe, g - 1, PROJ_AT.index(st))
                if has_next and st == TURN_AT:
                    turn_pe(pe, g + 1, g)
                if st >= 1:
                    pe.wait_ge(s["exps"], ONE + KT * g + st)
                    if st == 1 and has_prev:
                        pe.wait_ge(s["normed"], ONE + g - 1)
                    mm = nc.tensor.matmul(ps[0:97, bass.ds(out_bank(qb), 1), :].rearrange("p a n -> p (a n)"),
                                          v_t[:, st - 1, :], p_sb[:, (st - 1) % 4, :],
                                          start=(st == 1), stop=(st == KT))
                    mm.then_inc(s["pv_done"], 1)
                if st < KT:
                    for n in items[1:]:
                        max_pe(pe, b, qb + 1, g + 1, n)

        OUTS = 2 + NT + CT
        EARLY = 5
        PER = XT_ + OUTS
        ALL = NB * PER

        SEQ = "a0 a1 a2 a3 a4 z0 m1 z1 z2 z3 a5 m2 z4 z5 a6 o0 o1 o2".split()
        SEQ_LAST = [n for n in SEQ if n[0] != "a"]

        def item(name, nxt):
            return XT_ + (SEQ if nxt else SEQ_LAST).index(name)

        def pj_wait(pe, b, i, at0):
            pe.wait_ge(s[f"pj_read{at0 % 2}"], ONE + b * (ALL // 2) + i * (PER // 2) + at0 // 2)

        def in_proj_pe(pe, b, i, j, at0, rows):
            pj_wait(pe, b, i, at0)
            t = ORDER[j]
            n = rows * W
            start = (i + 1) * TB + W
            for k in range(CT):
                mm = nc.tensor.matmul(ps[:, at0 % 2, 0:n], w_in[:, k, DI + t * P:DI + (t + 1) * P],
                                      xs_[:, k, bass.ds(start, n)], start=(k == 0), stop=(k == CT - 1))
            mm.then_inc(s["pj_mm"], 1)

        def dt_pe(pe, G, i1):
            pe.wait_ge(s["small_copied"], ONE + NC * G)
            for k in range(CT):
                mm = nc.tensor.matmul(ps[0:R3, 5, :], w_dt[:, k, :], xs_[:, k, bass.ds(i1 * TB, TB)],
                                      start=(k == 0), stop=(k == CT - 1))
            mm.then_inc(s["dt_mm"], 1)

        def unit_a_pe(pe, G, u):
            c, hf = u // 2, u % 2
            tok = slice(c * CH, (c + 1) * CH)
            pairs = slice(HP * hf, HP * hf + HP)
            if hf == 0:
                if c == 0:
                    pe.wait_ge(s["bc_dup"], ONE + 32 * G + 32)
                    pe.wait_ge(s["cs_negated"], ONE + G + 1)
                    pe.wait_ge(s["dt_ready"], ONE + G + 1)
                    pe.wait_ge(s["dt_abs"], ONE + G + 1)
                    pe.wait_ge(s["dt_relu"], ONE + G + 1)
                pe.wait_ge(s["small_copied"], ONE + NC * G + c)
                nc.tensor.matmul(ps[:, 5, 0:P], xbc[0:NS, XT_ - 1, tok], c_dup[0:NS, tok], start=True, stop=True)
                nc.tensor.transpose(ps[:, 5, P:P + NS], xbc[0:NS, XT_ - 1, tok], ident[0:NS, 0:NS])
                nc.tensor.transpose(ps[:, 5, P + NS:P + NS + NH], dt_sb[0:NH, tok], ident[0:NH, 0:NH])\
                    .then_inc(s["small_mm"], 1)
            if hf == 0:
                pe.wait_ge(s["diag_ready"], ONE + NC * G + c + 1)
            for par in range(3):
                e = 3 * u + par
                if par == 2:
                    if u < 2:
                        pe.wait_ge(s["silu_done"], ONE + XT_ * G + 1 + HP * (u + 1))
                    pe.wait_ge(s["xdt_ready"], ONE + NU * G + u)
                    for t in range(HP):
                        mm = nc.tensor.transpose(ps[:, 4, t * P:(t + 1) * P], xbc[:, HP * hf + t, tok], ident)
                    mm.then_inc(s["xt_mm"], 1)
                pe.wait_ge(s["exp_done"], ONE + 3 * NU * G + (e - 1 if e >= 2 else 0))
                bank = ps[:, 2 + e % 2, 0:HP * CH]
                diag = cs_diag[0:R3, pairs, tok]
                if par == 2:
                    mm = nc.tensor.matmul(bank, kb[0:R3, B_SEL:B_SEL + P], diag, start=True, stop=True)
                else:
                    nc.tensor.matmul(bank, kb[0:R3, B_ONES + par * P:B_ONES + (par + 1) * P], diag,
                                     start=True, stop=False)
                    nc.tensor.matmul(bank, cs_neg[0:R3, par, tok],
                                     kb[0:R3, B_DELTA + HP * hf * CH:B_DELTA + HP * (hf + 1) * CH],
                                     start=False, stop=False)
                    mm = nc.tensor.matmul(bank, kb[:, B_ID:B_ID + P], kb[:, B_BIG:B_BIG + HP * CH],
                                          start=False, stop=True)
                mm.then_inc(s["e_mm"], 1)

        def unit_b_pe(pe, b, G, u):
            c, hf, d = u // 2, u % 2, u % 2
            pe.wait_ge(s["y_read"], ONE + NU * G + u)
            pe.wait_ge(s["cd_ready"], ONE + NU * G + u + 1)
            pe.wait_ge(s["att_ready"], ONE + NU * G + u + 1)
            pe.wait_ge(s["state_done"], ONE + NU * G + max(u - 1, 0))
            if u < 2:
                pe.wait_ge(s["state_clear"], ONE + b + 1)
            for t in range(HP):
                y = ps[:, 6, t * CH:(t + 1) * CH]
                nc.tensor.matmul(y, state[:, HP * hf + t, :], c_dec[:, d, t, :], start=True, stop=False,
                                 skip_group_check=True)
                for par in range(2):
                    mm = nc.tensor.matmul(y[64 * par:64 * par + 64, :], x_dt[:, d, t, par, :], att[:, d, par, t, :],
                                          start=False, stop=(par == 1), skip_group_check=True)
            mm.then_inc(s["y_mm"], 1)
            pe.wait_ge(s["state_done"], ONE + NU * G + u)
            pe.wait_ge(s["xw_ready"], ONE + NU * G + u + 1)
            for par in range(2):
                mm = nc.tensor.matmul(ps[64 * par:64 * par + 64, 7, 0:HP * HD], small[:, c % 2, P:P + NS],
                                      x_w[:, d, :, par, :], start=True, stop=True)
            mm.then_inc(s["st_mm"], 1)

        def block_pe(pe, b, i, nxt):
            G = b * NB + i if isinstance(i, int) else pe.snap(b * NB + i)
            for u in range(NU):
                unit_a_pe(pe, G, u)
                if u:
                    unit_b_pe(pe, b, G, u - 1)
                if nxt and u % 2 == 1:
                    for t in (u - 1, u):
                        if t < EARLY:
                            in_proj_pe(pe, b, i, t, item(f"a{t}", nxt), nxt)
            unit_b_pe(pe, b, G, NU - 1)

            def moment(name, ready, count):
                at0 = item(name, nxt)
                pj_wait(pe, b, i, at0)
                pe.wait_ge(s[ready], count)
                nc.tensor.matmul(ps[:, at0 % 2, :], mean768, row, start=True, stop=True).then_inc(s["pj_mm"], 1)

            def z(t):
                at0 = item(f"z{t}", nxt)
                pj_wait(pe, b, i, at0)
                for k in range(CT):
                    mm = nc.tensor.matmul(ps[:, at0 % 2, :], w_in[:, k, t * P:(t + 1) * P],
                                          xs_[:, k, bass.ds(i * TB, TB)], start=(k == 0), stop=(k == CT - 1))
                mm.then_inc(s["pj_mm"], 1)

            z(0)
            moment("m1", "sum1_ready", ONE + NC * (G + 1))
            for t in (1, 2, 3):
                z(t)
            if nxt:
                in_proj_pe(pe, b, i, 5, item("a5", nxt), nxt)
            moment("m2", "sum2_ready", ONE + G + 1)
            for t in (4, 5):
                z(t)
            if nxt:
                in_proj_pe(pe, b, i, 6, item("a6", nxt), nxt)
                dt_pe(pe, G + 1, i + 1)
            for m in range(CT):
                at0 = item(f"o{m}", nxt)
                pj_wait(pe, b, i, at0)
                for t in range(NT):
                    if m == 0:
                        pe.wait_ge(s["gated"], ONE + NT * G + t + 1)
                    mm = nc.tensor.matmul(ps[:, at0 % 2, :], w_out[:, t, m * P:(m + 1) * P], y_sb[:, t, :],
                                          start=(t == 0), stop=(t == NT - 1))
                mm.then_inc(s["pj_mm"], 1)

        @block.tensor
        def _(pe):
            begin(pe)
            pe.wait_ge(s["weights_loaded"], ONE + 16 * 7)
            with pe.Fori(0, B) as b:
                gn_pe(pe, 2 * b)
                pe.wait_ge(s["xn0_ready"], ONE + b + 1)
                own(pe)
                with pe.Fori(0, NB // 2) as u:
                    qkv_pe(pe, b, u)
                meet(pe, b, 0)
                for n in range(32):
                    max_pe(pe, b, 0, b * NB, n)
                turn_pe(pe, b * NB, b * NB)
                attend_pe(pe, b, 0, False, True)
                with pe.Fori(1, NB - 1) as qb:
                    attend_pe(pe, b, qb, True, True)
                attend_pe(pe, b, NB - 1, True, False)
                spread_pe(pe, b * NB + (NB - 1), b * NB + NB)
                for m in range(CT):
                    proj_pe(pe, b * NB + (NB - 1), m)
                meet(pe, b, 1)
                gn_pe(pe, 2 * b + 1)
                pe.wait_ge(s["win_loaded"], ONE + 16 * b + 16)
                pe.wait_ge(s["ab_ready"], ONE + 2 * b + 2)
                for m in range(XT_ + NT + 1):
                    rows = P if m < XT_ + NT else R3
                    for k in range(CT):
                        w = w_in[:, k, m * P:(m + 1) * P] if m < XT_ + NT else w_dt_raw[:, k, :]
                        mm = nc.tensor.matmul(ps[0:rows, 6, m:m + 1], w, gn_ab[:, k, 1:2], start=(k == 0),
                                              stop=(k == CT - 1))
                mm.then_inc(s["beta_mm"], 1)
                meet(pe, b, 2)
                for t in range(XT_):
                    for k in range(CT):
                        mm = nc.tensor.matmul(ps[:, 4, t * W:(t + 1) * W], w_in[:, k, DI + t * P:DI + (t + 1) * P],
                                              xs_[:, k, 0:W], start=(k == 0), stop=(k == CT - 1))
                mm.then_inc(s["row0_mm"], 1)
                dt_pe(pe, b * NB, 0)
                for t in range(XT_):
                    in_proj_pe(pe, b, -1, t, PER + t, ROWS)
                pe.wait_ge(s["row0_done"], ONE + b + 1)
                own(pe)
                with pe.Fori(0, NB - 2) as i:
                    block_pe(pe, b, i, ROWS)
                block_pe(pe, b, NB - 2, ROWS - 1)
                block_pe(pe, b, NB - 1, 0)
                meet(pe, b, 3)

        def gn_act(act, n):
            act.wait_ge(s["vars_ready"], ONE + n + 1)
            nc.scalar.activation(group_sc[:, 1:2], group_sc[:, 1:2], ACT.Sqrt, bias=eps(slice(0, GROUPS)))\
                .then_inc(s["roots_ready"], 1)

        def block_act(act, b, i, nxt, step):
            G = b * NB + i if isinstance(i, int) else act.snap(b * NB + i)
            for j, t in enumerate(ORDER):
                if j == 1:
                    act.wait_ge(s["gated"], ONE + NT * G)
                act.wait_ge(s["conv_done"], ONE + XT_ * G + j + 1)
                nc.scalar.activation(xbc[:, t, :], acc[:, t, :], ACT.Silu).then_inc(s["silu_done"], 1)
            for u in range(NU):
                c, hf, d = u // 2, u % 2, u % 2
                if hf == 0:
                    act.wait_ge(s["small_mm"], ONE + NC * G + c + 1)
                    act.wait_ge(s["att_ready"], ONE + NU * G + max(2 * c - 2, 0))
                    act.wait_ge(s["st_mm"], ONE + NU * G + max(2 * c - 2, 0))
                    nc.scalar.copy(small[:, c % 2, :], ps[:, 5, 0:204]).then_inc(s["small_copied"], 1)
                for par in range(3):
                    e = 3 * u + par
                    act.wait_ge(s["e_mm"], ONE + 3 * NU * G + e + 1)
                    if par == 0:
                        for name in ("att_ready", "xw_ready", "cd_ready", "sdec_ready"):
                            act.wait_ge(s[name], ONE + NU * G + max(u - 1, 0))
                        if u == 0:
                            act.wait_ge(s["sum2_ready"], ONE + G)
                    dst = grow[:, d, :, :] if par == 2 else decay[:, d, par, :, :]
                    nc.scalar.activation(dst, shaped(ps[:, 2 + e % 2, 0:HP * CH], HP, CH), ACT.Exp)\
                        .then_inc(s["exp_done"], 1)
                if nxt and hf == 1:
                    for t in (u - 1, u):
                        if t < EARLY:
                            take_pre(act, b, i, G + 1, t, item(f"a{t}", nxt), nxt)

            def z_copy(t):
                at0 = item(f"z{t}", nxt)
                act.wait_ge(s["pj_mm"], ONE + b * ALL + i * PER + at0 + 1)
                if t == 0:
                    act.wait_ge(s["y_read"], ONE + NU * G + NU)
                    act.wait_ge(s["st_mm"], ONE + NU * G + NU)
                nc.scalar.activation(xbc[:, t, :], ps[:, at0 % 2, :], ACT.Identity, bias=beta[:, t:t + 1])\
                    .then_inc(s[f"pj_read{at0 % 2}"], 1)

            z_copy(0)
            for half in range(2):
                act.wait_ge(s["y_centred"], ONE + 2 * G + half + 1)
                if half == 0:
                    act.wait_ge(s["y_mm"], ONE + NU * G + NU)
                nc.scalar.activation(sq[:, HP * half:HP * half + HP, :], y_sb[:, HP * half:HP * half + HP, :],
                                     ACT.Square).then_inc(s["sq_ready"], 1)
            for t in (1, 2, 3):
                z_copy(t)
            if nxt:
                take_pre(act, b, i, G + 1, 5, item("a5", nxt), nxt)
            at0 = item("m2", nxt)
            act.wait_ge(s["pj_mm"], ONE + b * ALL + i * PER + at0 + 1)
            nc.scalar.activation(row, ps[:, at0 % 2, :], ACT.Sqrt, bias=eps()).then_inc(s[f"pj_read{at0 % 2}"], 1)
            for t in (4, 5):
                z_copy(t)
            if nxt:
                take_pre(act, b, i, G + 1, 6, item("a6", nxt), nxt)
            if nxt:
                softplus_act(act, G + 1)
            for t in range(NT):
                act.wait_ge(s["y_scaled"], ONE + 2 * G + t // HP + 1)
                nc.scalar.activation(y_sb[:, t, :], y_sb[:, t, :], ACT.Identity, bias=vec[:, V_NB + t:V_NB + t + 1],
                                     scale=vec[:, V_NW + t:V_NW + t + 1]).then_inc(s["y_affine"], 1)

        def take_pre(act, b, i, G1, j, at0, rows):
            act.wait_ge(s["pj_mm"], ONE + b * ALL + i * PER + at0 + 1)
            act.wait_ge(s["carried"], ONE + G1 + 1)
            t = ORDER[j]
            nc.scalar.activation(pre[:, t, 2:2 + rows, 1:1 + W], shaped(ps[:, at0 % 2, 0:rows * W], rows, W),
                                 ACT.Identity, bias=beta[:, NT + t:NT + t + 1]).then_inc(s[f"pj_read{at0 % 2}"], 1)
            act.wait_ge(s[f"pj_read{at0 % 2}"], ONE + b * (ALL // 2) + i * (PER // 2) + at0 // 2 + 1)
            act.wait_ge(s["silu_done"], ONE + G1 * XT_)
            nc.scalar.activation(shaped(acc[:, t, :], ROWS, W), pre[:, t, 1:1 + ROWS, 1:1 + W], ACT.Identity,
                                 bias=vec[:, V_CB + t:V_CB + t + 1],
                                 scale=vec[:, V_CW + 9 * t + 4:V_CW + 9 * t + 5]).then_inc(s["centre_done"], 1)

        def softplus_act(act, G1):
            act.wait_ge(s["dt_mm"], ONE + G1 + 1)
            act.wait_ge(s["sp_prod"], ONE + G1)
            dtb = beta[0:R3, XT_ + NT:XT_ + NT + 1]
            nc.scalar.activation(sp_l[0:R3, :], ps[0:R3, 5, :], ACT.Abs, bias=dtb).then_inc(s["dt_abs"], 1)
            act.wait_ge(s["cs_stacked"], ONE + G1)
            nc.scalar.activation(cs[0:R3, :], ps[0:R3, 5, :], ACT.Relu, bias=dtb).then_inc(s["dt_relu"], 1)
            act.wait_ge(s["dt_abs"], ONE + G1 + 1)
            nc.scalar.activation(sp_e[0:R3, :], sp_l[0:R3, :], ACT.Exp, scale=-1.0).then_inc(s["sp_ln"], 1)
            act.wait_ge(s["sp_ln"], ONE + 2 * G1 + 1)
            nc.scalar.activation(sp_l[0:R3, :], sp_e[0:R3, :], ACT.Ln, bias=one[0:R3, 0:1]).then_inc(s["sp_ln"], 1)

        @block.scalar
        def _(act):
            begin(act)
            act.wait_ge(s["weights_loaded"], ONE + 16 * 7)
            nc.scalar.activation(a_neg[:, :], vec[0:R3, V_AL:V_AL + 1], ACT.Exp).then_inc(s["steps_a"], 1)
            act.wait_ge(s["steps_a"], ONE + 1)
            nc.scalar.activation(a_neg[:, :], a_neg[:, :], ACT.Copy, scale=-1.0).then_inc(s["prepared"], 1)
            nc.scalar.activation(bn1s[:], vec[0:PD, V_BN1 + 9:V_BN1 + 12], ACT.Sqrt, bias=eps(slice(0, PD)))\
                .then_inc(s["prepared"], 1)
            nc.scalar.activation(bn2s[:], vec[:, V_BN2 + 9:V_BN2 + 12], ACT.Sqrt, bias=eps()).then_inc(s["prepared"], 1)
            act.wait_ge(s["vec_prepared"], ONE + 1)
            with act.Fori(0, B) as b:
                gn_act(act, 2 * b)
                act.wait_ge(s["ab_ready"], ONE + 2 * b + 1)
                nc.scalar.activation(xn[:, 0, :], xs_[:, 0, :], ACT.Identity, bias=gn_ab[:, 0, 1:2],
                                     scale=gn_ab[:, 0, 0:1]).then_inc(s["xn0_ready"], 1)
                with act.Fori(0, NB // 2) as u:
                    G = act.snap(b * (NB // 2) + u)
                    for j in range(2):
                        act.wait_ge(s["centred"], ONE + 2 * G + j + 1)
                        act.wait_ge(s["scaled"], ONE + 2 * G)
                        nc.scalar.activation(ln_sq[0:PD, j, :], ln_x[0:PD, j, :], ACT.Square).then_inc(s["squared"], 1)
                    for j in range(2):
                        act.wait_ge(s["var_ready"], ONE + 2 * G + j + 1)
                        nc.scalar.activation(ln_sq[0:PD, j, :], ps[0:PD, 2 + j, :], ACT.Sqrt, bias=eps(slice(0, PD)))\
                            .then_inc(s["ln_root"], 1)
                    for j in range(2):
                        act.wait_ge(s["scaled"], ONE + 2 * G + j + 1)
                        act.wait_ge(s["v_ready"], ONE + 2 * G)
                        nc.scalar.activation(ln_y[0:PD, j, :], ln_x[0:PD, j, :], ACT.Identity,
                                             bias=vec[0:PD, V_LN + 1:V_LN + 2], scale=vec[0:PD, V_LN:V_LN + 1])\
                            .then_inc(s["ln_ready"], 1)
                    for j in range(2):
                        act.wait_ge(s["v_ready"], ONE + 2 * G + j + 1)
                        act.wait_ge(s["q_stacked"], ONE + 2 * G)
                        act.wait_ge(s["k_stacked"], ONE + 2 * G)
                        act.wait_ge(s["vt_ready"], ONE + 2 * G)
                        nc.scalar.activation(v_sb[0:PD, j, :], ps[0:PD, j, :], ACT.Identity, bias=bn1o[:, 2:3],
                                             scale=bn1s[:, 2:3]).then_inc(s["v_taken"], 1)
                        for w in range(2):
                            bank = ps[0:PD, 4 + 2 * w + j, :]
                            nc.scalar.activation(qk_f[0:PD, w, j, :], bank, ACT.Identity, bias=bn1o[:, w:w + 1],
                                                 scale=bn1s[:, w:w + 1])
                            nc.scalar.activation(qk_h[0:PD, w, j, :], bank, ACT.Identity, bias=bn1o[:, w:w + 1],
                                                 scale=bn1s[:, w:w + 1]).then_inc(s["qk_taken"], 1)
                meet(act, b, 0)

                def take_max(g):
                    act.wait_ge(s["nm_turned"], ONE + g + 1)
                    nc.scalar.copy(nm_f[96:99, :], ps[96:99, 4, :])
                    nc.scalar.copy(nm_h[96:99, :], ps[96:99, 4, :]).then_inc(s["nm_taken"], 1)

                def take_recip(g):
                    act.wait_ge(s["recip_spread"], ONE + g + 1)
                    nc.scalar.copy(rec_b[0:PD, :], ps[0:PD, 4, :]).then_inc(s["recip_copied"], 1)

                def take_proj(g, m):
                    act.wait_ge(s["proj_mm"], ONE + CT * g + m + 1)
                    act.wait_ge(s["x1_added"], ONE + CT * g)
                    nc.scalar.activation(proj_y[:, m, :], ps[:, 4, :], ACT.Identity, bias=bn2o[:, m:m + 1],
                                         scale=bn2s[:, m:m + 1]).then_inc(s["proj_taken"], 1)

                def attend_act(qb, has_prev, has_next):
                    g = act.snap(b * NB + qb) if not isinstance(qb, int) else b * NB + qb
                    blk = bass.ds(qb * TB, TB)
                    for st in range(KT):
                        act.wait_ge(s["scores"], ONE + KT * g + st + 1)
                        act.wait_ge(s["pv_done"], ONE + KT * g + max(st - 3, 0))
                        nc.scalar.activation(p_sb[:, st % 4, :], ps[:, st % 2, :], ACT.Exp,
                                             scale=QK ** -0.5).then_inc(s["exps"], 1)
                        if has_prev:
                            if st == SPREAD_AT:
                                take_recip(g - 1)
                            if st - 1 in PROJ_AT:
                                take_proj(g - 1, PROJ_AT.index(st - 1))
                        if st == 16:
                            act.wait_ge(s["proj_mm"], ONE + CT * g)
                            act.wait_ge(s["xn1_ready"], ONE + b + 1)
                            act.wait_ge(s["xn2_ready"], ONE + b + 1)
                            nc.scalar.activation(cat[PD:P, 0, :], xn[PD:P, 0, blk], ACT.Relu).then_inc(s["skip_relu"], 1)
                            nc.scalar.activation(cat[:, 1:CT, :], xn[:, 1:CT, blk], ACT.Relu)\
                                .then_inc(s["skip_relu"], 1)
                        if has_next and st == TURN_AT:
                            take_max(g + 1)

                take_max(b * NB)
                attend_act(0, False, True)
                with act.Fori(1, NB - 1) as qb:
                    attend_act(qb, True, True)
                attend_act(NB - 1, True, False)
                take_recip(b * NB + (NB - 1))
                for m in range(CT):
                    take_proj(b * NB + (NB - 1), m)
                meet(act, b, 1)
                gn_act(act, 2 * b + 1)
                meet(act, b, 2)
                act.wait_ge(s["row0_mm"], ONE + b + 1)
                act.wait_ge(s["top_clear"], ONE + 2 * b + 2)
                for t in range(XT_):
                    ins = nc.scalar.activation(pre[:, t, 9, 1:1 + W], ps[:, 4, t * W:(t + 1) * W], ACT.Identity,
                                               bias=beta[:, NT + t:NT + t + 1])
                ins.then_inc(s["row0_done"], 1)
                softplus_act(act, b * NB)
                for t in range(XT_):
                    take_pre(act, b, -1, b * NB, t, PER + t, ROWS)
                with act.Fori(0, NB - 2) as i:
                    block_act(act, b, i, ROWS, None)
                block_act(act, b, NB - 2, ROWS - 1, None)
                block_act(act, b, NB - 1, 0, None)
                meet(act, b, 3)

        def dt_pool(pool, G1, step):
            r = slice(0, R3)
            pool.wait_ge(s["sp_zero"], ONE + G1 + 1)
            step(nc.gpsimd.tensor_tensor(sp_d[r, :], sp_d[r, :], sp_r[r, :], ALU.add))
            pool.wait_ge(s["sp_ln"], ONE + 2 * G1 + 2)
            step(nc.gpsimd.tensor_tensor(sp_r[r, :], sp_l[r, :], sp_r[r, :], ALU.add))
            step.join()
            nc.gpsimd.tensor_tensor(sp_l[r, :], sp_r[r, :], sp_e[r, :], ALU.mult).then_inc(s["sp_prod"], 1)

        def diag_pool(pool, G1):
            pool.wait_ge(s["cs_stacked"], ONE + G1 + 1)
            own(pool)
            for c in range(NC):
                tok = slice(c * CH, (c + 1) * CH)
                nc.gpsimd.tensor_tensor(cs_diag[0:R3, :, tok],
                                        cs_st[0:R3, tok].unsqueeze(1).broadcast_to([R3, NT, CH]),
                                        shaped(kb[0:R3, B_DELTA:B_DELTA + NT * CH], NT, CH), ALU.mult)\
                    .then_inc(s["diag_ready"], 1)

        def carry_pool(pool, G1):
            pool.wait_ge(s["conv_done"], ONE + G1 * XT_)
            own(pool)
            nc.gpsimd.tensor_copy(pre[:, :, 0:2, :], pre[:, :, ROWS:ROWS + 2, :]).then_inc(s["carried"], 1)

        def block_pool(pool, b, i, nxt, step):
            G = b * NB + i if isinstance(i, int) else pool.snap(b * NB + i)
            if nxt:
                carry_pool(pool, G + 1)
            def sum_y(c):
                tok = slice(c * CH, (c + 1) * CH)
                pool.wait_ge(s["y_read"], ONE + NU * G + 2 * c + 2)
                step(nc.gpsimd.tensor_tensor(row[:, tok], y_sb[:, 0, tok], y_sb[:, 1, tok], ALU.add))
                for t in range(2, NT):
                    step.join()
                    ins = nc.gpsimd.tensor_tensor(row[:, tok], row[:, tok], y_sb[:, t, tok], ALU.add)
                    if t < NT - 1:
                        step(ins)
                ins.then_inc(s["sum1_ready"], 1)

            if nxt == ROWS - 1:
                pool.wait_ge(s["carried"], ONE + G + 2)
                own(pool)
                nc.gpsimd.memset(pre[:, :, ROWS + 1, :], 0.0).then_inc(s["bottom_clear"], 1)
            for u in range(NU):
                c, hf, d = u // 2, u % 2, u % 2
                tok = slice(c * CH, (c + 1) * CH)
                pool.wait_ge(s["exp_done"], ONE + 3 * NU * G + 3 * u + 3)
                if u == 0:
                    pool.wait_ge(s["bc_dup"], ONE + 32 * G + 32)
                pool.wait_ge(s["y_mm"], ONE + NU * G + max(u - 1, 0))
                nc.gpsimd.tensor_tensor(c_dec[:, d, :, :], grow[:, d, :, :],
                                        c_dup[:, tok].unsqueeze(1).broadcast_to([P, HP, CH]), ALU.mult)\
                    .then_inc(s["cd_ready"], 1)
                pool.wait_ge(s["st_mm"], ONE + NU * G + max(u - 1, 0))
                pool.wait_ge(s["xdt_ready"], ONE + NU * G + u + 1)
                last = decay[:, d, :, :, CH - 1].rearrange("p a t -> p t a")
                nc.gpsimd.tensor_tensor(x_w[:, d, :, :, :], x_dt[:, d, :, :, :],
                                        last.unsqueeze(3).broadcast_to([P, HP, 2, HD]), ALU.mult)\
                    .then_inc(s["xw_ready"], 1)
                pool.wait_ge(s["state_done"], ONE + NU * G + u)
                if u < 2:
                    pool.wait_ge(s["state_clear"], ONE + b + 1)
                nc.gpsimd.tensor_tensor(st_dec, state[:, HP * hf:HP * hf + HP, :],
                                        grow[:, d, :, CH - 1:CH].broadcast_to([P, HP, P]), ALU.mult)\
                    .then_inc(s["sdec_ready"], 1)
                if u % 2 == 0 and u:
                    sum_y(c - 1)
            sum_y(NC - 1)
            pool.wait_ge(s["st_mm"], ONE + NU * G + NU)
            pool.wait_ge(s["sq_ready"], ONE + 2 * G + 2)
            step(nc.gpsimd.tensor_tensor(sum3[:, :, :], sq[:, 0:HP, :], sq[:, HP:NT, :], ALU.add))
            step.join()
            step(nc.gpsimd.tensor_tensor(row, sum3[:, 0, :], sum3[:, 1, :], ALU.add))
            step.join()
            step(nc.gpsimd.tensor_tensor(row, row, sum3[:, 2, :], ALU.add))
            step.join()
            pool.sem_inc(s["sum2_ready"], 1)
            if nxt:
                dt_pool(pool, G + 1, step)
                pool.wait_ge(s["e_mm"], ONE + 3 * NU * G + 3 * NU)
                diag_pool(pool, G + 1)

        POOL_BLK, POOL_END, POOL_PRO = 4 * NC + 3 + 2, 4 * NC + 3, 2
        POOL_ALL = POOL_PRO + POOL_BLK * (NB - 1) + POOL_END

        @block.gpsimd
        def _(pool):
            step = Steps(pool, s["steps_p"])
            begin(pool)
            pool.wait_ge(s["weights_loaded"], ONE + 16 * 7)
            with pool.Fori(0, B) as b:
                nc.gpsimd.memset(v_t[:, :, 96:97], 1.0)
                pool.wait_ge(s["ab_ready"], ONE + 2 * b + 1)
                own(pool)
                nc.gpsimd.tensor_scalar(xn[:, 2, :], xs_[:, 2, :], gn_ab[:, 2, 0:1], gn_ab[:, 2, 1:2], ALU.mult,
                                        ALU.add).then_inc(s["xn2_ready"], 1)
                meet(pool, b, 0)
                with pool.Fori(0, NB) as qb:
                    g = pool.snap(b * NB + qb)
                    for m in range(CT):
                        pool.wait_ge(s["proj_taken"], ONE + CT * g + m + 1)
                        xb = xs_[:, m, bass.ds(qb * TB, TB)]
                        nc.gpsimd.tensor_tensor(xb, xb, proj_y[:, m, :], ALU.add).then_inc(s["x1_added"], 1)
                meet(pool, b, 1)
                nc.gpsimd.memset(pre[:, :, :, :], 0.0).then_inc(s["top_clear"], 1)
                nc.gpsimd.memset(state[:, :, :], 0.0).then_inc(s["state_clear"], 1)
                pool.wait_ge(s["top_clear"], ONE + 2 * b + 1)
                pool.sem_inc(s["top_clear"], 1)
                meet(pool, b, 2)
                step.enter(b * POOL_ALL)
                pool.wait_ge(s["row0_done"], ONE + b + 1)
                carry_pool(pool, b * NB)
                dt_pool(pool, b * NB, step)
                assert step.n == POOL_PRO, step.n
                diag_pool(pool, b * NB)
                with pool.Fori(0, NB - 2) as i:
                    step.enter(pool.snap(b * POOL_ALL + i * POOL_BLK + POOL_PRO))
                    block_pool(pool, b, i, ROWS, step)
                    assert step.n == POOL_BLK, step.n
                step.enter(b * POOL_ALL + (NB - 2) * POOL_BLK + POOL_PRO)
                block_pool(pool, b, NB - 2, ROWS - 1, step)
                step.enter(b * POOL_ALL + (NB - 1) * POOL_BLK + POOL_PRO)
                block_pool(pool, b, NB - 1, 0, step)
                assert step.n == POOL_END, step.n
                meet(pool, b, 3)

        V = nc.vector

        def gn_dve(dve, n, step):
            own(dve)
            for t in range(CT):
                step(V.bn_aggr(chan_mv[:, t, :], chan_stats[:, t, :, :]))
            step.join()
            for t in range(CT):
                ins = V.scalar_tensor_tensor(chan_mv[:, t, 1:2], chan_mv[:, t, 0:1], chan_mv[:, t, 0:1],
                                             chan_mv[:, t, 1:2], ALU.mult, ALU.add)
            ins.then_inc(s["stats_ready"], 1)
            dve.wait_ge(s["group_sums"], ONE + n + 1)
            step(V.tensor_copy(group_mv[:], ps[0:GROUPS, 7, 0:2]))
            step.join()
            step(V.tensor_scalar(group_sc[:, 0:1], group_mv[:, 0:1], group_mv[:, 0:1], None, ALU.mult))
            step.join()
            V.tensor_tensor(group_sc[:, 1:2], group_mv[:, 1:2], group_sc[:, 0:1], ALU.subtract)\
                .then_inc(s["vars_ready"], 1)
            dve.wait_ge(s["roots_ready"], ONE + n + 1)
            step(V.reciprocal(group_sc[:, 2:3], group_sc[:, 1:2]))
            step.join()
            V.scalar_tensor_tensor(group_sc[:, 3:4], group_mv[:, 0:1], -1.0, group_sc[:, 2:3], ALU.mult, ALU.mult)\
                .then_inc(s["groups_ready"], 1)
            dve.wait_ge(s["group_back"], ONE + n + 1)
            V.tensor_copy(gn_ab[:], shaped(ps[:, 7, 8:8 + 2 * CT], CT, 2)).then_inc(s["ab_ready"], 1)
        GN_STEPS = CT + 3

        def max_dve(dve, g, n):
            dve.wait_ge(s["max_scores"], ONE + 32 * g + n + 1)
            V.tensor_reduce(maxes[:, n // NB, n % NB:n % NB + 1], ps[:, 2 + n % 2, :], AX.X, ALU.max)\
                .then_inc(s["max_read"], 1)

        def negmax_dve(dve, g, step):
            dve.wait_ge(s["max_read"], ONE + 32 * g + 32)
            step(V.tensor_reduce(max4[:], maxes[:], AX.X, ALU.max))
            step.join()
            dve.wait_ge(s["nm_turned"], ONE + g)
            V.tensor_scalar(negmax[:, :, QR:KS], max4[:].unsqueeze(2).broadcast_to([P, 4, 3]), -1.0, None, ALU.mult)\
                .then_inc(s["nm_ready"], 1)

        def split_max(dve, g, nq, step):
            r = slice(96, 99)
            dve.wait_ge(s["nm_taken"], ONE + g + 1)
            step(V.scalar_tensor_tensor(nm_f[r, :], nm_h[r, :], mask(0, r), nm_f[r, :], ALU.mult, ALU.add))
            step.join()
            step(V.tensor_copy(nm_m[r, :], nm_f[r, :]))
            step.join()
            V.scalar_tensor_tensor(q_st[r, bass.ds(nq * TB, TB)], nm_m[r, :], mask(1, r), nm_f[r, :], ALU.mult,
                                   ALU.add).then_inc(s["nm_stacked"], 1)

        def recip_dve(dve, g, qb):
            dve.wait_ge(s["pv_done"], ONE + KT * (g + 1))
            V.reciprocal(rec[96:97, :], ps[96:97, bass.ds(out_bank(qb), 1), :].rearrange("p a n -> p (a n)"))\
                .then_inc(s["recip_ready"], 1)

        def norm_dve(dve, g, qb):
            dve.wait_ge(s["recip_copied"], ONE + g + 1)
            V.scalar_tensor_tensor(cat[0:PD, 0, :],
                                   ps[0:PD, bass.ds(out_bank(qb), 1), :].rearrange("p a n -> p (a n)"), 0.0,
                                   rec_b[0:PD, :], ALU.max, ALU.mult).then_inc(s["normed"], 1)

        def stats_dve(dve, g, qb, m, step):
            dve.wait_ge(s["x1_added"], ONE + CT * g + m + 1)
            step(V.bn_stats(chan_stats[:, m, bass.ds(qb, 1), :], xs_[:, m, bass.ds(qb * TB, TB)]))

        STATS_AT = (20, 23, 26)

        def attend_dve(dve, b, qb, has_prev, has_next, step):
            g = b * NB + qb if isinstance(qb, int) else dve.snap(b * NB + qb)
            if has_prev:
                recip_dve(dve, g - 1, qb - 1)
            for n in range(KT):
                if has_next:
                    max_dve(dve, g + 1, n)
                if has_prev and n == 0:
                    norm_dve(dve, g - 1, qb - 1)
                if has_prev and n in STATS_AT:
                    stats_dve(dve, g - 1, qb - 1, STATS_AT.index(n), step)
            if has_next:
                negmax_dve(dve, g + 1, step)
                split_max(dve, g + 1, qb + 1, step)

        def conv_dve(dve, G1, lo, hi, step):
            for j, k in CONV[lo:hi]:
                t, last, alone = ORDER[j], k == len(TAPS) - 1, j >= 4
                if k == 0:
                    dve.wait_ge(s["centre_done"], ONE + XT_ * G1 + j + 1)
                else:
                    step.join(0 if alone or (last and j % 2 == 1) else 1)
                dy, dx = TAPS[k] // 3, TAPS[k] % 3
                a = shaped(acc[:, t, :], ROWS, W)
                ins = V.scalar_tensor_tensor(a, pre[:, t, dy:dy + ROWS, dx:dx + W],
                                             vec[:, V_CW + 9 * t + TAPS[k]:V_CW + 9 * t + TAPS[k] + 1], a, ALU.mult,
                                             ALU.add)
                if last:
                    ins.then_inc(s["conv_done"], 1)
                else:
                    step(ins)

        def dt_dve(dve, G1, step, between=None):
            r = slice(0, R3)
            dve.wait_ge(s["sp_ln"], ONE + 2 * G1 + 1)
            step(V.tensor_scalar(sp_d[r, :], sp_e[r, :], 1.0, -1.0, ALU.add, ALU.add))
            step.join()
            V.tensor_scalar(sp_r[r, :], sp_d[r, :], 0.0, None, ALU.is_equal).then_inc(s["sp_zero"], 1)
            if between:
                between()
            dve.wait_ge(s["sp_prod"], ONE + G1 + 1)
            step(V.reciprocal(sp_r[r, :], sp_d[r, :]))
            step.join()
            step(V.tensor_tensor(sp_d[r, :], sp_l[r, :], sp_r[r, :], ALU.mult))
            step.join()
            dve.wait_ge(s["small_mm"], ONE + NC * G1)
            dve.wait_ge(s["dt_relu"], ONE + G1 + 1)
            V.tensor_tensor(dt_sb[r, :], sp_d[r, :], cs[r, :], ALU.add).then_inc(s["dt_ready"], 1)
            dve.wait_ge(s["dt_ready"], ONE + G1 + 1)
            step(V.tensor_scalar(sp_r[r, :], dt_sb[r, :], a_neg[r, :], None, ALU.mult))
            step.join()
            for c in range(NC):
                tok = slice(c * CH, (c + 1) * CH)
                step(V.tensor_tensor_scan(cs[r, tok], one[r, 0:CH], sp_r[r, tok], 0.0, ALU.mult, ALU.add))
            step.join()
            step(V.tensor_copy(cs_h[r, :], cs[r, :]))
            step.join()
            step(V.scalar_tensor_tensor(cs[r, :], cs_h[r, :], mask(4, r), cs[r, :], ALU.mult, ALU.add))
            step.join()
            step(V.tensor_copy(cs_h[r, :], cs[r, :]))
            step.join()
            dve.wait_ge(s["diag_ready"], ONE + NC * G1)
            V.scalar_tensor_tensor(cs_st[r, :], cs_h[r, :], mask(5, r), cs[r, :], ALU.mult, ALU.add)\
                .then_inc(s["cs_stacked"], 1)
            dve.wait_ge(s["cs_stacked"], ONE + G1 + 1)
            dve.wait_ge(s["e_mm"], ONE + 3 * NU * G1)
            for par in range(2):
                ins = V.tensor_scalar(cs_neg[r, par, :], cs_st[r, :], mask(6 + par, r), None, ALU.mult)
            ins.then_inc(s["cs_negated"], 1)
        DT_STEPS = 11

        def unit_a_dve(dve, G, u):
            c, hf, d = u // 2, u % 2, u % 2
            dve.wait_ge(s["xt_mm"], ONE + NU * G + u + 1)
            dve.wait_ge(s["small_copied"], ONE + NC * G + c + 1)
            for name in ("y_mm", "xw_ready"):
                dve.wait_ge(s[name], ONE + NU * G + max(u - 1, 0))
            if u == 0:
                dve.wait_ge(s["sum2_ready"], ONE + G)
            heads = slice(P + NS + 2 * HP * hf, P + NS + 2 * HP * (hf + 1))
            V.tensor_tensor(x_dt[:, d, :, :, :].rearrange("p a b c -> p (a b) c"),
                            shaped(ps[:, 4, 0:HP * P], 2 * HP, HD),
                            small[:, c % 2, heads].unsqueeze(2).broadcast_to([P, 2 * HP, HD]), ALU.mult)\
                .then_inc(s["xdt_ready"], 1)
            dve.wait_ge(s["exp_done"], ONE + 3 * NU * G + 3 * u + 2)
            V.tensor_tensor(att[:, d, :, :, :].rearrange("p a b c -> p (a b) c"),
                            decay[:, d, :, :, :].rearrange("p a b c -> p (a b) c"),
                            small[:, c % 2, 0:P].unsqueeze(1).broadcast_to([P, 2 * HP, CH]), ALU.mult)\
                .then_inc(s["att_ready"], 1)

        def unit_b_dve(dve, G, u):
            c, hf, d = u // 2, u % 2, u % 2
            tok = slice(c * CH, (c + 1) * CH)
            dve.wait_ge(s["y_mm"], ONE + NU * G + u + 1)
            for t in range(HP):
                T = HP * hf + t
                ins = V.scalar_tensor_tensor(y_sb[:, T, tok], xbc[:, T, tok], vec[:, V_D + T:V_D + T + 1],
                                             ps[:, 6, t * CH:(t + 1) * CH], ALU.mult, ALU.add)
            ins.then_inc(s["y_read"], 1)
            dve.wait_ge(s["st_mm"], ONE + NU * G + u + 1)
            dve.wait_ge(s["sdec_ready"], ONE + NU * G + u + 1)
            for par in range(2):
                rr = slice(64 * par, 64 * par + 64)
                ins = V.tensor_tensor(state[rr, HP * hf:HP * hf + HP, rr], shaped(ps[rr, 7, 0:HP * HD], HP, HD),
                                      st_dec[rr, :, rr], ALU.add)
            ins.then_inc(s["state_done"], 1)

        CONV_AT = [0, 0, 0, 5, 10, 15, 21, 27, 32]
        CONV_MID = 40

        def block_dve(dve, b, i, nxt, step):
            G = b * NB + i if isinstance(i, int) else dve.snap(b * NB + i)
            dve.wait_ge(s["pj_mm"], ONE + b * ALL + i * PER)
            if nxt == ROWS - 1:
                dve.wait_ge(s["bottom_clear"], ONE + b + 1)
            for u in range(NU):
                unit_a_dve(dve, G, u)
                if u:
                    unit_b_dve(dve, G, u - 1)
                if nxt:
                    conv_dve(dve, G + 1, CONV_AT[u], CONV_AT[u + 1], step)
            unit_b_dve(dve, G, NU - 1)
            at0 = item("m1", nxt)
            pj = b * ALL + i * PER
            dve.wait_ge(s["pj_mm"], ONE + pj + at0 + 1)
            for half in range(2):
                h3 = slice(HP * half, HP * half + HP)
                V.tensor_tensor(y_sb[:, h3, :], y_sb[:, h3, :],
                                ps[:, at0 % 2:at0 % 2 + 1, :].broadcast_to([P, HP, TB]), ALU.subtract)\
                    .then_inc(s["y_centred"], 1)
            dve.wait_ge(s["y_centred"], ONE + 2 * G + 2)
            dve.sem_inc(s[f"pj_read{at0 % 2}"], 1)
            if nxt:
                conv_dve(dve, G + 1, CONV_AT[NU], CONV_MID, step)
            at0 = item("m2", nxt)
            dve.wait_ge(s[f"pj_read{at0 % 2}"], ONE + b * (ALL // 2) + i * (PER // 2) + at0 // 2 + 1)
            V.reciprocal(row, row).then_inc(s["row_root"], 1)
            dve.wait_ge(s["row_root"], ONE + G + 1)
            dve.wait_ge(s["sq_ready"], ONE + 2 * G + 2)
            for half in range(2):
                h3 = slice(HP * half, HP * half + HP)
                V.tensor_tensor(y_sb[:, h3, :], y_sb[:, h3, :], row.unsqueeze(1).broadcast_to([P, HP, TB]),
                                ALU.mult).then_inc(s["y_scaled"], 1)
            for t in range(NT):
                dve.wait_ge(s["y_affine"], ONE + NT * G + t + 1)
                z_at = item(f"z{t}", nxt)
                dve.wait_ge(s[f"pj_read{z_at % 2}"], ONE + b * (ALL // 2) + i * (PER // 2) + z_at // 2 + 1)
                V.tensor_tensor(y_sb[:, t, :], y_sb[:, t, :], xbc[:, t, :], ALU.mult).then_inc(s["gated"], 1)

            def residual(m):
                at0 = item(f"o{m}", nxt)
                dve.wait_ge(s["pj_mm"], ONE + pj + at0 + 1)
                xb = xs_[:, m, bass.ds(i * TB, TB)]
                V.tensor_tensor(xb, ps[:, at0 % 2, :], xb, ALU.add).then_inc(s["out_read"], 1)
                dve.wait_ge(s["out_read"], ONE + CT * G + m + 1)
                dve.sem_inc(s[f"pj_read{at0 % 2}"], 1)

            def between():
                conv_dve(dve, G + 1, CONV_MID, 44, step)
                residual(0)

            if nxt:
                dt_dve(dve, G + 1, step, between)
                residual(1)
                conv_dve(dve, G + 1, 44, 52, step)
                residual(2)
                conv_dve(dve, G + 1, 52, len(CONV), step)
            else:
                for m in range(CT):
                    residual(m)

        QKV_STEPS = 6
        ATT_FIRST, ATT_STEPS, ATT_LAST = 3, 6, 6
        BLK_STEPS = 7 * XT_ + DT_STEPS
        V_GN0 = 24 + GN_STEPS
        V_QKV = V_GN0 + QKV_STEPS * (NB // 2)
        V_MAX0 = V_QKV + 3
        V_ATT = V_MAX0 + ATT_FIRST + ATT_STEPS * (NB - 2) + ATT_LAST
        V_GN1 = V_ATT + GN_STEPS
        V_SSD = V_GN1 + BLK_STEPS
        V_ALL = V_SSD + BLK_STEPS * (NB - 1)

        @block.vector
        def _(dve):
            step = Steps(dve, s["steps_v"])
            begin(dve)
            dve.wait_ge(s["weights_loaded"], ONE + 16 * 7)
            dve.wait_ge(s["prepared"], ONE + 3)
            b1 = shaped(vec[0:PD, V_BN1:V_BN1 + 12], 4, 3)
            b2 = shaped(vec[:, V_BN2:V_BN2 + 12], 4, 3)
            for v, sc, of in ((b1, bn1s, bn1o), (b2, bn2s, bn2o)):
                step(V.reciprocal(of[:], sc[:]))
                step.join()
                step(V.tensor_tensor(sc[:], v[:, 0, :], of[:], ALU.mult))
                step.join()
                step(V.tensor_tensor(of[:], v[:, 2, :], sc[:], ALU.mult))
                step.join()
                step(V.tensor_tensor(of[:], v[:, 1, :], of[:], ALU.subtract))
                step.join()
            V_PRE = step.n
            V.memset(rec[96:97, 0:1], 0.0).then_inc(s["vec_prepared"], 1)
            with dve.Fori(0, B) as b:
                base = dve.snap(b * V_ALL + V_PRE)
                step.enter(base)
                V.memset(k_st[96:99, :], 1.0)
                for t in range(CT):
                    dve.wait_ge(s[f"x_loaded{t}"], ONE + 16 * b + 16)
                    for k in range(NB):
                        step(V.bn_stats(chan_stats[:, t, k, :], xs_[:, t, k * TB:(k + 1) * TB]))
                step.join()
                gn_dve(dve, 2 * b, step)
                assert step.n == V_GN0
                dve.wait_ge(s["ab_ready"], ONE + 2 * b + 1)
                V.tensor_scalar(xn[:, 1, :], xs_[:, 1, :], gn_ab[:, 1, 0:1], gn_ab[:, 1, 1:2], ALU.mult, ALU.add)\
                    .then_inc(s["xn1_ready"], 1)
                with dve.Fori(0, NB // 2) as u:
                    step.enter(dve.snap(b * V_ALL + u * QKV_STEPS + (V_PRE + V_GN0)))
                    G = dve.snap(b * (NB // 2) + u)
                    dve.wait_ge(s["xn0_ready"], ONE + b + 1)
                    for j in range(2):
                        dve.wait_ge(s["mean_ready"], ONE + 2 * G + j + 1)
                        dve.wait_ge(s["ln_ready"], ONE + 2 * G)
                        V.tensor_tensor(ln_x[0:PD, j, :], xn[0:PD, 0, bass.ds(u * (2 * TB) + j * TB, TB)],
                                        ps[0:PD, j, :], ALU.subtract).then_inc(s["centred"], 1)
                    for j in range(2):
                        dve.wait_ge(s["ln_root"], ONE + 2 * G + j + 1)
                        dve.wait_ge(s["centred"], ONE + 2 * G + j + 1)
                        step(V.reciprocal(ln_sq[0:PD, j, :], ln_sq[0:PD, j, :]))
                        step.join()
                        V.tensor_tensor(ln_x[0:PD, j, :], ln_x[0:PD, j, :], ln_sq[0:PD, j, :], ALU.mult)\
                            .then_inc(s["scaled"], 1)
                    for w, name in ((0, "q_stacked"), (1, "k_stacked")):
                        st = (q_st, k_st)[w]
                        dve.wait_ge(s["qk_taken"], ONE + 4 * G + 4)
                        f, h, m = (v[0:PD, w, :, :] for v in (qk_f, qk_h, qk_m))
                        step(V.scalar_tensor_tensor(f, h, mask(2 * w, slice(0, PD)), f, ALU.mult, ALU.add))
                        step.join()
                        step(V.tensor_copy(m, f))
                        step.join()
                        V.scalar_tensor_tensor(st[0:PD, bass.ds(u * (2 * TB), 2 * TB)],
                                               m.rearrange("p a b -> p (a b)"), mask(2 * w + 1, slice(0, PD)),
                                               f.rearrange("p a b -> p (a b)"), ALU.mult, ALU.add)\
                            .then_inc(s[name], 2)
                    for j in range(2):
                        dve.wait_ge(s["vt_ready"], ONE + 2 * G + j + 1)
                        V.tensor_copy(v_t[:, bass.ds(u * 8 + j * 4, 4), 0:PD], shaped(ps[:, 2 + j, 0:4 * PD], 4, PD))\
                            .then_inc(s["vt_copied"], 1)
                    assert step.n == QKV_STEPS, step.n
                meet(dve, b, 0)
                step.enter(dve.snap(b * V_ALL + (V_PRE + V_QKV)))
                for n in range(32):
                    max_dve(dve, b * NB, n)
                V.memset(negmax[:], 0.0).then_inc(s["cleared"], 1)
                dve.wait_ge(s["cleared"], ONE + b + 1)
                negmax_dve(dve, b * NB, step)
                split_max(dve, b * NB, 0, step)
                assert step.n == 3
                attend_dve(dve, b, 0, False, True, step)
                assert step.n == 3 + ATT_FIRST
                with dve.Fori(1, NB - 1) as qb:
                    step.enter(dve.snap(b * V_ALL + qb * ATT_STEPS + (V_PRE + V_MAX0 + ATT_FIRST - ATT_STEPS)))
                    attend_dve(dve, b, qb, True, True, step)
                    assert step.n == ATT_STEPS
                step.enter(dve.snap(b * V_ALL + (V_PRE + V_MAX0 + ATT_FIRST + ATT_STEPS * (NB - 2))))
                attend_dve(dve, b, NB - 1, True, False, step)
                recip_dve(dve, b * NB + (NB - 1), NB - 1)
                norm_dve(dve, b * NB + (NB - 1), NB - 1)
                for m in range(CT):
                    stats_dve(dve, b * NB + (NB - 1), NB - 1, m, step)
                assert step.n == ATT_LAST
                step.join()
                meet(dve, b, 1)
                step.enter(dve.snap(b * V_ALL + (V_PRE + V_ATT)))
                gn_dve(dve, 2 * b + 1, step)
                dve.wait_ge(s["beta_mm"], ONE + b + 1)
                dve.wait_ge(s["ab_ready"], ONE + 2 * b + 2)
                V.tensor_copy(beta[:, 0:XT_ + NT], ps[:, 6, 0:XT_ + NT])
                V.tensor_tensor(beta[0:R3, XT_ + NT:XT_ + NT + 1], ps[0:R3, 6, XT_ + NT:XT_ + NT + 1],
                                vec[0:R3, V_DTB:V_DTB + 1], ALU.add)
                for k in range(CT):
                    V.tensor_scalar(w_in[:, k, :], w_in[:, k, :], gn_ab[:, k, 0:1], None, ALU.mult)
                    V.tensor_scalar(w_dt[:, k, :], w_dt_raw[:, k, :], gn_ab[:, k, 0:1], None, ALU.mult)
                meet(dve, b, 2)
                step.enter(dve.snap(b * V_ALL + (V_PRE + V_GN1)))
                dt_dve(dve, b * NB, step)
                conv_dve(dve, b * NB, 0, len(CONV), step)
                assert step.n == BLK_STEPS, step.n
                with dve.Fori(0, NB - 2) as i:
                    step.enter(dve.snap(b * V_ALL + i * BLK_STEPS + (V_PRE + V_SSD)))
                    block_dve(dve, b, i, ROWS, step)
                    assert step.n == BLK_STEPS, step.n
                step.enter(dve.snap(b * V_ALL + (V_PRE + V_SSD + (NB - 2) * BLK_STEPS)))
                block_dve(dve, b, NB - 2, ROWS - 1, step)
                step.enter(dve.snap(b * V_ALL + (V_PRE + V_SSD + (NB - 1) * BLK_STEPS)))
                block_dve(dve, b, NB - 1, 0, step)
                meet(dve, b, 3)


def lay_out(i):
    f = {k: np.asarray(v) for k, v in i.items()}
    x = np.ascontiguousarray(f["x"].reshape(B, C, L))
    g = lambda n: f["L0_conv_" + n]
    m = lambda n: f["L1_conv_" + n]
    qkv = g("w_qkv")
    wq, wk, wv = qkv[:QK], qkv[QK:2 * QK], qkv[2 * QK:]
    rep = lambda a: np.concatenate([a] * QG, 0)
    wqkv = np.stack([rep(wq).T, rep(wk).T, wv.T], 1)
    vecs = np.zeros((P, NV), np.float32)
    for n, name in enumerate(("bn1_g", "bn1_b", "bn1_m", "bn1_v")):
        v = g(name)
        for k, part in enumerate((rep(v[:QK]), rep(v[QK:2 * QK]), v[2 * QK:])):
            vecs[:PD, V_BN1 + 3 * n + k] = part
    vecs[:PD, V_LN], vecs[:PD, V_LN + 1] = g("ln_w"), g("ln_b")
    tiles = lambda v: v.reshape(-1, P).T
    for n, name in enumerate(("bn2_g", "bn2_b", "bn2_m", "bn2_v")):
        vecs[:, V_BN2 + 3 * n:V_BN2 + 3 * n + 3] = tiles(g(name))
    cw = m("conv_w").reshape(XT_, P, 9)
    vecs[:, V_CW:V_CW + 63] = cw.transpose(1, 0, 2).reshape(P, 63)
    vecs[:, V_CB:V_CB + XT_] = tiles(m("conv_b"))
    vecs[:, V_NW:V_NW + NT], vecs[:, V_NB:V_NB + NT] = tiles(m("norm_w")), tiles(m("norm_b"))
    vecs[:, V_D:V_D + NT] = tiles(np.repeat(m("D"), HD))
    w = m("in_proj_w")
    wdt = np.zeros((R3, C), np.float32)
    for part in range(3):
        r = slice(32 * part, 32 * part + NH)
        vecs[r, V_DTB], vecs[r, V_AL] = m("dt_bias"), m("A_log")
        wdt[r] = w[DIN:]
    kmajor = lambda a: np.ascontiguousarray(a.T.reshape(-1, P, a.shape[0]).transpose(1, 0, 2))
    consts, constb = constants()
    return {"x": x, "vecs": vecs, "wqkv": np.ascontiguousarray(wqkv), "wproj": kmajor(g("w_proj")),
            "win": kmajor(w[:DIN]), "wdt": kmajor(wdt), "wout": kmajor(m("out_proj_w")),
            "consts": consts, "constb": constb}


def kernel(**inputs):
    import concourse.bacc as bacc
    from concourse.bass_utils import run_bass_kernel_spmd

    nc = bacc.Bacc("TRN2", target_bir_lowering=False, num_devices=1)
    arrays = lay_out(inputs)
    args = [nc.dram_tensor(n, a.shape, mybir.dt.from_np(a.dtype), kind="ExternalInput").ap()
            for n, a in arrays.items()]
    args.append(nc.dram_tensor("out", (B, C, L), F32, kind="ExternalOutput").ap())
    program(nc, *args)
    r = run_bass_kernel_spmd(nc, [arrays], core_ids=[0])
    return r.results[0]["out"].reshape(B, C, H, W)
```

```python
from contextlib import ExitStack

import concourse.bass as bass
import concourse.mybir as mybir
import numpy as np

F32 = mybir.dt.float32
BF16 = mybir.dt.bfloat16
ALU = mybir.AluOpType
ACT = mybir.ActivationFunctionType
AX = mybir.AxisListType

B, C, H, W = 4, 384, 64, 64
L = H * W
P = 128
CT = C // P
TB = 512
NB = L // TB
ROWS = TB // W
WP = W + 2
GROUPS = 32
PD, QK = 96, 16
DI = 768
NT = DI // P
NS = 64
HD = 64
NH = DI // HD
XT_ = (DI + 2 * NS) // P
DIN = 2 * DI + 2 * NS
CH = 128
NC = TB // CH
HP = NT // 2
NU = 2 * NC
HALF = TB // 2
PART = 32
COPY = 16
R3 = 2 * PART + COPY + NH
QG = 6
QR = QG * QK
KS = QR + 3
QPART = (0, 0, 1, 1, 0, 2)
KPART = (0, 1, 0, 1, 2, 0)
NEG = -1e30
ORDER = (XT_ - 1, *range(XT_ - 1))
TAPS = (0, 1, 2, 3, 5, 6, 7, 8)
CONV = [(j, k) for js in ((0, 1), (2, 3), (4,), (5,)) for k in range(len(TAPS)) for j in js]
VT = XT_ - 1

V_BN1, V_LN, V_BN2, V_CW, V_CB, V_NW, V_NB, V_D, V_DTB, V_AL = 0, 12, 14, 26, 89, 96, 102, 108, 114, 115
NV = 116
K_ID, K_ONE, K_M768, K_M96, K_G, K_GT, K_MASK = 0, 128, 256, 384, 480, 576, 960
K_EPS = K_MASK + 12
NK = K_EPS + 1
B_ID, B_BIG, B_DELTA, B_SEL = 0, 128, 512, 1280
NBF = 1408


def constants():
    k = np.zeros((P, NK), np.float32)
    k[:, K_ID:K_ID + P] = np.eye(P)
    k[:, K_ONE:K_ONE + P] = 1
    k[:, K_M768:K_M768 + P] = 1 / DI
    k[:, K_M96:K_M96 + PD] = 1 / PD
    k[:, K_EPS] = 1e-5
    per = C // GROUPS
    for t in range(CT):
        for p in range(P):
            g = (t * P + p) // per
            k[p, K_G + t * GROUPS + g] = 1 / per
            k[g, K_GT + t * P + p] = 1
    for r in range(QR + 3):
        q = QPART[r // QK] if r < QR else r - QR
        kk = KPART[r // QK] if r < QR else 0
        k[r, K_MASK + 0], k[r, K_MASK + 1] = -(q > 0), -(q == 2)
        k[r, K_MASK + 2], k[r, K_MASK + 3] = -(kk > 0), -(kk == 2)
    bf = np.zeros((P, NBF), np.float32)
    bf[:, B_ID:B_ID + P] = np.eye(P)
    j, i = np.arange(P)[:, None], np.arange(CH)[None, :]
    bf[:, B_BIG:B_BIG + HP * CH] = np.tile(np.where(j > i, NEG, 0), (1, HP))
    for part in range(3):
        for h in range(NH):
            first = PART * part + h
            again = first + COPY
            for r in (first, again):
                k[r, K_MASK + 4], k[r, K_MASK + 5] = -(part > 0), -(part == 2)
                bf[r, B_DELTA + (h // 2) * CH:B_DELTA + (h // 2 + 1) * CH] = 1
            k[again, K_MASK + 6 + h % 2] = -1
            k[first, K_MASK + 8 + h % 2] = 1
            k[first, K_MASK + 10] = 1
            k[again, K_MASK + 11] = 1
            bf[first, B_SEL + (h % 2) * 64:B_SEL + (h % 2 + 1) * 64] = 1
    return k, bf.astype(mybir.dt.np(BF16))


ONE = 1


class Steps:

    def __init__(self, eng, sem):
        self.eng, self.sem, self.base, self.n = eng, sem, 0, 0

    def enter(self, base):
        self.base, self.n = base, 0

    def __call__(self, ins):
        ins.then_inc(self.sem, 1)
        self.n += 1

    def join(self, but=0):
        self.eng.wait_ge(self.sem, self.base + (self.n - but + ONE))


def program(nc, x, vecs, wqkv, wproj, win, wdt, wout, consts, constb, out):
    ctx = ExitStack()
    with ctx:
        def sb(name, shape, dt=F32):
            return ctx.enter_context(nc.sbuf_tensor(name, shape, dt))

        def sem(name):
            return ctx.enter_context(nc.semaphore(name))

        xs_ = sb("x_sample", [P, CT, L])
        w_in = sb("w_in", [P, CT, DIN])
        w_out = sb("w_out", [P, NT, C])
        w_proj = sb("w_proj", [P, CT, C])
        w_dt_raw = sb("w_dt_raw", [P, CT, R3])
        w_dt = sb("w_dt", [P, CT, R3])
        w_qkv = sb("w_qkv", [PD, 3, PD])
        vec = sb("vec", [P, NV])
        kf = sb("kf", [P, NK])
        kb = sb("kb", [P, NBF], BF16)
        bn1s, bn1o = sb("bn1s", [PD, 3]), sb("bn1o", [PD, 3])
        bn2s, bn2o = sb("bn2s", [P, CT]), sb("bn2o", [P, CT])
        a_neg = sb("a_neg", [R3, 1])
        chan_stats = sb("chan_stats", [P, CT, NB, 6])
        chan_mv = sb("chan_mv", [P, CT, 2])
        group_mv = sb("group_mv", [GROUPS, 2])
        group_sc = sb("group_sc", [GROUPS, 4])
        gn_ab = sb("gn_ab", [P, CT, 2])
        beta = sb("beta", [P, XT_ + NT + 1])
        maxes = sb("maxes", [P, 4, 8])
        max4 = sb("max4", [P, 4])
        ident, one, mean768 = kf[:, K_ID:K_ID + P], kf[:, K_ONE:K_ONE + P], kf[:, K_M768:K_M768 + P]
        mean96 = kf[0:PD, K_M96:K_M96 + PD]

        def eps(rows=slice(0, P)):
            return kf[rows, K_EPS:K_EPS + 1]

        def mask(n, rows):
            return kf[rows, K_MASK + n:K_MASK + n + 1]

        AR = 29424
        arena = sb("arena", [P, AR])
        at = [0]

        def take(cols, dt=F32, rows=slice(0, P)):
            words = cols if dt == F32 else cols // 2
            v = arena[rows, at[0]:at[0] + words]
            at[0] += words
            assert at[0] <= AR, at[0]
            return v if dt == F32 else v.bitcast(dt)

        def shaped(v, *dims):
            names = "abcd"[:len(dims)]
            return v.rearrange(f"p ({' '.join(names)}) -> p {' '.join(names)}", **dict(zip(names, dims)))

        xn = shaped(take(CT * L), CT, L)
        q_st, k_st = take(L, BF16), take(L, BF16)
        v_t = shaped(take(32 * 97), 32, 97)
        common = at[0]
        ln_x = shaped(take(2 * TB), 2, TB)
        ln_sq = shaped(take(2 * TB), 2, TB)
        ln_y = shaped(take(2 * TB), 2, TB)
        qk_f = shaped(take(4 * TB), 2, 2, TB)
        qk_h = shaped(take(4 * TB, BF16), 2, 2, TB)
        qk_m = shaped(take(4 * TB, BF16), 2, 2, TB)
        v_sb = shaped(take(2 * TB), 2, TB)
        at[0] = common
        p_sb = shaped(take(4 * TB), 4, TB)
        cat = shaped(take(CT * TB), CT, TB)
        rec_b = take(TB)
        rec = take(TB)
        proj_y = shaped(take(CT * TB), CT, TB)
        negmax = shaped(take(4 * KS), 4, KS)
        nm_f, nm_h, nm_m = take(TB), take(TB, BF16), take(TB, BF16)
        at[0] = 0
        pre = shaped(take(XT_ * (ROWS + 2) * WP), XT_, ROWS + 2, WP)
        acc = shaped(take(XT_ * TB), XT_, TB)
        xbc = shaped(take(XT_ * TB), XT_, TB)
        y_sb = shaped(take(NT * TB), NT, TB)
        both = take(4 * HP * CH * 2)
        decay = shaped(both[:, 0:4 * HP * CH], 2, 2, HP, CH)
        att = shaped(both[:, 4 * HP * CH:], 2, 2, HP, CH)
        sq = shaped(both, NT, TB)
        grow = shaped(take(2 * HP * CH), 2, HP, CH)
        c_dec = shaped(take(2 * HP * CH), 2, HP, CH)
        both_x = take(2 * 2 * 2 * HP * HD)
        x_dt = shaped(both_x[:, 0:4 * HP * HD], 2, HP, 2, HD)
        x_w = shaped(both_x[:, 4 * HP * HD:], 2, HP, 2, HD)
        sum3 = shaped(both_x, HP, TB)
        tap_prod = [both[:, n:n + TB] for n in (2 * HP * CH, 6 * HP * CH)]
        c_dup = take(TB)
        state = shaped(take(NT * P), NT, P)
        st_dec = shaped(take(HP * P), HP, P)
        small = shaped(take(2 * (P + NS)), 2, P + NS)
        dt_t = take(NC * NH)
        cs_diag = shaped(take(NT * TB, BF16), NT, TB)
        cs_neg = shaped(take(2 * TB, BF16), 2, TB)
        sp_e, sp_l, sp_d, sp_r, dt_sb, cs = (take(TB) for _ in range(6))
        cs_st, cs_h = take(TB, BF16), take(TB, BF16)
        row = take(TB)

        ps = ctx.enter_context(nc.psum_tensor("ps", [P, 8, TB], F32))

        names = """
        weights_loaded waited steps_v steps_a steps_p prepared vec_prepared met_v met
        x_loaded0 x_loaded1 x_loaded2 win_loaded stored stats_ready group_sums groups_ready group_back ab_ready
        vars_ready roots_ready ln_root row_root xn0_ready xn1_ready xn2_ready cleared
        mean_ready centred squared var_ready scaled ln_ready q_ready k_ready v_ready q_taken k_taken
        v_taken vt_ready vt_copied q_stacked k_stacked
        max_scores max_read nm_ready nm_turned nm_taken nm_stacked
        scores exps pv_done recip_ready recip_spread recip_copied normed skip_relu proj_mm proj_taken x1_added
        beta_mm beta_ready w_scaled row0_mm row0_done row0_carried top_clear bottom_clear state_clear
        pj_mm pj_read0 pj_read1 centre_done conv_done tap_ready tap_added silu_done carried bc_dup
        small_mm small_copied xt_mm xdt_ready e_mm exp_done xw_ready cd_ready sdec_ready att_ready
        y_mm y_read st_mm state_done
        dt_abs sp_exp sp_ln sp_zero sp_prod sp_recip dt_ready cs_rounded cs_stacked cs_negated diag_ready
        sum1_ready y_centred sq_ready sum2_ready y_scaled y_affine z_copied gated out_read
        """.split()
        s = {n: sem(n) for n in names}

        started = sem("started")
        block = ctx.enter_context(nc.Block())
        MEETS = 3

        def own(eng):
            eng.sem_inc(s["waited"], 1)

        def meet(eng, b, n):
            own(eng)
            eng.drain().then_inc(s["met"], 1)
            eng.wait_ge(s["met"], ONE + 5 * (MEETS * b + n + 1))
            own(eng)

        def begin(eng):
            eng.wait_ge(started, 1)

        @block.sync
        def _(sp):
            for first in s.values():
                sp.sem_inc(first, ONE)
            sp.sem_inc(started, 1)
            for dst, src in ((vec, vecs), (kf, consts), (kb, constb), (w_qkv, wqkv), (w_proj, wproj),
                             (w_dt_raw, wdt), (w_out, wout)):
                sp.dma_start(dst[:], src[:]).then_inc(s["weights_loaded"], 16)
            with sp.Fori(0, B) as b:
                sp.wait_ge(s["stored"], ONE + b * (16 * CT * NB))
                own(sp)
                for t in range(CT):
                    src = x.rearrange("b (t p) l -> (b t) p l", p=P)
                    sp.dma_start(xs_[:, t, :], src[b * CT + t]).then_inc(s[f"x_loaded{t}"], 16)
                sp.dma_start(w_in[:], win[:]).then_inc(s["win_loaded"], 16)
                for n in range(MEETS - 1):
                    meet(sp, b, n)

                def repeat_c(G):
                    sp.wait_ge(s["cd_ready"], ONE + NU * G)
                    own(sp)
                    sp.wait_ge(s["small_mm"], ONE + NC * G)
                    own(sp)
                    sp.wait_ge(s["silu_done"], ONE + G * XT_ + 1)
                    for half in range(2):
                        sp.dma_start(c_dup[64 * half:64 * half + 64, :], xbc[64:128, XT_ - 1, :]).then_inc(s["bc_dup"], 16)

                def store(G, i):
                    for m in range(CT):
                        sp.wait_ge(s["out_read"], ONE + G * CT + m + 1)
                        own(sp)
                        dst = out.rearrange("b (t p) l -> (b t) p l", p=P)
                        sp.dma_start(dst[b * CT + m, :, bass.ds(i * TB, TB)],
                                     xs_[:, m, bass.ds(i * TB, TB)]).then_inc(s["stored"], 16)

                repeat_c(sp.snap(b * NB))
                with sp.Fori(0, NB - 1) as i:
                    G = sp.snap(b * NB + i)
                    repeat_c(sp.snap(G + 1))
                    store(G, i)
                store(b * NB + (NB - 1), NB - 1)
                meet(sp, b, MEETS - 1)
            sp.wait_ge(s["stored"], ONE + 16 * B * CT * NB)

        def gn_pe(pe, n):
            pe.wait_ge(s["stats_ready"], ONE + n + 1)
            for t in range(CT):
                mm = nc.tensor.matmul(ps[0:GROUPS, 7, 0:2], kf[:, K_G + t * GROUPS:K_G + (t + 1) * GROUPS],
                                      chan_mv[:, t, :], start=(t == 0), stop=(t == CT - 1))
            mm.then_inc(s["group_sums"], 1)
            pe.wait_ge(s["groups_ready"], ONE + n + 1)
            for t in range(CT):
                mm = nc.tensor.matmul(ps[:, 7, 8 + 2 * t:10 + 2 * t], kf[0:GROUPS, K_GT + t * P:K_GT + (t + 1) * P],
                                      group_sc[:, 2:4], start=True, stop=True)
            mm.then_inc(s["group_back"], 1)

        QP = NB // 2

        def qkv_pe(pe, b, u, has_prev):
            G = b * QP + u if isinstance(u, int) else pe.snap(b * QP + u)
            for j in range(2):
                pe.wait_ge(s["v_taken"], ONE + 2 * G)
                nc.tensor.matmul(ps[0:PD, j, :], mean96, xn[0:PD, 0, bass.ds(u * (2 * TB) + j * TB, TB)],
                                 start=True, stop=True).then_inc(s["mean_ready"], 1)
            if has_prev:
                qk_pe(pe, b * QP + (u - 1), 1)
                turn_v_pe(pe, b * QP + (u - 1))
            for j in range(2):
                pe.wait_ge(s["squared"], ONE + 2 * G + j + 1)
                pe.wait_ge(s["vt_copied"], ONE + 2 * G)
                nc.tensor.matmul(ps[0:PD, 2 + j, :], mean96, ln_sq[0:PD, j, :], start=True, stop=True)\
                    .then_inc(s["var_ready"], 1)
            for j in range(2):
                pe.wait_ge(s["ln_ready"], ONE + 2 * G + j + 1)
                nc.tensor.matmul(ps[0:PD, j, :], w_qkv[:, 2, :], ln_y[0:PD, j, :], start=True, stop=True)\
                    .then_inc(s["v_ready"], 1)
            qk_pe(pe, G, 0)

        def qk_pe(pe, G, w):
            for j in range(2):
                pe.wait_ge(s[("q_taken", "k_taken")[w]], ONE + 2 * G)
                nc.tensor.matmul(ps[0:PD, 4 + 2 * w + j, :], w_qkv[:, w, :], ln_y[0:PD, j, :],
                                 start=True, stop=True).then_inc(s[("q_ready", "k_ready")[w]], 1)

        def turn_v_pe(pe, G):
            for j in range(2):
                pe.wait_ge(s["v_taken"], ONE + 2 * G + j + 1)
                pe.wait_ge(s["ln_root"], ONE + 2 * G + j + 1)
                for c in range(TB // P):
                    mm = nc.tensor.transpose(ps[:, 2 + j, c * PD:(c + 1) * PD], v_sb[0:PD, j, c * P:(c + 1) * P],
                                             ident[0:PD, 0:PD])
                mm.then_inc(s["vt_ready"], 1)

        KT = L // P
        MAX_AT = [min(KT, max(0, st - 3) * 3 // 2) for st in range(KT + 2)]
        TURN_AT, SPREAD_AT, PROJ_AT = 27, 3, (6, 9, 12)

        def out_bank(qb):
            return 6 + qb % 2

        def max_pe(pe, b, nq, g, n):
            mt, kc = n // NB, n % NB
            pe.wait_ge(s["max_read"], ONE + KT * g + (n - 1 if n >= 2 else 0))
            nc.tensor.matmul(ps[:, 2 + n % 2, :], q_st[0:QR, bass.ds(nq * TB + mt * P, P)],
                             k_st[0:QR, kc * TB:(kc + 1) * TB], start=True, stop=True).then_inc(s["max_scores"], 1)

        def turn_pe(pe, g, now):
            pe.wait_ge(s["nm_ready"], ONE + g + 1)
            pe.wait_ge(s["proj_taken"], ONE + CT * now)
            for mt in range(4):
                mm = nc.tensor.matmul(ps[0:KS, 4, mt * P:(mt + 1) * P], negmax[:, mt, :], ident,
                                      start=True, stop=True)
            mm.then_inc(s["nm_turned"], 1)

        def spread_pe(pe, g, turned):
            pe.wait_ge(s["recip_ready"], ONE + g + 1)
            pe.wait_ge(s["nm_taken"], ONE + turned)
            nc.tensor.matmul(ps[0:PD, 4, :], one[96:97, 0:PD], rec[96:97, :], start=True, stop=True)\
                .then_inc(s["recip_spread"], 1)

        def proj_pe(pe, g, m):
            if m == 0:
                pe.wait_ge(s["normed"], ONE + g + 1)
                pe.wait_ge(s["skip_relu"], ONE + 2 * g + 2)
            else:
                pe.wait_ge(s["proj_taken"], ONE + CT * g + m)
            for t in range(CT):
                mm = nc.tensor.matmul(ps[:, 4, :], w_proj[:, t, m * P:(m + 1) * P], cat[:, t, :],
                                      start=(t == 0), stop=(t == CT - 1))
            mm.then_inc(s["proj_mm"], 1)

        def attend_pe(pe, b, qb, has_prev, has_next):
            g = pe.snap(b * NB + qb) if not isinstance(qb, int) else b * NB + qb
            pe.wait_ge(s["nm_stacked"], ONE + g + 1)
            for st in range(KT + 1):
                if st < KT:
                    pe.wait_ge(s["exps"], ONE + KT * g + (st - 1 if st >= 2 else 0))
                    nc.tensor.matmul(ps[:, st % 2, :], k_st[0:KS, st * P:(st + 1) * P],
                                     q_st[0:KS, bass.ds(qb * TB, TB)], start=True, stop=True).then_inc(s["scores"], 1)
                    items = range(MAX_AT[st], MAX_AT[st + 1]) if has_next else ()
                    for n in items[:1]:
                        max_pe(pe, b, qb + 1, g + 1, n)
                if has_prev:
                    if st == SPREAD_AT:
                        spread_pe(pe, g - 1, g + 1)
                    if st in PROJ_AT:
                        proj_pe(pe, g - 1, PROJ_AT.index(st))
                if has_next and st == TURN_AT:
                    turn_pe(pe, g + 1, g)
                if st >= 1:
                    pe.wait_ge(s["exps"], ONE + KT * g + st)
                    if st == 1 and has_prev:
                        pe.wait_ge(s["normed"], ONE + g - 1)
                    mm = nc.tensor.matmul(ps[0:97, bass.ds(out_bank(qb), 1), :].rearrange("p a n -> p (a n)"),
                                          v_t[:, st - 1, :], p_sb[:, (st - 1) % 4, :],
                                          start=(st == 1), stop=(st == KT))
                    mm.then_inc(s["pv_done"], 1)
                if st < KT:
                    for n in items[1:]:
                        max_pe(pe, b, qb + 1, g + 1, n)

        OUTS = 2 + NT + CT
        FIRST = XT_ + 2
        PER = FIRST + OUTS
        ALL = NB * PER

        SEQ = "a0 a1 d0 d1 a2 a3 z0 z1 m1 z2 z3 a4 m2 z4 z5 a5 a6 o0 o1 o2".split()
        SEQ_LAST = [n for n in SEQ if n[0] not in "ad"]
        AT_UNIT = {1: ("a0", "a1"), 2: ("d0", "d1"), 3: ("a2",), 4: ("a3",)}
        EARLY = 4
        assert len(SEQ) == PER and PER % 2 == 0

        def item(name, nxt):
            return FIRST + (SEQ if nxt else SEQ_LAST).index(name)

        def pj_wait(pe, b, i, at0):
            pe.wait_ge(s[f"pj_read{at0 % 2}"], ONE + b * (ALL // 2) + i * (PER // 2) + at0 // 2)

        def in_proj_pe(pe, b, i, j, at0, rows):
            pj_wait(pe, b, i, at0)
            t = ORDER[j]
            n = rows * W
            start = (i + 1) * TB + W
            for k in range(CT):
                mm = nc.tensor.matmul(ps[:, at0 % 2, 0:n], w_in[:, k, DI + t * P:DI + (t + 1) * P],
                                      xs_[:, k, bass.ds(start, n)], start=(k == 0), stop=(k == CT - 1))
            mm.then_inc(s["pj_mm"], 1)

        def dt_pe(pe, b, i, h, at0):
            pj_wait(pe, b, i, at0)
            for k in range(CT):
                mm = nc.tensor.matmul(ps[0:R3, at0 % 2, 0:HALF], w_dt[:, k, :],
                                      xs_[:, k, bass.ds((i + 1) * TB + h * HALF, HALF)],
                                      start=(k == 0), stop=(k == CT - 1))
            mm.then_inc(s["pj_mm"], 1)

        def unit_a_pe(pe, G, u):
            c, hf = u // 2, u % 2
            tok = slice(c * CH, (c + 1) * CH)
            pairs = slice(HP * hf, HP * hf + HP)
            if hf == 0:
                if c == 0:
                    pe.wait_ge(s["bc_dup"], ONE + 32 * G + 32)
                    pe.wait_ge(s["cs_negated"], ONE + G + 1)
                    pe.wait_ge(s["dt_ready"], ONE + G + 1)
                pe.wait_ge(s["small_copied"], ONE + NC * G + c)
                nc.tensor.matmul(ps[:, 5, 0:P], xbc[0:NS, XT_ - 1, tok], c_dup[0:NS, tok], start=True, stop=True)
                mm = nc.tensor.transpose(ps[:, 5, P:P + NS], xbc[0:NS, XT_ - 1, tok], ident[0:NS, 0:NS])
                if c == 0:
                    for cc in range(NC):
                        mm = nc.tensor.transpose(ps[:, 5, P + NS + cc * NH:P + NS + (cc + 1) * NH],
                                                 dt_sb[0:NH, cc * CH:(cc + 1) * CH], ident[0:NH, 0:NH])
                mm.then_inc(s["small_mm"], 1)
            if hf == 0:
                pe.wait_ge(s["diag_ready"], ONE + NC * G + c + 1)
            for par in range(3):
                e = 3 * u + par
                if par == 2:
                    if u < 2:
                        pe.wait_ge(s["silu_done"], ONE + XT_ * G + 1 + HP * (u + 1))
                    pe.wait_ge(s["xdt_ready"], ONE + NU * G + u)
                    for t in range(HP):
                        mm = nc.tensor.transpose(ps[:, 4, t * P:(t + 1) * P], xbc[:, HP * hf + t, tok], ident)
                    mm.then_inc(s["xt_mm"], 1)
                pe.wait_ge(s["exp_done"], ONE + 3 * NU * G + (e - 1 if e >= 2 else 0))
                bank = ps[:, 2 + e % 2, 0:HP * CH]
                diag = cs_diag[0:R3, pairs, tok]
                if par == 2:
                    mm = nc.tensor.matmul(bank, kb[0:R3, B_SEL:B_SEL + P], diag, start=True, stop=True)
                else:
                    nc.tensor.matmul(bank, cs_neg[0:R3, par, tok], diag, start=True, stop=False)
                    mm = nc.tensor.matmul(bank, kb[:, B_ID:B_ID + P], kb[:, B_BIG:B_BIG + HP * CH],
                                          start=False, stop=True)
                mm.then_inc(s["e_mm"], 1)

        def unit_b_pe(pe, b, G, u):
            c, hf, d = u // 2, u % 2, u % 2
            pe.wait_ge(s["y_read"], ONE + NU * G + u)
            pe.wait_ge(s["cd_ready"], ONE + NU * G + u + 1)
            pe.wait_ge(s["att_ready"], ONE + NU * G + u + 1)
            pe.wait_ge(s["state_done"], ONE + NU * G + max(u - 1, 0))
            if u < 2:
                pe.wait_ge(s["state_clear"], ONE + b + 1)
            for t in range(HP):
                y = ps[:, 6, t * CH:(t + 1) * CH]
                nc.tensor.matmul(y, state[:, HP * hf + t, :], c_dec[:, d, t, :], start=True, stop=False,
                                 skip_group_check=True)
                for par in range(2):
                    mm = nc.tensor.matmul(y[64 * par:64 * par + 64, :], x_dt[:, d, t, par, :], att[:, d, par, t, :],
                                          start=False, stop=(par == 1), skip_group_check=True)
            mm.then_inc(s["y_mm"], 1)
            pe.wait_ge(s["state_done"], ONE + NU * G + u)
            pe.wait_ge(s["xw_ready"], ONE + NU * G + u + 1)
            for par in range(2):
                mm = nc.tensor.matmul(ps[64 * par:64 * par + 64, 7, 0:HP * HD], small[:, c % 2, P:P + NS],
                                      x_w[:, d, :, par, :], start=True, stop=True)
            mm.then_inc(s["st_mm"], 1)

        def block_pe(pe, b, i, nxt):
            G = b * NB + i if isinstance(i, int) else pe.snap(b * NB + i)
            for u in range(NU):
                unit_a_pe(pe, G, u)
                if u:
                    unit_b_pe(pe, b, G, u - 1)
                for name in AT_UNIT.get(u, ()) if nxt else ():
                    if name[0] == "a":
                        in_proj_pe(pe, b, i, int(name[1]), item(name, nxt), nxt)
                    else:
                        dt_pe(pe, b, i, int(name[1]), item(name, nxt))

            def moment(name, ready, count):
                at0 = item(name, nxt)
                pj_wait(pe, b, i, at0)
                pe.wait_ge(s[ready], count)
                nc.tensor.matmul(ps[:, at0 % 2, :], mean768, row, start=True, stop=True).then_inc(s["pj_mm"], 1)

            def z(t):
                at0 = item(f"z{t}", nxt)
                pj_wait(pe, b, i, at0)
                for k in range(CT):
                    mm = nc.tensor.matmul(ps[:, at0 % 2, :], w_in[:, k, t * P:(t + 1) * P],
                                          xs_[:, k, bass.ds(i * TB, TB)], start=(k == 0), stop=(k == CT - 1))
                mm.then_inc(s["pj_mm"], 1)

            z(0)
            unit_b_pe(pe, b, G, NU - 1)
            z(1)
            moment("m1", "sum1_ready", ONE + NC * (G + 1))
            for t in (2, 3):
                z(t)
            if nxt:
                in_proj_pe(pe, b, i, 4, item("a4", nxt), nxt)
            moment("m2", "sum2_ready", ONE + G + 1)
            for t in (4, 5):
                z(t)
            if nxt:
                for t in (5, 6):
                    in_proj_pe(pe, b, i, t, item(f"a{t}", nxt), nxt)
            for m in range(CT):
                at0 = item(f"o{m}", nxt)
                pj_wait(pe, b, i, at0)
                for t in range(NT):
                    if m == 0:
                        pe.wait_ge(s["gated"], ONE + NT * G + t + 1)
                    mm = nc.tensor.matmul(ps[:, at0 % 2, :], w_out[:, t, m * P:(m + 1) * P], y_sb[:, t, :],
                                          start=(t == 0), stop=(t == NT - 1))
                mm.then_inc(s["pj_mm"], 1)

        @block.tensor
        def _(pe):
            begin(pe)
            pe.wait_ge(s["weights_loaded"], ONE + 16 * 7)
            with pe.Fori(0, B) as b:
                gn_pe(pe, 2 * b)
                pe.wait_ge(s["xn0_ready"], ONE + b + 1)
                own(pe)
                qkv_pe(pe, b, 0, False)
                with pe.Fori(1, QP) as u:
                    qkv_pe(pe, b, u, True)
                qk_pe(pe, b * QP + (QP - 1), 1)
                turn_v_pe(pe, b * QP + (QP - 1))
                meet(pe, b, 0)
                for n in range(32):
                    max_pe(pe, b, 0, b * NB, n)
                turn_pe(pe, b * NB, b * NB)
                attend_pe(pe, b, 0, False, True)
                with pe.Fori(1, NB - 1) as qb:
                    attend_pe(pe, b, qb, True, True)
                attend_pe(pe, b, NB - 1, True, False)
                spread_pe(pe, b * NB + (NB - 1), b * NB + NB)
                for m in range(CT):
                    proj_pe(pe, b * NB + (NB - 1), m)
                meet(pe, b, 1)
                gn_pe(pe, 2 * b + 1)
                pe.wait_ge(s["win_loaded"], ONE + 16 * b + 16)
                pe.wait_ge(s["ab_ready"], ONE + 2 * b + 2)
                for bank, ms in ((5, (XT_ + NT,)), (6, range(NT, XT_ + NT)), (7, range(NT))):
                    for m in ms:
                        rows = P if m < XT_ + NT else R3
                        for k in range(CT):
                            w = w_in[:, k, m * P:(m + 1) * P] if m < XT_ + NT else w_dt_raw[:, k, :]
                            mm = nc.tensor.matmul(ps[0:rows, bank, m:m + 1], w, gn_ab[:, k, 1:2], start=(k == 0),
                                                  stop=(k == CT - 1))
                    mm.then_inc(s["beta_mm"], 1)
                pe.wait_ge(s["w_scaled"], ONE + 3 * b + 1)
                for h in range(2):
                    dt_pe(pe, b, -1, h, PER + h)
                pe.wait_ge(s["w_scaled"], ONE + 3 * b + 2)
                for t in range(XT_):
                    for k in range(CT):
                        mm = nc.tensor.matmul(ps[:, 4, t * W:(t + 1) * W], w_in[:, k, DI + t * P:DI + (t + 1) * P],
                                              xs_[:, k, 0:W], start=(k == 0), stop=(k == CT - 1))
                mm.then_inc(s["row0_mm"], 1)
                for t in range(XT_):
                    in_proj_pe(pe, b, -1, t, PER + 2 + t, ROWS)
                pe.wait_ge(s["row0_done"], ONE + b + 1)
                own(pe)
                pe.wait_ge(s["w_scaled"], ONE + 3 * b + 3)
                own(pe)
                with pe.Fori(0, NB - 2) as i:
                    block_pe(pe, b, i, ROWS)
                block_pe(pe, b, NB - 2, ROWS - 1)
                block_pe(pe, b, NB - 1, 0)
                meet(pe, b, 2)

        def gn_act(act, n):
            act.wait_ge(s["vars_ready"], ONE + n + 1)
            nc.scalar.activation(group_sc[:, 1:2], group_sc[:, 1:2], ACT.Sqrt, bias=eps(slice(0, GROUPS)))\
                .then_inc(s["roots_ready"], 1)

        def block_act(act, b, i, nxt, step):
            G = b * NB + i if isinstance(i, int) else act.snap(b * NB + i)
            for j in range(1, XT_):
                silu(act, G, j)
            for u in range(NU):
                c, hf, d = u // 2, u % 2, u % 2
                if hf == 0:
                    act.wait_ge(s["small_mm"], ONE + NC * G + c + 1)
                    act.wait_ge(s["att_ready"], ONE + NU * G + max(2 * c - 2, 0))
                    act.wait_ge(s["st_mm"], ONE + NU * G + max(2 * c - 2, 0))
                    if c == 0:
                        nc.scalar.copy(dt_t, ps[:, 5, P + NS:P + NS + NC * NH])
                    nc.scalar.copy(small[:, c % 2, :], ps[:, 5, 0:P + NS]).then_inc(s["small_copied"], 1)
                for par in range(3):
                    e = 3 * u + par
                    act.wait_ge(s["e_mm"], ONE + 3 * NU * G + e + 1)
                    if par == 0:
                        for name in ("att_ready", "xw_ready", "cd_ready", "sdec_ready"):
                            act.wait_ge(s[name], ONE + NU * G + max(u - 1, 0))
                        if u == 0:
                            act.wait_ge(s["sum2_ready"], ONE + G)
                    dst = grow[:, d, :, :] if par == 2 else decay[:, d, par, :, :]
                    nc.scalar.activation(dst, shaped(ps[:, 2 + e % 2, 0:HP * CH], HP, CH), ACT.Exp)\
                        .then_inc(s["exp_done"], 1)
                for name in AT_UNIT.get(u, ()) if nxt else ():
                    if name[0] == "a":
                        take_pre(act, b, i, G + 1, int(name[1]), item(name, nxt), nxt)
                    else:
                        take_dt(act, b, i, G + 1, int(name[1]), item(name, nxt))

            def z_copy(t):
                at0 = item(f"z{t}", nxt)
                act.wait_ge(s["pj_mm"], ONE + b * ALL + i * PER + at0 + 1)
                if t == 0:
                    act.wait_ge(s["y_read"], ONE + NU * G + NU)
                    act.wait_ge(s["st_mm"], ONE + NU * G + NU)
                nc.scalar.activation(xbc[:, t, :], ps[:, at0 % 2, :], ACT.Identity, bias=beta[:, t:t + 1])\
                    .then_inc(s[f"pj_read{at0 % 2}"], 1)

            if nxt:
                ln_act(act, G + 1)
            z_copy(0)
            z_copy(1)
            for half in range(2):
                act.wait_ge(s["y_centred"], ONE + 2 * G + half + 1)
                if half == 0:
                    act.wait_ge(s["y_mm"], ONE + NU * G + NU)
                nc.scalar.activation(sq[:, HP * half:HP * half + HP, :], y_sb[:, HP * half:HP * half + HP, :],
                                     ACT.Square).then_inc(s["sq_ready"], 1)
            if nxt:
                silu(act, G + 1, 0)
            for t in (2, 3):
                z_copy(t)
            if nxt:
                take_pre(act, b, i, G + 1, 4, item("a4", nxt), nxt)
            at0 = item("m2", nxt)
            act.wait_ge(s["pj_mm"], ONE + b * ALL + i * PER + at0 + 1)
            nc.scalar.activation(row, ps[:, at0 % 2, :], ACT.Sqrt, bias=eps()).then_inc(s[f"pj_read{at0 % 2}"], 1)
            for t in (4, 5):
                z_copy(t)
            for half in range(2):
                for t in range(HP * half, HP * half + HP):
                    act.wait_ge(s["y_scaled"], ONE + 2 * G + half + 1)
                    nc.scalar.activation(y_sb[:, t, :], y_sb[:, t, :], ACT.Identity, bias=vec[:, V_NB + t:V_NB + t + 1],
                                         scale=vec[:, V_NW + t:V_NW + t + 1]).then_inc(s["y_affine"], 1)
                if nxt:
                    t = 5 + half
                    take_pre(act, b, i, G + 1, t, item(f"a{t}", nxt), nxt)
            if nxt:
                conv_act(act, G + 1)

        def silu(act, G, j):
            if j == 0:
                act.wait_ge(s["small_mm"], ONE + NC * G)
            if j == 1:
                act.wait_ge(s["gated"], ONE + NT * G)
            if j < VT:
                act.wait_ge(s["conv_done"], ONE + VT * G + j + 1)
            else:
                act.wait_ge(s["tap_added"], ONE + len(TAPS) * (G + 1))
            t = ORDER[j]
            nc.scalar.activation(xbc[:, t, :], acc[:, t, :], ACT.Silu).then_inc(s["silu_done"], 1)

        def take_pre(act, b, i, G1, j, at0, rows):
            act.wait_ge(s["pj_mm"], ONE + b * ALL + i * PER + at0 + 1)
            act.wait_ge(s["carried"], ONE + G1 + 1)
            t = ORDER[j]
            nc.scalar.activation(pre[:, t, 2:2 + rows, 1:1 + W], shaped(ps[:, at0 % 2, 0:rows * W], rows, W),
                                 ACT.Identity, bias=beta[:, NT + t:NT + t + 1]).then_inc(s[f"pj_read{at0 % 2}"], 1)
            act.wait_ge(s[f"pj_read{at0 % 2}"], ONE + b * (ALL // 2) + i * (PER // 2) + at0 // 2 + 1)
            act.wait_ge(s["silu_done"], ONE + G1 * XT_)
            nc.scalar.activation(shaped(acc[:, t, :], ROWS, W), pre[:, t, 1:1 + ROWS, 1:1 + W], ACT.Identity,
                                 bias=vec[:, V_CB + t:V_CB + t + 1],
                                 scale=vec[:, V_CW + 9 * t + 4:V_CW + 9 * t + 5]).then_inc(s["centre_done"], 1)

        def conv_act(act, G1):
            t = ORDER[VT]
            act.wait_ge(s["sum2_ready"], ONE + G1)
            for k, tap in enumerate(TAPS):
                dy, dx = tap // 3, tap % 3
                act.wait_ge(s["tap_added"], ONE + len(TAPS) * G1 + max(k - 1, 0))
                nc.scalar.activation(shaped(tap_prod[k % 2], ROWS, W), pre[:, t, dy:dy + ROWS, dx:dx + W],
                                     ACT.Identity, scale=vec[:, V_CW + 9 * t + tap:V_CW + 9 * t + tap + 1])\
                    .then_inc(s["tap_ready"], 1)

        def take_dt(act, b, i, G1, h, at0):
            tok = slice(h * HALF, (h + 1) * HALF)
            dtb = beta[0:R3, XT_ + NT:XT_ + NT + 1]
            act.wait_ge(s["pj_mm"], ONE + b * ALL + i * PER + at0 + 1)
            act.wait_ge(s["dt_ready"], ONE + G1)
            act.wait_ge(s["cs_negated"], ONE + G1)
            v = ps[0:R3, at0 % 2, 0:HALF]
            nc.scalar.activation(sp_l[0:R3, tok], v, ACT.Abs, bias=dtb).then_inc(s["dt_abs"], 1)
            nc.scalar.activation(cs[0:R3, tok], v, ACT.Relu, bias=dtb).then_inc(s[f"pj_read{at0 % 2}"], 1)
            act.wait_ge(s["dt_abs"], ONE + 2 * G1 + h + 1)
            nc.scalar.activation(sp_e[0:R3, tok], sp_l[0:R3, tok], ACT.Exp, scale=-1.0).then_inc(s["sp_exp"], 1)

        def ln_act(act, G1):
            act.wait_ge(s["sp_exp"], ONE + 2 * G1 + 2)
            nc.scalar.activation(sp_l[0:R3, :], sp_e[0:R3, :], ACT.Ln, bias=one[0:R3, 0:1]).then_inc(s["sp_ln"], 1)

        def take_qk(act, G, w):
            for j in range(2):
                act.wait_ge(s[("q_ready", "k_ready")[w]], ONE + 2 * G + j + 1)
                act.wait_ge(s[("q_stacked", "k_stacked")[w]], ONE + 2 * G)
                bank = ps[0:PD, 4 + 2 * w + j, :]
                nc.scalar.activation(qk_f[0:PD, w, j, :], bank, ACT.Identity, bias=bn1o[:, w:w + 1],
                                     scale=bn1s[:, w:w + 1])
                nc.scalar.activation(qk_h[0:PD, w, j, :], bank, ACT.Identity, bias=bn1o[:, w:w + 1],
                                     scale=bn1s[:, w:w + 1]).then_inc(s[("q_taken", "k_taken")[w]], 1)

        def qkv_act(act, b, u, has_prev):
            G = b * QP + u if isinstance(u, int) else act.snap(b * QP + u)
            for j in range(2):
                act.wait_ge(s["centred"], ONE + 2 * G + j + 1)
                act.wait_ge(s["scaled"], ONE + 2 * G)
                nc.scalar.activation(ln_sq[0:PD, j, :], ln_x[0:PD, j, :], ACT.Square).then_inc(s["squared"], 1)
            if has_prev:
                take_qk(act, b * QP + (u - 1), 1)
            for j in range(2):
                act.wait_ge(s["var_ready"], ONE + 2 * G + j + 1)
                nc.scalar.activation(ln_sq[0:PD, j, :], ps[0:PD, 2 + j, :], ACT.Sqrt, bias=eps(slice(0, PD)))\
                    .then_inc(s["ln_root"], 1)
            for j in range(2):
                act.wait_ge(s["scaled"], ONE + 2 * G + j + 1)
                act.wait_ge(s["k_ready"], ONE + 2 * G)
                nc.scalar.activation(ln_y[0:PD, j, :], ln_x[0:PD, j, :], ACT.Identity,
                                     bias=vec[0:PD, V_LN + 1:V_LN + 2], scale=vec[0:PD, V_LN:V_LN + 1])\
                    .then_inc(s["ln_ready"], 1)
            for j in range(2):
                act.wait_ge(s["v_ready"], ONE + 2 * G + j + 1)
                act.wait_ge(s["vt_ready"], ONE + 2 * G)
                nc.scalar.activation(v_sb[0:PD, j, :], ps[0:PD, j, :], ACT.Identity, bias=bn1o[:, 2:3],
                                     scale=bn1s[:, 2:3]).then_inc(s["v_taken"], 1)
            take_qk(act, G, 0)

        @block.scalar
        def _(act):
            begin(act)
            act.wait_ge(s["weights_loaded"], ONE + 16 * 7)
            nc.scalar.activation(a_neg[:, :], vec[0:R3, V_AL:V_AL + 1], ACT.Exp).then_inc(s["steps_a"], 1)
            act.wait_ge(s["steps_a"], ONE + 1)
            nc.scalar.activation(a_neg[:, :], a_neg[:, :], ACT.Copy, scale=-1.0).then_inc(s["prepared"], 1)
            nc.scalar.activation(bn1s[:], vec[0:PD, V_BN1 + 9:V_BN1 + 12], ACT.Sqrt, bias=eps(slice(0, PD)))\
                .then_inc(s["prepared"], 1)
            nc.scalar.activation(bn2s[:], vec[:, V_BN2 + 9:V_BN2 + 12], ACT.Sqrt, bias=eps()).then_inc(s["prepared"], 1)
            act.wait_ge(s["vec_prepared"], ONE + 1)
            with act.Fori(0, B) as b:
                gn_act(act, 2 * b)
                act.wait_ge(s["ab_ready"], ONE + 2 * b + 1)
                nc.scalar.activation(xn[:, 0, :], xs_[:, 0, :], ACT.Identity, bias=gn_ab[:, 0, 1:2],
                                     scale=gn_ab[:, 0, 0:1]).then_inc(s["xn0_ready"], 1)
                qkv_act(act, b, 0, False)
                with act.Fori(1, QP) as u:
                    qkv_act(act, b, u, True)
                take_qk(act, b * QP + (QP - 1), 1)
                meet(act, b, 0)

                def take_max(g):
                    act.wait_ge(s["nm_turned"], ONE + g + 1)
                    nc.scalar.copy(nm_f[96:99, :], ps[96:99, 4, :])
                    nc.scalar.copy(nm_h[96:99, :], ps[96:99, 4, :]).then_inc(s["nm_taken"], 1)

                def take_recip(g):
                    act.wait_ge(s["recip_spread"], ONE + g + 1)
                    nc.scalar.copy(rec_b[0:PD, :], ps[0:PD, 4, :]).then_inc(s["recip_copied"], 1)

                def take_proj(g, m):
                    act.wait_ge(s["proj_mm"], ONE + CT * g + m + 1)
                    act.wait_ge(s["x1_added"], ONE + CT * g)
                    nc.scalar.activation(proj_y[:, m, :], ps[:, 4, :], ACT.Identity, bias=bn2o[:, m:m + 1],
                                         scale=bn2s[:, m:m + 1]).then_inc(s["proj_taken"], 1)

                def attend_act(qb, has_prev, has_next):
                    g = act.snap(b * NB + qb) if not isinstance(qb, int) else b * NB + qb
                    blk = bass.ds(qb * TB, TB)
                    for st in range(KT):
                        act.wait_ge(s["scores"], ONE + KT * g + st + 1)
                        act.wait_ge(s["pv_done"], ONE + KT * g + max(st - 3, 0))
                        nc.scalar.activation(p_sb[:, st % 4, :], ps[:, st % 2, :], ACT.Exp,
                                             scale=QK ** -0.5).then_inc(s["exps"], 1)
                        if has_prev:
                            if st == SPREAD_AT:
                                take_recip(g - 1)
                            if st - 1 in PROJ_AT:
                                take_proj(g - 1, PROJ_AT.index(st - 1))
                        if st == 16:
                            act.wait_ge(s["proj_mm"], ONE + CT * g)
                            act.wait_ge(s["xn1_ready"], ONE + b + 1)
                            act.wait_ge(s["xn2_ready"], ONE + b + 1)
                            nc.scalar.activation(cat[PD:P, 0, :], xn[PD:P, 0, blk], ACT.Relu).then_inc(s["skip_relu"], 1)
                            nc.scalar.activation(cat[:, 1:CT, :], xn[:, 1:CT, blk], ACT.Relu)\
                                .then_inc(s["skip_relu"], 1)
                        if has_next and st == TURN_AT:
                            take_max(g + 1)

                take_max(b * NB)
                attend_act(0, False, True)
                with act.Fori(1, NB - 1) as qb:
                    attend_act(qb, True, True)
                attend_act(NB - 1, True, False)
                take_recip(b * NB + (NB - 1))
                for m in range(CT):
                    take_proj(b * NB + (NB - 1), m)
                meet(act, b, 1)
                gn_act(act, 2 * b + 1)
                for h in range(2):
                    take_dt(act, b, -1, b * NB, h, PER + h)
                ln_act(act, b * NB)
                act.wait_ge(s["row0_mm"], ONE + b + 1)
                act.wait_ge(s["top_clear"], ONE + 2 * b + 2)
                for t in range(XT_):
                    ins = nc.scalar.activation(pre[:, t, 9, 1:1 + W], ps[:, 4, t * W:(t + 1) * W], ACT.Identity,
                                               bias=beta[:, NT + t:NT + t + 1])
                ins.then_inc(s["row0_done"], 1)
                for t in range(XT_):
                    take_pre(act, b, -1, b * NB, t, PER + 2 + t, ROWS)
                conv_act(act, b * NB)
                silu(act, b * NB, 0)
                with act.Fori(0, NB - 2) as i:
                    block_act(act, b, i, ROWS, None)
                block_act(act, b, NB - 2, ROWS - 1, None)
                block_act(act, b, NB - 1, 0, None)
                meet(act, b, 2)

        def dt_pool(pool, G1, step):
            r = slice(0, R3)
            pool.wait_ge(s["sp_zero"], ONE + G1 + 1)
            step(nc.gpsimd.tensor_tensor(sp_d[r, :], sp_d[r, :], sp_r[r, :], ALU.add))
            pool.wait_ge(s["sp_ln"], ONE + G1 + 1)
            step(nc.gpsimd.tensor_tensor(sp_r[r, :], sp_l[r, :], sp_r[r, :], ALU.add))
            step.join()
            nc.gpsimd.tensor_tensor(sp_l[r, :], sp_r[r, :], sp_e[r, :], ALU.mult).then_inc(s["sp_prod"], 1)

        def diag_pool(pool, G1, lo, hi):
            if lo == 0:
                pool.wait_ge(s["cs_stacked"], ONE + G1 + 1)
                own(pool)
                pool.wait_ge(s["e_mm"], ONE + 3 * NU * G1)
                own(pool)
            for c in range(lo, hi):
                tok = slice(c * CH, (c + 1) * CH)
                nc.gpsimd.tensor_tensor(cs_diag[0:R3, :, tok],
                                        cs_st[0:R3, tok].unsqueeze(1).broadcast_to([R3, NT, CH]),
                                        shaped(kb[0:R3, B_DELTA:B_DELTA + NT * CH], NT, CH), ALU.mult)\
                    .then_inc(s["diag_ready"], 1)

        def conv_pool(pool, G1):
            t = ORDER[VT]
            pool.wait_ge(s["centre_done"], ONE + XT_ * (G1 + 1))
            for k in range(len(TAPS)):
                pool.wait_ge(s["tap_ready"], ONE + len(TAPS) * G1 + k + 1)
                if k:
                    pool.wait_ge(s["tap_added"], ONE + len(TAPS) * G1 + k)
                nc.gpsimd.tensor_tensor(acc[:, t, :], acc[:, t, :], tap_prod[k % 2], ALU.add)\
                    .then_inc(s["tap_added"], 1)

        def carry_pool(pool, G1):
            pool.wait_ge(s["conv_done"], ONE + G1 * VT)
            own(pool)
            pool.wait_ge(s["tap_ready"], ONE + len(TAPS) * G1)
            own(pool)
            nc.gpsimd.tensor_copy(pre[:, :, 0:2, :], pre[:, :, ROWS:ROWS + 2, :]).then_inc(s["carried"], 1)

        def block_pool(pool, b, i, nxt, step):
            G = b * NB + i if isinstance(i, int) else pool.snap(b * NB + i)
            if nxt:
                carry_pool(pool, G + 1)
            def sum_y(c):
                tok = slice(c * CH, (c + 1) * CH)
                pool.wait_ge(s["y_read"], ONE + NU * G + 2 * c + 2)
                step(nc.gpsimd.tensor_tensor(row[:, tok], y_sb[:, 0, tok], y_sb[:, 1, tok], ALU.add))
                for t in range(2, NT):
                    step.join()
                    ins = nc.gpsimd.tensor_tensor(row[:, tok], row[:, tok], y_sb[:, t, tok], ALU.add)
                    if t < NT - 1:
                        step(ins)
                ins.then_inc(s["sum1_ready"], 1)

            if nxt == ROWS - 1:
                pool.wait_ge(s["carried"], ONE + G + 2)
                own(pool)
                nc.gpsimd.memset(pre[:, :, ROWS + 1, :], 0.0).then_inc(s["bottom_clear"], 1)
            for u in range(NU):
                c, hf, d = u // 2, u % 2, u % 2
                tok = slice(c * CH, (c + 1) * CH)
                pool.wait_ge(s["exp_done"], ONE + 3 * NU * G + 3 * u + 3)
                if u == 0:
                    pool.wait_ge(s["bc_dup"], ONE + 32 * G + 32)
                pool.wait_ge(s["y_mm"], ONE + NU * G + max(u - 1, 0))
                nc.gpsimd.tensor_tensor(c_dec[:, d, :, :], grow[:, d, :, :],
                                        c_dup[:, tok].unsqueeze(1).broadcast_to([P, HP, CH]), ALU.mult)\
                    .then_inc(s["cd_ready"], 1)
                pool.wait_ge(s["st_mm"], ONE + NU * G + max(u - 1, 0))
                pool.wait_ge(s["xdt_ready"], ONE + NU * G + u + 1)
                last = decay[:, d, :, :, CH - 1].rearrange("p a t -> p t a")
                nc.gpsimd.tensor_tensor(x_w[:, d, :, :, :], x_dt[:, d, :, :, :],
                                        last.unsqueeze(3).broadcast_to([P, HP, 2, HD]), ALU.mult)\
                    .then_inc(s["xw_ready"], 1)
                pool.wait_ge(s["state_done"], ONE + NU * G + u)
                if u < 2:
                    pool.wait_ge(s["state_clear"], ONE + b + 1)
                nc.gpsimd.tensor_tensor(st_dec, state[:, HP * hf:HP * hf + HP, :],
                                        grow[:, d, :, CH - 1:CH].broadcast_to([P, HP, P]), ALU.mult)\
                    .then_inc(s["sdec_ready"], 1)
                if u % 2 == 0 and u:
                    sum_y(c - 1)
            if nxt:
                dt_pool(pool, G + 1, step)
            sum_y(NC - 1)
            pool.wait_ge(s["st_mm"], ONE + NU * G + NU)
            pool.wait_ge(s["sq_ready"], ONE + 2 * G + 2)
            step(nc.gpsimd.tensor_tensor(sum3[:, :, :], sq[:, 0:HP, :], sq[:, HP:NT, :], ALU.add))
            step.join()
            step(nc.gpsimd.tensor_tensor(row, sum3[:, 0, :], sum3[:, 1, :], ALU.add))
            step.join()
            step(nc.gpsimd.tensor_tensor(row, row, sum3[:, 2, :], ALU.add))
            step.join()
            pool.sem_inc(s["sum2_ready"], 1)
            if nxt:
                diag_pool(pool, G + 1, 0, NC)
                conv_pool(pool, G + 1)

        POOL_BLK, POOL_END, POOL_PRO = 4 * NC + 3 + 2, 4 * NC + 3, 2
        POOL_ALL = POOL_PRO + POOL_BLK * (NB - 1) + POOL_END

        @block.gpsimd
        def _(pool):
            step = Steps(pool, s["steps_p"])
            begin(pool)
            pool.wait_ge(s["weights_loaded"], ONE + 16 * 7)
            with pool.Fori(0, B) as b:
                nc.gpsimd.memset(v_t[:, :, 96:97], 1.0)
                pool.wait_ge(s["ab_ready"], ONE + 2 * b + 1)
                own(pool)
                nc.gpsimd.tensor_scalar(xn[:, 2, :], xs_[:, 2, :], gn_ab[:, 2, 0:1], gn_ab[:, 2, 1:2], ALU.mult,
                                        ALU.add).then_inc(s["xn2_ready"], 1)
                meet(pool, b, 0)
                with pool.Fori(0, NB) as qb:
                    g = pool.snap(b * NB + qb)
                    for m in range(CT):
                        pool.wait_ge(s["proj_taken"], ONE + CT * g + m + 1)
                        xb = xs_[:, m, bass.ds(qb * TB, TB)]
                        nc.gpsimd.tensor_tensor(xb, xb, proj_y[:, m, :], ALU.add).then_inc(s["x1_added"], 1)
                meet(pool, b, 1)
                nc.gpsimd.memset(pre[:, :, :, :], 0.0).then_inc(s["top_clear"], 1)
                nc.gpsimd.memset(state[:, :, :], 0.0).then_inc(s["state_clear"], 1)
                pool.wait_ge(s["top_clear"], ONE + 2 * b + 1)
                pool.sem_inc(s["top_clear"], 1)
                step.enter(b * POOL_ALL)
                dt_pool(pool, b * NB, step)
                pool.wait_ge(s["row0_done"], ONE + b + 1)
                carry_pool(pool, b * NB)
                assert step.n == POOL_PRO, step.n
                diag_pool(pool, b * NB, 0, NC)
                conv_pool(pool, b * NB)
                with pool.Fori(0, NB - 2) as i:
                    step.enter(pool.snap(b * POOL_ALL + i * POOL_BLK + POOL_PRO))
                    block_pool(pool, b, i, ROWS, step)
                    assert step.n == POOL_BLK, step.n
                step.enter(b * POOL_ALL + (NB - 2) * POOL_BLK + POOL_PRO)
                block_pool(pool, b, NB - 2, ROWS - 1, step)
                step.enter(b * POOL_ALL + (NB - 1) * POOL_BLK + POOL_PRO)
                block_pool(pool, b, NB - 1, 0, step)
                assert step.n == POOL_END, step.n
                meet(pool, b, 2)

        V = nc.vector

        def gn_dve(dve, n, step):
            own(dve)
            for t in range(CT):
                step(V.bn_aggr(chan_mv[:, t, :], chan_stats[:, t, :, :]))
            step.join()
            for t in range(CT):
                ins = V.scalar_tensor_tensor(chan_mv[:, t, 1:2], chan_mv[:, t, 0:1], chan_mv[:, t, 0:1],
                                             chan_mv[:, t, 1:2], ALU.mult, ALU.add)
            ins.then_inc(s["stats_ready"], 1)
            dve.wait_ge(s["group_sums"], ONE + n + 1)
            step(V.tensor_copy(group_mv[:], ps[0:GROUPS, 7, 0:2]))
            step.join()
            step(V.tensor_scalar(group_sc[:, 0:1], group_mv[:, 0:1], group_mv[:, 0:1], None, ALU.mult))
            step.join()
            V.tensor_tensor(group_sc[:, 1:2], group_mv[:, 1:2], group_sc[:, 0:1], ALU.subtract)\
                .then_inc(s["vars_ready"], 1)
            dve.wait_ge(s["roots_ready"], ONE + n + 1)
            step(V.reciprocal(group_sc[:, 2:3], group_sc[:, 1:2]))
            step.join()
            V.scalar_tensor_tensor(group_sc[:, 3:4], group_mv[:, 0:1], -1.0, group_sc[:, 2:3], ALU.mult, ALU.mult)\
                .then_inc(s["groups_ready"], 1)
            dve.wait_ge(s["group_back"], ONE + n + 1)
            V.tensor_copy(gn_ab[:], shaped(ps[:, 7, 8:8 + 2 * CT], CT, 2)).then_inc(s["ab_ready"], 1)
        GN_STEPS = CT + 3

        def stack_qk(dve, G, u, w, step):
            st = (q_st, k_st)[w]
            dve.wait_ge(s[("q_taken", "k_taken")[w]], ONE + 2 * G + 2)
            f, h, m = (v[0:PD, w, :, :] for v in (qk_f, qk_h, qk_m))
            step(V.scalar_tensor_tensor(f, h, mask(2 * w, slice(0, PD)), f, ALU.mult, ALU.add))
            step.join()
            step(V.tensor_copy(m, f))
            step.join()
            V.scalar_tensor_tensor(st[0:PD, bass.ds(u * (2 * TB), 2 * TB)],
                                   m.rearrange("p a b -> p (a b)"), mask(2 * w + 1, slice(0, PD)),
                                   f.rearrange("p a b -> p (a b)"), ALU.mult, ALU.add)\
                .then_inc(s[("q_stacked", "k_stacked")[w]], 2)

        def take_vt(dve, G, u):
            for j in range(2):
                dve.wait_ge(s["vt_ready"], ONE + 2 * G + j + 1)
                V.tensor_copy(v_t[:, bass.ds(u * 8 + j * 4, 4), 0:PD], shaped(ps[:, 2 + j, 0:4 * PD], 4, PD))\
                    .then_inc(s["vt_copied"], 1)

        def qkv_dve(dve, b, u, has_prev, step):
            G = b * QP + u if isinstance(u, int) else dve.snap(b * QP + u)
            dve.wait_ge(s["xn0_ready"], ONE + b + 1)
            for j in range(2):
                dve.wait_ge(s["mean_ready"], ONE + 2 * G + j + 1)
                dve.wait_ge(s["ln_ready"], ONE + 2 * G)
                V.tensor_tensor(ln_x[0:PD, j, :], xn[0:PD, 0, bass.ds(u * (2 * TB) + j * TB, TB)],
                                ps[0:PD, j, :], ALU.subtract).then_inc(s["centred"], 1)
            if has_prev:
                before = dve.snap(b * QP + (u - 1))
                take_vt(dve, before, u - 1)
                stack_qk(dve, before, u - 1, 0, step)
            for j in range(2):
                dve.wait_ge(s["ln_root"], ONE + 2 * G + j + 1)
                dve.wait_ge(s["centred"], ONE + 2 * G + j + 1)
                step(V.reciprocal(ln_sq[0:PD, j, :], ln_sq[0:PD, j, :]))
                step.join()
                V.tensor_tensor(ln_x[0:PD, j, :], ln_x[0:PD, j, :], ln_sq[0:PD, j, :], ALU.mult)\
                    .then_inc(s["scaled"], 1)
            if has_prev:
                stack_qk(dve, before, u - 1, 1, step)

        def max_dve(dve, g, n):
            dve.wait_ge(s["max_scores"], ONE + 32 * g + n + 1)
            V.tensor_reduce(maxes[:, n // NB, n % NB:n % NB + 1], ps[:, 2 + n % 2, :], AX.X, ALU.max)\
                .then_inc(s["max_read"], 1)

        def negmax_dve(dve, g, step):
            dve.wait_ge(s["max_read"], ONE + 32 * g + 32)
            step(V.tensor_reduce(max4[:], maxes[:], AX.X, ALU.max))
            step.join()
            dve.wait_ge(s["nm_turned"], ONE + g)
            V.tensor_scalar(negmax[:, :, QR:KS], max4[:].unsqueeze(2).broadcast_to([P, 4, 3]), -1.0, None, ALU.mult)\
                .then_inc(s["nm_ready"], 1)

        def split_max(dve, g, nq, step):
            r = slice(96, 99)
            dve.wait_ge(s["nm_taken"], ONE + g + 1)
            step(V.scalar_tensor_tensor(nm_f[r, :], nm_h[r, :], mask(0, r), nm_f[r, :], ALU.mult, ALU.add))
            step.join()
            step(V.tensor_copy(nm_m[r, :], nm_f[r, :]))
            step.join()
            V.scalar_tensor_tensor(q_st[r, bass.ds(nq * TB, TB)], nm_m[r, :], mask(1, r), nm_f[r, :], ALU.mult,
                                   ALU.add).then_inc(s["nm_stacked"], 1)

        def recip_dve(dve, g, qb):
            dve.wait_ge(s["pv_done"], ONE + KT * (g + 1))
            V.reciprocal(rec[96:97, :], ps[96:97, bass.ds(out_bank(qb), 1), :].rearrange("p a n -> p (a n)"))\
                .then_inc(s["recip_ready"], 1)

        def norm_dve(dve, g, qb):
            dve.wait_ge(s["recip_copied"], ONE + g + 1)
            V.scalar_tensor_tensor(cat[0:PD, 0, :],
                                   ps[0:PD, bass.ds(out_bank(qb), 1), :].rearrange("p a n -> p (a n)"), 0.0,
                                   rec_b[0:PD, :], ALU.max, ALU.mult).then_inc(s["normed"], 1)

        def stats_dve(dve, g, qb, m, step):
            dve.wait_ge(s["x1_added"], ONE + CT * g + m + 1)
            step(V.bn_stats(chan_stats[:, m, bass.ds(qb, 1), :], xs_[:, m, bass.ds(qb * TB, TB)]))

        STATS_AT = (20, 23, 26)

        def attend_dve(dve, b, qb, has_prev, has_next, step):
            g = b * NB + qb if isinstance(qb, int) else dve.snap(b * NB + qb)
            if has_prev:
                recip_dve(dve, g - 1, qb - 1)
            for n in range(KT):
                if has_next:
                    max_dve(dve, g + 1, n)
                if has_prev and n == 0:
                    norm_dve(dve, g - 1, qb - 1)
                if has_prev and n in STATS_AT:
                    stats_dve(dve, g - 1, qb - 1, STATS_AT.index(n), step)
            if has_next:
                negmax_dve(dve, g + 1, step)
                split_max(dve, g + 1, qb + 1, step)

        def conv_dve(dve, G1, lo, hi, step):
            for j, k in CONV[lo:hi]:
                t, last, alone = ORDER[j], k == len(TAPS) - 1, j >= 4
                if k == 0:
                    dve.wait_ge(s["centre_done"], ONE + XT_ * G1 + j + 1)
                else:
                    step.join(0 if alone or (last and j % 2 == 1) else 1)
                dy, dx = TAPS[k] // 3, TAPS[k] % 3
                a = shaped(acc[:, t, :], ROWS, W)
                ins = V.scalar_tensor_tensor(a, pre[:, t, dy:dy + ROWS, dx:dx + W],
                                             vec[:, V_CW + 9 * t + TAPS[k]:V_CW + 9 * t + TAPS[k] + 1], a, ALU.mult,
                                             ALU.add)
                if last:
                    ins.then_inc(s["conv_done"], 1)
                else:
                    step(ins)

        def dt_start(dve, G1, step):
            r = slice(0, R3)
            dve.wait_ge(s["sp_exp"], ONE + 2 * G1 + 2)
            step(V.tensor_scalar(sp_d[r, :], sp_e[r, :], 1.0, -1.0, ALU.add, ALU.add))
            step.join()
            V.tensor_scalar(sp_r[r, :], sp_d[r, :], 0.0, None, ALU.is_equal).then_inc(s["sp_zero"], 1)

        def dt_mid(dve, G1, step, turned):
            r = slice(0, R3)
            dve.wait_ge(s["sp_prod"], ONE + G1 + 1)
            step(V.reciprocal(sp_r[r, :], sp_d[r, :]))
            step.join()
            step(V.tensor_tensor(sp_d[r, :], sp_l[r, :], sp_r[r, :], ALU.mult))
            step.join()
            dve.wait_ge(s["small_mm"], ONE + turned)
            V.tensor_tensor(dt_sb[r, :], sp_d[r, :], cs[r, :], ALU.add).then_inc(s["dt_ready"], 1)

        def dt_end(dve, G1, step):
            r = slice(0, R3)
            dve.wait_ge(s["dt_ready"], ONE + G1 + 1)
            step(V.tensor_scalar(sp_r[r, :], dt_sb[r, :], a_neg[r, :], None, ALU.mult))
            step.join()
            for c in range(NC):
                tok = slice(c * CH, (c + 1) * CH)
                step(V.tensor_tensor_scan(cs[r, tok], one[r, 0:CH], sp_r[r, tok], 0.0, ALU.mult, ALU.add))
            step.join()
            step(V.tensor_copy(cs_h[r, :], cs[r, :]))
            step.join()
            step(V.scalar_tensor_tensor(cs[r, :], cs_h[r, :], mask(4, r), cs[r, :], ALU.mult, ALU.add))
            step.join()
            step(V.tensor_copy(cs_h[r, :], cs[r, :]))
            step.join()
            dve.wait_ge(s["diag_ready"], ONE + NC * G1)
            step(V.scalar_tensor_tensor(cs_st[r, :], cs_h[r, :], mask(5, r), cs[r, :], ALU.mult, ALU.add))
            step.join()
            dve.wait_ge(s["e_mm"], ONE + 3 * NU * G1)
            for par in range(2):
                ins = V.tensor_scalar(cs_neg[r, par, :], cs_st[r, :], mask(6 + par, r), mask(8 + par, r), ALU.mult,
                                      ALU.add)
            ins.then_inc(s["cs_negated"], 1)
            V.tensor_scalar(cs_st[r, :], cs_st[r, :], mask(10, r), mask(11, r), ALU.mult, ALU.add)\
                .then_inc(s["cs_stacked"], 1)
        DT_STEPS = 12

        def unit_a_dve(dve, G, u):
            c, hf, d = u // 2, u % 2, u % 2
            dve.wait_ge(s["xt_mm"], ONE + NU * G + u + 1)
            dve.wait_ge(s["small_copied"], ONE + NC * G + c + 1)
            for name in ("y_mm", "xw_ready"):
                dve.wait_ge(s[name], ONE + NU * G + max(u - 1, 0))
            if u == 0:
                dve.wait_ge(s["sum2_ready"], ONE + G)
            heads = slice(NH * c + 2 * HP * hf, NH * c + 2 * HP * (hf + 1))
            V.tensor_tensor(x_dt[:, d, :, :, :].rearrange("p a b c -> p (a b) c"),
                            shaped(ps[:, 4, 0:HP * P], 2 * HP, HD),
                            dt_t[:, heads].unsqueeze(2).broadcast_to([P, 2 * HP, HD]), ALU.mult)\
                .then_inc(s["xdt_ready"], 1)
            dve.wait_ge(s["exp_done"], ONE + 3 * NU * G + 3 * u + 2)
            V.tensor_tensor(att[:, d, :, :, :].rearrange("p a b c -> p (a b) c"),
                            decay[:, d, :, :, :].rearrange("p a b c -> p (a b) c"),
                            small[:, c % 2, 0:P].unsqueeze(1).broadcast_to([P, 2 * HP, CH]), ALU.mult)\
                .then_inc(s["att_ready"], 1)

        def unit_b_dve(dve, G, u):
            c, hf, d = u // 2, u % 2, u % 2
            tok = slice(c * CH, (c + 1) * CH)
            dve.wait_ge(s["y_mm"], ONE + NU * G + u + 1)
            for t in range(HP):
                T = HP * hf + t
                ins = V.scalar_tensor_tensor(y_sb[:, T, tok], xbc[:, T, tok], vec[:, V_D + T:V_D + T + 1],
                                             ps[:, 6, t * CH:(t + 1) * CH], ALU.mult, ALU.add)
            ins.then_inc(s["y_read"], 1)
            dve.wait_ge(s["st_mm"], ONE + NU * G + u + 1)
            dve.wait_ge(s["sdec_ready"], ONE + NU * G + u + 1)
            for par in range(2):
                rr = slice(64 * par, 64 * par + 64)
                ins = V.tensor_tensor(state[rr, HP * hf:HP * hf + HP, rr], shaped(ps[rr, 7, 0:HP * HD], HP, HD),
                                      st_dec[rr, :, rr], ALU.add)
            ins.then_inc(s["state_done"], 1)

        CONV_AT = [0, 0, 0, 4, 8, 12, 16, 20, 25]
        DT_AT = 4

        def block_dve(dve, b, i, nxt, step):
            G = b * NB + i if isinstance(i, int) else dve.snap(b * NB + i)
            dve.wait_ge(s["pj_mm"], ONE + b * ALL + i * PER)
            if nxt == ROWS - 1:
                dve.wait_ge(s["bottom_clear"], ONE + b + 1)
            for u in range(NU):
                unit_a_dve(dve, G, u)
                if u:
                    unit_b_dve(dve, G, u - 1)
                if nxt:
                    conv_dve(dve, G + 1, CONV_AT[u], CONV_AT[u + 1], step)
                    if u == DT_AT:
                        dt_start(dve, G + 1, step)
            unit_b_dve(dve, G, NU - 1)
            if nxt:
                dt_mid(dve, G + 1, step, NC * G + 1)
            at0 = item("m1", nxt)
            pj = b * ALL + i * PER
            dve.wait_ge(s["pj_mm"], ONE + pj + at0 + 1)
            for half in range(2):
                h3 = slice(HP * half, HP * half + HP)
                V.tensor_tensor(y_sb[:, h3, :], y_sb[:, h3, :],
                                ps[:, at0 % 2:at0 % 2 + 1, :].broadcast_to([P, HP, TB]), ALU.subtract)\
                    .then_inc(s["y_centred"], 1)
            dve.wait_ge(s["y_centred"], ONE + 2 * G + 2)
            dve.sem_inc(s[f"pj_read{at0 % 2}"], 1)
            if nxt:
                dt_end(dve, G + 1, step)
                conv_dve(dve, G + 1, CONV_AT[NU], 32, step)
            at0 = item("m2", nxt)
            dve.wait_ge(s[f"pj_read{at0 % 2}"], ONE + b * (ALL // 2) + i * (PER // 2) + at0 // 2 + 1)
            V.reciprocal(row, row).then_inc(s["row_root"], 1)
            dve.wait_ge(s["row_root"], ONE + G + 1)
            dve.wait_ge(s["sq_ready"], ONE + 2 * G + 2)
            for half in range(2):
                h3 = slice(HP * half, HP * half + HP)
                V.tensor_tensor(y_sb[:, h3, :], y_sb[:, h3, :], row.unsqueeze(1).broadcast_to([P, HP, TB]),
                                ALU.mult).then_inc(s["y_scaled"], 1)
            if nxt:
                conv_dve(dve, G + 1, 32, 34, step)
            for t in range(NT):
                dve.wait_ge(s["y_affine"], ONE + NT * G + t + 1)
                z_at = item(f"z{t}", nxt)
                dve.wait_ge(s[f"pj_read{z_at % 2}"], ONE + b * (ALL // 2) + i * (PER // 2) + z_at // 2 + 1)
                V.tensor_tensor(y_sb[:, t, :], y_sb[:, t, :], xbc[:, t, :], ALU.mult).then_inc(s["gated"], 1)

            def residual(m):
                at0 = item(f"o{m}", nxt)
                dve.wait_ge(s["pj_mm"], ONE + pj + at0 + 1)
                xb = xs_[:, m, bass.ds(i * TB, TB)]
                V.tensor_tensor(xb, ps[:, at0 % 2, :], xb, ALU.add).then_inc(s["out_read"], 1)
                dve.wait_ge(s["out_read"], ONE + CT * G + m + 1)
                dve.sem_inc(s[f"pj_read{at0 % 2}"], 1)

            if nxt:
                conv_dve(dve, G + 1, 34, 40, step)
                residual(0)
                conv_dve(dve, G + 1, 40, 44, step)
                residual(1)
                conv_dve(dve, G + 1, 44, len(CONV), step)
                residual(2)
            else:
                for m in range(CT):
                    residual(m)

        QKV_STEPS = 6
        ATT_FIRST, ATT_STEPS, ATT_LAST = 3, 6, 6
        BLK_STEPS = 7 * VT + DT_STEPS
        V_GN0 = 24 + GN_STEPS
        V_QKV = V_GN0 + QKV_STEPS * (NB // 2)
        V_MAX0 = V_QKV + 3
        V_ATT = V_MAX0 + ATT_FIRST + ATT_STEPS * (NB - 2) + ATT_LAST
        V_GN1 = V_ATT + GN_STEPS
        V_SSD = V_GN1 + BLK_STEPS
        V_ALL = V_SSD + BLK_STEPS * (NB - 1)

        @block.vector
        def _(dve):
            step = Steps(dve, s["steps_v"])
            begin(dve)
            dve.wait_ge(s["weights_loaded"], ONE + 16 * 7)
            dve.wait_ge(s["prepared"], ONE + 3)
            b1 = shaped(vec[0:PD, V_BN1:V_BN1 + 12], 4, 3)
            b2 = shaped(vec[:, V_BN2:V_BN2 + 12], 4, 3)
            for v, sc, of in ((b1, bn1s, bn1o), (b2, bn2s, bn2o)):
                step(V.reciprocal(of[:], sc[:]))
                step.join()
                step(V.tensor_tensor(sc[:], v[:, 0, :], of[:], ALU.mult))
                step.join()
                step(V.tensor_tensor(of[:], v[:, 2, :], sc[:], ALU.mult))
                step.join()
                step(V.tensor_tensor(of[:], v[:, 1, :], of[:], ALU.subtract))
                step.join()
            V_PRE = step.n
            V.memset(rec[96:97, 0:1], 0.0).then_inc(s["vec_prepared"], 1)
            with dve.Fori(0, B) as b:
                base = dve.snap(b * V_ALL + V_PRE)
                step.enter(base)
                V.memset(k_st[96:99, :], 1.0)
                for t in range(CT):
                    dve.wait_ge(s[f"x_loaded{t}"], ONE + 16 * b + 16)
                    for k in range(NB):
                        step(V.bn_stats(chan_stats[:, t, k, :], xs_[:, t, k * TB:(k + 1) * TB]))
                step.join()
                gn_dve(dve, 2 * b, step)
                assert step.n == V_GN0
                dve.wait_ge(s["ab_ready"], ONE + 2 * b + 1)
                V.tensor_scalar(xn[:, 1, :], xs_[:, 1, :], gn_ab[:, 1, 0:1], gn_ab[:, 1, 1:2], ALU.mult, ALU.add)\
                    .then_inc(s["xn1_ready"], 1)
                qkv_dve(dve, b, 0, False, step)
                with dve.Fori(1, QP) as u:
                    step.enter(dve.snap(b * V_ALL + u * QKV_STEPS + (V_PRE + V_GN0 + 2 - QKV_STEPS)))
                    qkv_dve(dve, b, u, True, step)
                    assert step.n == QKV_STEPS, step.n
                step.enter(dve.snap(b * V_ALL + (V_PRE + V_GN0 + 2 + QKV_STEPS * (QP - 1))))
                take_vt(dve, b * QP + (QP - 1), QP - 1)
                for w in range(2):
                    stack_qk(dve, b * QP + (QP - 1), QP - 1, w, step)
                assert step.n == QKV_STEPS - 2, step.n
                meet(dve, b, 0)
                step.enter(dve.snap(b * V_ALL + (V_PRE + V_QKV)))
                for n in range(32):
                    max_dve(dve, b * NB, n)
                V.memset(negmax[:], 0.0).then_inc(s["cleared"], 1)
                dve.wait_ge(s["cleared"], ONE + b + 1)
                negmax_dve(dve, b * NB, step)
                split_max(dve, b * NB, 0, step)
                assert step.n == 3
                attend_dve(dve, b, 0, False, True, step)
                assert step.n == 3 + ATT_FIRST
                with dve.Fori(1, NB - 1) as qb:
                    step.enter(dve.snap(b * V_ALL + qb * ATT_STEPS + (V_PRE + V_MAX0 + ATT_FIRST - ATT_STEPS)))
                    attend_dve(dve, b, qb, True, True, step)
                    assert step.n == ATT_STEPS
                step.enter(dve.snap(b * V_ALL + (V_PRE + V_MAX0 + ATT_FIRST + ATT_STEPS * (NB - 2))))
                attend_dve(dve, b, NB - 1, True, False, step)
                recip_dve(dve, b * NB + (NB - 1), NB - 1)
                norm_dve(dve, b * NB + (NB - 1), NB - 1)
                for m in range(CT):
                    stats_dve(dve, b * NB + (NB - 1), NB - 1, m, step)
                assert step.n == ATT_LAST
                step.join()
                meet(dve, b, 1)
                step.enter(dve.snap(b * V_ALL + (V_PRE + V_ATT)))
                gn_dve(dve, 2 * b + 1, step)
                dve.wait_ge(s["ab_ready"], ONE + 2 * b + 2)
                dve.wait_ge(s["beta_mm"], ONE + 3 * b + 1)
                V.tensor_tensor(beta[0:R3, XT_ + NT:XT_ + NT + 1], ps[0:R3, 5, XT_ + NT:XT_ + NT + 1],
                                vec[0:R3, V_DTB:V_DTB + 1], ALU.add)
                for k in range(CT):
                    ins = V.tensor_scalar(w_dt[:, k, :], w_dt_raw[:, k, :], gn_ab[:, k, 0:1], None, ALU.mult)
                ins.then_inc(s["w_scaled"], 1)
                for n, (lo, hi) in enumerate(((NT, XT_ + NT), (0, NT))):
                    dve.wait_ge(s["beta_mm"], ONE + 3 * b + 2 + n)
                    V.tensor_copy(beta[:, lo:hi], ps[:, 6 + n, lo:hi])
                    for k in range(CT):
                        w = w_in[:, k, lo * P:hi * P]
                        ins = V.tensor_scalar(w, w, gn_ab[:, k, 0:1], None, ALU.mult)
                    ins.then_inc(s["w_scaled"], 1)
                step.enter(dve.snap(b * V_ALL + (V_PRE + V_GN1)))
                dt_start(dve, b * NB, step)
                dt_mid(dve, b * NB, step, NC * NB * b)
                dt_end(dve, b * NB, step)
                conv_dve(dve, b * NB, 0, len(CONV), step)
                assert step.n == BLK_STEPS, step.n
                with dve.Fori(0, NB - 2) as i:
                    step.enter(dve.snap(b * V_ALL + i * BLK_STEPS + (V_PRE + V_SSD)))
                    block_dve(dve, b, i, ROWS, step)
                    assert step.n == BLK_STEPS, step.n
                step.enter(dve.snap(b * V_ALL + (V_PRE + V_SSD + (NB - 2) * BLK_STEPS)))
                block_dve(dve, b, NB - 2, ROWS - 1, step)
                step.enter(dve.snap(b * V_ALL + (V_PRE + V_SSD + (NB - 1) * BLK_STEPS)))
                block_dve(dve, b, NB - 1, 0, step)
                meet(dve, b, 2)


def lay_out(i):
    f = {k: np.asarray(v) for k, v in i.items()}
    x = np.ascontiguousarray(f["x"].reshape(B, C, L))
    g = lambda n: f["L0_conv_" + n]
    m = lambda n: f["L1_conv_" + n]
    qkv = g("w_qkv")
    wq, wk, wv = qkv[:QK], qkv[QK:2 * QK], qkv[2 * QK:]
    rep = lambda a: np.concatenate([a] * QG, 0)
    wqkv = np.stack([rep(wq).T, rep(wk).T, wv.T], 1)
    vecs = np.zeros((P, NV), np.float32)
    for n, name in enumerate(("bn1_g", "bn1_b", "bn1_m", "bn1_v")):
        v = g(name)
        for k, part in enumerate((rep(v[:QK]), rep(v[QK:2 * QK]), v[2 * QK:])):
            vecs[:PD, V_BN1 + 3 * n + k] = part
    vecs[:PD, V_LN], vecs[:PD, V_LN + 1] = g("ln_w"), g("ln_b")
    tiles = lambda v: v.reshape(-1, P).T
    for n, name in enumerate(("bn2_g", "bn2_b", "bn2_m", "bn2_v")):
        vecs[:, V_BN2 + 3 * n:V_BN2 + 3 * n + 3] = tiles(g(name))
    cw = m("conv_w").reshape(XT_, P, 9)
    vecs[:, V_CW:V_CW + 63] = cw.transpose(1, 0, 2).reshape(P, 63)
    vecs[:, V_CB:V_CB + XT_] = tiles(m("conv_b"))
    vecs[:, V_NW:V_NW + NT], vecs[:, V_NB:V_NB + NT] = tiles(m("norm_w")), tiles(m("norm_b"))
    vecs[:, V_D:V_D + NT] = tiles(np.repeat(m("D"), HD))
    w = m("in_proj_w")
    wdt = np.zeros((R3, C), np.float32)
    for first in [PART * part + copy for part in range(3) for copy in (0, COPY)]:
        r = slice(first, first + NH)
        vecs[r, V_DTB], vecs[r, V_AL] = m("dt_bias"), m("A_log")
        wdt[r] = w[DIN:]
    kmajor = lambda a: np.ascontiguousarray(a.T.reshape(-1, P, a.shape[0]).transpose(1, 0, 2))
    consts, constb = constants()
    return {"x": x, "vecs": vecs, "wqkv": np.ascontiguousarray(wqkv), "wproj": kmajor(g("w_proj")),
            "win": kmajor(w[:DIN]), "wdt": kmajor(wdt), "wout": kmajor(m("out_proj_w")),
            "consts": consts, "constb": constb}


def kernel(**inputs):
    import concourse.bacc as bacc
    from concourse.bass_utils import run_bass_kernel_spmd

    nc = bacc.Bacc("TRN2", target_bir_lowering=False, num_devices=1)
    arrays = lay_out(inputs)
    args = [nc.dram_tensor(n, a.shape, mybir.dt.from_np(a.dtype), kind="ExternalInput").ap()
            for n, a in arrays.items()]
    args.append(nc.dram_tensor("out", (B, C, L), F32, kind="ExternalOutput").ap())
    program(nc, *args)
    r = run_bass_kernel_spmd(nc, [arrays], core_ids=[0])
    return r.results[0]["out"].reshape(B, C, H, W)
```
